# Optimizing a Trainium2 kernel written in Bass

```python
import numpy as np
import jax
import jax.numpy as jnp

def _softmax(x, axis=-1):
    return jax.nn.softmax(x, axis=axis)

def _gelu(x):
    return jax.nn.gelu(x, approximate=True)

def _silu(x):
    return jax.nn.silu(x)

def _sigmoid(x):
    return jax.nn.sigmoid(x)

def _layernorm(x, axis=-1, eps=1e-05):
    m = jnp.mean(x, axis=axis, keepdims=True)
    v = jnp.var(x, axis=axis, keepdims=True)
    return (x - m) / jnp.sqrt(v + eps)

def _scatter_add(tgt, idx, src, axis=0):
    return tgt.at[idx].add(src)

def _segment_sum(src, seg, n):
    return jax.ops.segment_sum(src, seg, n)
kernel_name = 'mk_lm_tower_d4_tok_ids256_r4_719f5c'

def setup_inputs(seed: int=0):
    np.random.seed(seed)
    _w = jnp.asarray

    def _rec_inputs():
        import jax
        import jax.numpy as jnp
        _rk = jax.random.key(seed)
        x = jax.random.randint(jax.random.fold_in(_rk, 1), (8, 512), 0, 64, jnp.int32)
        return x
    x = _rec_inputs()

    def _L0_tok_setup():
        import jax, jax.numpy as jnp
        import numpy as np
        PRIME = 31
        VOCAB = 125000
        NGRAM_SIZES = (2, 3, 4)

        def _ngram_hash(byte_ids, n):
            T = byte_ids.shape[1]
            powers = PRIME ** jnp.arange(n - 1, -1, -1, dtype=jnp.int64) % VOCAB
            windows = jnp.stack([byte_ids[:, i:T - n + 1 + i] for i in range(n)], axis=-1)
            return (windows.astype(jnp.int64) * powers).sum(axis=-1) % VOCAB
        key = jax.random.key(seed)
        k0, k1, k2, k3 = jax.random.split(key, 4)
        byte_ids = jax.random.randint(k0, (8, 1024), 0, 64, dtype=jnp.int64)
        emb_2 = jax.random.normal(k1, (VOCAB, 64), dtype=jnp.float32)
        emb_3 = jax.random.normal(k2, (VOCAB, 64), dtype=jnp.float32)
        emb_4 = jax.random.normal(k3, (VOCAB, 64), dtype=jnp.float32)
        return {'byte_ids': byte_ids, 'emb_2': emb_2, 'emb_3': emb_3, 'emb_4': emb_4}
    _L0_tok_all = _L0_tok_setup()
    _L0_tok_in = {k: v for k, v in _L0_tok_all.items() if k in ('emb_2', 'emb_3', 'emb_4')}
    del _L0_tok_all

    def _L0_attn_setup():
        import jax, jax.numpy as jnp
        import numpy as np
        S, B, D, H, DH = (128, 32, 64, 8, 32)
        LN_EPS = 1e-05

        def elu_p1(x):
            return jax.nn.elu(x) + 1.0

        def sum_norm(x):
            return x / jnp.sum(x, axis=-1, keepdims=True)

        def layer_norm(x, g, b):
            mu = jnp.mean(x, axis=-1, keepdims=True)
            var = jnp.mean(jnp.square(x - mu), axis=-1, keepdims=True)
            return (x - mu) * jax.lax.rsqrt(var + LN_EPS) * g + b

        def _fast_rnn_forward(x, slow_W, out_W, ln_g, ln_b):
            slen, bsz, _ = x.shape
            o = layer_norm(x, ln_g, ln_b)
            qkv = jnp.einsum('sbd,ed->sbe', o, slow_W)
            qkv = qkv.reshape(slen, bsz, H, 5 * DH + 2)
            q, k, v, rk, rv, beta, rbeta = jnp.split(qkv, [DH, 2 * DH, 3 * DH, 4 * DH, 5 * DH, 5 * DH + 1], axis=-1)
            beta = jax.nn.sigmoid(beta)
            rbeta = jax.nn.sigmoid(rbeta)
            q = sum_norm(elu_p1(q))
            k = sum_norm(elu_p1(k))
            rk = jax.nn.softmax(rk, axis=-1)

            def ff_step(W, inp):
                qt, kt, vt, bt = inp
                v_old = jnp.einsum('bhij,bhj->bhi', W, kt)
                W = W + (bt * (vt - v_old))[..., :, None] * kt[..., None, :]
                z = jnp.einsum('bhij,bhj->bhi', W, qt)
                return (W, z)
            W0 = jnp.zeros((bsz, H, DH, DH), x.dtype)
            _, z = jax.lax.scan(ff_step, W0, (q, k, v, beta))

            def rec_step(carry, inp):
                R, h = carry
                zt, kt, vt, bt = inp
                q_rec = jax.nn.softmax(h, axis=-1)
                v_old = jnp.einsum('bhij,bhj->bhi', R, kt)
                R = R + (bt * (vt - v_old))[..., :, None] * kt[..., None, :]
                h = zt + jnp.einsum('bhij,bhj->bhi', R, q_rec)
                return ((R, h), h)
            R0 = jnp.zeros((bsz, H, DH, DH), x.dtype)
            h0 = jnp.zeros((bsz, H, DH), x.dtype)
            _, hs = jax.lax.scan(rec_step, (R0, h0), (z, rk, rv, rbeta))
            out = hs.reshape(slen, bsz, H * DH)
            out = jnp.einsum('sbe,de->sbd', out, out_W)
            return x + out
        key = jax.random.key(seed)
        k1, k2, k3 = jax.random.split(key, 3)
        x = jax.random.normal(k1, (S, B, D), jnp.float32)
        slow_W = jax.random.normal(k2, (H * (5 * DH + 2), D), jnp.float32) * 0.02
        out_W = jax.random.normal(k3, (D, H * DH), jnp.float32) * 0.02
        ln_g = jnp.ones((D,), jnp.float32)
        ln_b = jnp.zeros((D,), jnp.float32)
        return {'x': x, 'slow_W': slow_W, 'out_W': out_W, 'ln_g': ln_g, 'ln_b': ln_b}
    _L0_attn_all = _L0_attn_setup()
    _L0_attn_in = {k: v for k, v in _L0_attn_all.items() if k in ('slow_W', 'out_W', 'ln_g', 'ln_b')}
    del _L0_attn_all

    def _L0_ffn_setup():
        import math
        import jax, jax.numpy as jnp
        import numpy as np
        CAPACITY_FACTOR = 1.25
        key = jax.random.key(seed)
        ks = jax.random.split(key, 5)
        B, L, D, F, E = (8, 2048, 64, 256, 8)
        h = jax.random.normal(ks[0], (B, L, D), dtype=jnp.float32)
        gate_w = jax.random.normal(ks[1], (D, E), dtype=jnp.float32) * 0.02
        gate_b = jnp.zeros((E,), dtype=jnp.float32)
        w1 = jax.random.normal(ks[2], (E, D, F), dtype=jnp.float32) * (1.0 / math.sqrt(D))
        b1 = jnp.zeros((E, F), dtype=jnp.float32)
        w2 = jax.random.normal(ks[3], (E, F, D), dtype=jnp.float32) * (1.0 / math.sqrt(F))
        b2 = jnp.zeros((E, D), dtype=jnp.float32)
        return {'h': h, 'gate_w': gate_w, 'gate_b': gate_b, 'w1': w1, 'b1': b1, 'w2': w2, 'b2': b2}
    _L0_ffn_all = _L0_ffn_setup()
    _L0_ffn_in = {k: v for k, v in _L0_ffn_all.items() if k in ('gate_w', 'gate_b', 'w1', 'b1', 'w2', 'b2')}
    del _L0_ffn_all

    def _L1_attn_setup():
        import jax, jax.numpy as jnp
        import numpy as np
        B, T, D, DH, C = (2, 512, 64, 256, 64)

        def _dwconv(x, w):
            y = jax.lax.conv_general_dilated(x.transpose(0, 2, 1), w, (1,), ((1, 1),), feature_group_count=x.shape[-1], dimension_numbers=('NCH', 'OIH', 'NCH'))
            return y.transpose(0, 2, 1)

        def _l2norm(z):
            return z / jnp.maximum(jnp.linalg.norm(z, axis=-1, keepdims=True), 1e-12)

        def _combine(e1, e2):
            a1, b1 = e1
            a2, b2 = e2
            return (a1 * a2, a2 * b1 + b2)
        key = jax.random.key(seed)
        ks = jax.random.split(key, 12)

        def xav(k, o, i):
            return jax.random.normal(k, (o, i), jnp.float32) * float(np.sqrt(2.0 / (o + i)))
        return {'x': jax.random.normal(ks[0], (B, T, D), jnp.float32), 'W_K': xav(ks[1], D, D), 'W_V': xav(ks[2], D, D), 'W_Q': xav(ks[3], D, D), 'conv_k': jax.random.normal(ks[4], (D, 1, 3), jnp.float32) * 0.2, 'conv_v': jax.random.normal(ks[5], (D, 1, 3), jnp.float32) * 0.2, 'conv_q': jax.random.normal(ks[6], (D, 1, 3), jnp.float32) * 0.2, 'W_th': xav(ks[7], D, D), 'b_th': jnp.zeros((D,), jnp.float32), 'W_et': xav(ks[8], D, D), 'b_et': jnp.zeros((D,), jnp.float32), 'W_al': xav(ks[9], D, D), 'b_al': jnp.zeros((D,), jnp.float32), 'W1': xav(ks[10], DH, D), 'W2': xav(ks[11], D, DH), 'ln_g': jnp.ones((D,), jnp.float32), 'ln_b': jnp.zeros((D,), jnp.float32), 'W_gate': xav(jax.random.fold_in(key, 101), D, D), 'W_proj': xav(jax.random.fold_in(key, 102), D, D)}
    _L1_attn_all = _L1_attn_setup()
    _L1_attn_in = {k: v for k, v in _L1_attn_all.items() if k in ('W_K', 'W_V', 'W_Q', 'conv_k', 'conv_v', 'conv_q', 'W_th', 'b_th', 'W_et', 'b_et', 'W_al', 'b_al', 'W1', 'W2', 'ln_g', 'ln_b', 'W_gate', 'W_proj')}
    del _L1_attn_all

    def _L1_ffn_setup():
        import jax, jax.numpy as jnp
        import numpy as np
        B, S, D, E, H, K = (4, 1024, 64, 8, 128, 2)
        key = jax.random.key(seed)
        ks = jax.random.split(key, 6)
        x = jax.random.normal(ks[0], (B, S, D), jnp.float32)
        Wg = jax.random.normal(ks[1], (D, E), jnp.float32) * 0.02
        bg = jnp.zeros((E,), jnp.float32)
        W1 = jax.random.normal(ks[2], (E, D, H), jnp.float32) * 0.02
        b1 = jnp.zeros((E, H), jnp.float32)
        W2 = jax.random.normal(ks[3], (E, H, D), jnp.float32) * 0.02
        b2 = jnp.zeros((E, D), jnp.float32)
        return {'x': x, 'Wg': Wg, 'bg': bg, 'W1': W1, 'b1': b1, 'W2': W2, 'b2': b2}
    _L1_ffn_all = _L1_ffn_setup()
    _L1_ffn_in = {k: v for k, v in _L1_ffn_all.items() if k in ('Wg', 'bg', 'W1', 'b1', 'W2', 'b2')}
    del _L1_ffn_all

    def _L2_attn_setup():
        import jax, jax.numpy as jnp
        import numpy as np
        NUM_HEADS = 8
        C_SHIFT = 5.0
        key = jax.random.key(seed)
        k1, k2, k3 = jax.random.split(key, 3)
        B, N, D = (8, 256, 64)
        x = jax.random.normal(k1, (B, N, D), dtype=jnp.float32)
        qkv_w = jax.random.normal(k2, (3 * D, D), dtype=jnp.float32) * D ** (-0.5)
        qkv_b = jnp.zeros((3 * D,), dtype=jnp.float32)
        proj_w = jax.random.normal(k3, (D, D), dtype=jnp.float32) * D ** (-0.5)
        proj_b = jnp.zeros((D,), dtype=jnp.float32)
        return {'x': x, 'qkv_w': qkv_w, 'qkv_b': qkv_b, 'proj_w': proj_w, 'proj_b': proj_b}
    _L2_attn_all = _L2_attn_setup()
    _L2_attn_in = {k: v for k, v in _L2_attn_all.items() if k in ('qkv_w', 'qkv_b', 'proj_w', 'proj_b')}
    del _L2_attn_all

    def _L2_ffn_setup():
        import jax, jax.numpy as jnp
        import numpy as np
        E = 8
        K = 2
        D = 64
        H = 128
        DOUT = 64
        EPS = 1e-05
        key = jax.random.key(seed)
        ks = jax.random.split(key, 9)
        s = 0.02
        return {'x': jax.random.normal(ks[0], (4, 2048, D), jnp.float32), 'gamma': 1.0 + 0.05 * jax.random.normal(ks[1], (D,), jnp.float32), 'beta': 0.05 * jax.random.normal(ks[2], (D,), jnp.float32), 'Wr': 0.01 * jax.random.normal(ks[3], (D, E), jnp.float32), 'br': jnp.zeros((E,), jnp.float32), 'W1': s * jax.random.normal(ks[4], (E, D, H), jnp.float32), 'b1': s * jax.random.normal(ks[5], (E, H), jnp.float32), 'W2': s * jax.random.normal(ks[6], (E, H, DOUT), jnp.float32), 'b2': s * jax.random.normal(ks[7], (E, DOUT), jnp.float32)}
    _L2_ffn_all = _L2_ffn_setup()
    _L2_ffn_in = {k: v for k, v in _L2_ffn_all.items() if k in ('gamma', 'beta', 'Wr', 'br', 'W1', 'b1', 'W2', 'b2')}
    del _L2_ffn_all

    def _L3_attn_setup():
        import jax, jax.numpy as jnp
        import numpy as np
        key = jax.random.key(seed)
        k1, k2 = jax.random.split(key)
        B, N, F = (4, 1024, 64)
        nodes = jax.random.normal(k1, (B, N, F), dtype=jnp.float32)
        limit = np.sqrt(6.0 / (F + F)).astype(np.float32)
        W = jax.random.uniform(k2, (F, F), dtype=jnp.float32, minval=-limit, maxval=limit)
        return {'nodes': nodes, 'W': W}
    _L3_attn_all = _L3_attn_setup()
    _L3_attn_in = {k: v for k, v in _L3_attn_all.items() if k in ('W',)}
    del _L3_attn_all

    def _L3_ffn_setup():
        import jax, jax.numpy as jnp
        import numpy as np
        TOP_K = 2
        LN_EPS = 1e-05
        key = jax.random.key(seed)
        ks = jax.random.split(key, 8)
        B, S, D, E, H = (16, 256, 64, 8, 256)
        x = jax.random.normal(ks[0], (B, S, D), dtype=jnp.float32)
        Wr = jax.random.normal(ks[1], (D, E), dtype=jnp.float32) * 0.1
        br = jnp.zeros((E,), dtype=jnp.float32)
        ln_g = jnp.ones((E, D), dtype=jnp.float32)
        ln_b = jnp.zeros((E, D), dtype=jnp.float32)
        W1 = jax.random.normal(ks[2], (E, D, H), dtype=jnp.float32) * (1.0 / np.sqrt(D))
        b1 = jnp.zeros((E, H), dtype=jnp.float32)
        W2 = jax.random.normal(ks[3], (E, H, D), dtype=jnp.float32) * (1.0 / np.sqrt(H))
        b2 = jnp.zeros((E, D), dtype=jnp.float32)
        return {'x': x, 'Wr': Wr, 'br': br, 'ln_g': ln_g, 'ln_b': ln_b, 'W1': W1, 'b1': b1, 'W2': W2, 'b2': b2}
    _L3_ffn_all = _L3_ffn_setup()
    _L3_ffn_in = {k: v for k, v in _L3_ffn_all.items() if k in ('Wr', 'br', 'ln_g', 'ln_b', 'W1', 'b1', 'W2', 'b2')}
    del _L3_ffn_all
    return {'x': x, 'L0_tok_emb_2': _L0_tok_in['emb_2'], 'L0_tok_emb_3': _L0_tok_in['emb_3'], 'L0_tok_emb_4': _L0_tok_in['emb_4'], 'L0_attn_slow_W': _L0_attn_in['slow_W'], 'L0_attn_out_W': _L0_attn_in['out_W'], 'L0_attn_ln_g': _L0_attn_in['ln_g'], 'L0_attn_ln_b': _L0_attn_in['ln_b'], 'L0_ffn_gate_w': _L0_ffn_in['gate_w'], 'L0_ffn_gate_b': _L0_ffn_in['gate_b'], 'L0_ffn_w1': _L0_ffn_in['w1'], 'L0_ffn_b1': _L0_ffn_in['b1'], 'L0_ffn_w2': _L0_ffn_in['w2'], 'L0_ffn_b2': _L0_ffn_in['b2'], 'L1_attn_W_K': _L1_attn_in['W_K'], 'L1_attn_W_V': _L1_attn_in['W_V'], 'L1_attn_W_Q': _L1_attn_in['W_Q'], 'L1_attn_conv_k': _L1_attn_in['conv_k'], 'L1_attn_conv_v': _L1_attn_in['conv_v'], 'L1_attn_conv_q': _L1_attn_in['conv_q'], 'L1_attn_W_th': _L1_attn_in['W_th'], 'L1_attn_b_th': _L1_attn_in['b_th'], 'L1_attn_W_et': _L1_attn_in['W_et'], 'L1_attn_b_et': _L1_attn_in['b_et'], 'L1_attn_W_al': _L1_attn_in['W_al'], 'L1_attn_b_al': _L1_attn_in['b_al'], 'L1_attn_W1': _L1_attn_in['W1'], 'L1_attn_W2': _L1_attn_in['W2'], 'L1_attn_ln_g': _L1_attn_in['ln_g'], 'L1_attn_ln_b': _L1_attn_in['ln_b'], 'L1_attn_W_gate': _L1_attn_in['W_gate'], 'L1_attn_W_proj': _L1_attn_in['W_proj'], 'L1_ffn_Wg': _L1_ffn_in['Wg'], 'L1_ffn_bg': _L1_ffn_in['bg'], 'L1_ffn_W1': _L1_ffn_in['W1'], 'L1_ffn_b1': _L1_ffn_in['b1'], 'L1_ffn_W2': _L1_ffn_in['W2'], 'L1_ffn_b2': _L1_ffn_in['b2'], 'L2_attn_qkv_w': _L2_attn_in['qkv_w'], 'L2_attn_qkv_b': _L2_attn_in['qkv_b'], 'L2_attn_proj_w': _L2_attn_in['proj_w'], 'L2_attn_proj_b': _L2_attn_in['proj_b'], 'L2_ffn_gamma': _L2_ffn_in['gamma'], 'L2_ffn_beta': _L2_ffn_in['beta'], 'L2_ffn_Wr': _L2_ffn_in['Wr'], 'L2_ffn_br': _L2_ffn_in['br'], 'L2_ffn_W1': _L2_ffn_in['W1'], 'L2_ffn_b1': _L2_ffn_in['b1'], 'L2_ffn_W2': _L2_ffn_in['W2'], 'L2_ffn_b2': _L2_ffn_in['b2'], 'L3_attn_W': _L3_attn_in['W'], 'L3_ffn_Wr': _L3_ffn_in['Wr'], 'L3_ffn_br': _L3_ffn_in['br'], 'L3_ffn_ln_g': _L3_ffn_in['ln_g'], 'L3_ffn_ln_b': _L3_ffn_in['ln_b'], 'L3_ffn_W1': _L3_ffn_in['W1'], 'L3_ffn_b1': _L3_ffn_in['b1'], 'L3_ffn_W2': _L3_ffn_in['W2'], 'L3_ffn_b2': _L3_ffn_in['b2']}

def reference(x, L0_tok_emb_2, L0_tok_emb_3, L0_tok_emb_4, L0_attn_slow_W, L0_attn_out_W, L0_attn_ln_g, L0_attn_ln_b, L0_ffn_gate_w, L0_ffn_gate_b, L0_ffn_w1, L0_ffn_b1, L0_ffn_w2, L0_ffn_b2, L1_attn_W_K, L1_attn_W_V, L1_attn_W_Q, L1_attn_conv_k, L1_attn_conv_v, L1_attn_conv_q, L1_attn_W_th, L1_attn_b_th, L1_attn_W_et, L1_attn_b_et, L1_attn_W_al, L1_attn_b_al, L1_attn_W1, L1_attn_W2, L1_attn_ln_g, L1_attn_ln_b, L1_attn_W_gate, L1_attn_W_proj, L1_ffn_Wg, L1_ffn_bg, L1_ffn_W1, L1_ffn_b1, L1_ffn_W2, L1_ffn_b2, L2_attn_qkv_w, L2_attn_qkv_b, L2_attn_proj_w, L2_attn_proj_b, L2_ffn_gamma, L2_ffn_beta, L2_ffn_Wr, L2_ffn_br, L2_ffn_W1, L2_ffn_b1, L2_ffn_W2, L2_ffn_b2, L3_attn_W, L3_ffn_Wr, L3_ffn_br, L3_ffn_ln_g, L3_ffn_ln_b, L3_ffn_W1, L3_ffn_b1, L3_ffn_W2, L3_ffn_b2):
    import jax
    import jax.numpy as jnp

    def _L0_tok_ref(byte_ids, emb_2, emb_3, emb_4):
        import jax, jax.numpy as jnp
        import numpy as np
        PRIME = 31
        VOCAB = 125000
        NGRAM_SIZES = (2, 3, 4)

        def _ngram_hash(byte_ids, n):
            T = byte_ids.shape[1]
            powers = PRIME ** jnp.arange(n - 1, -1, -1, dtype=jnp.int64) % VOCAB
            windows = jnp.stack([byte_ids[:, i:T - n + 1 + i] for i in range(n)], axis=-1)
            return (windows.astype(jnp.int64) * powers).sum(axis=-1) % VOCAB
        tables = {2: emb_2, 3: emb_3, 4: emb_4}
        B, T = byte_ids.shape
        D = emb_2.shape[1]
        out = jnp.zeros((B, T, D), dtype=emb_2.dtype)
        for n in NGRAM_SIZES:
            idx = _ngram_hash(byte_ids, n)
            gathered = tables[n][idx]
            out = out + jnp.pad(gathered, ((0, 0), (n - 1, 0), (0, 0)))
        return out / (len(NGRAM_SIZES) + 1)

    def _L0_attn_ref(x, slow_W, out_W, ln_g, ln_b):
        import jax, jax.numpy as jnp
        import numpy as np
        S, B, D, H, DH = (128, 32, 64, 8, 32)
        LN_EPS = 1e-05

        def elu_p1(x):
            return jax.nn.elu(x) + 1.0

        def sum_norm(x):
            return x / jnp.sum(x, axis=-1, keepdims=True)

        def layer_norm(x, g, b):
            mu = jnp.mean(x, axis=-1, keepdims=True)
            var = jnp.mean(jnp.square(x - mu), axis=-1, keepdims=True)
            return (x - mu) * jax.lax.rsqrt(var + LN_EPS) * g + b

        def _fast_rnn_forward(x, slow_W, out_W, ln_g, ln_b):
            slen, bsz, _ = x.shape
            o = layer_norm(x, ln_g, ln_b)
            qkv = jnp.einsum('sbd,ed->sbe', o, slow_W)
            qkv = qkv.reshape(slen, bsz, H, 5 * DH + 2)
            q, k, v, rk, rv, beta, rbeta = jnp.split(qkv, [DH, 2 * DH, 3 * DH, 4 * DH, 5 * DH, 5 * DH + 1], axis=-1)
            beta = jax.nn.sigmoid(beta)
            rbeta = jax.nn.sigmoid(rbeta)
            q = sum_norm(elu_p1(q))
            k = sum_norm(elu_p1(k))
            rk = jax.nn.softmax(rk, axis=-1)

            def ff_step(W, inp):
                qt, kt, vt, bt = inp
                v_old = jnp.einsum('bhij,bhj->bhi', W, kt)
                W = W + (bt * (vt - v_old))[..., :, None] * kt[..., None, :]
                z = jnp.einsum('bhij,bhj->bhi', W, qt)
                return (W, z)
            W0 = jnp.zeros((bsz, H, DH, DH), x.dtype)
            _, z = jax.lax.scan(ff_step, W0, (q, k, v, beta))

            def rec_step(carry, inp):
                R, h = carry
                zt, kt, vt, bt = inp
                q_rec = jax.nn.softmax(h, axis=-1)
                v_old = jnp.einsum('bhij,bhj->bhi', R, kt)
                R = R + (bt * (vt - v_old))[..., :, None] * kt[..., None, :]
                h = zt + jnp.einsum('bhij,bhj->bhi', R, q_rec)
                return ((R, h), h)
            R0 = jnp.zeros((bsz, H, DH, DH), x.dtype)
            h0 = jnp.zeros((bsz, H, DH), x.dtype)
            _, hs = jax.lax.scan(rec_step, (R0, h0), (z, rk, rv, rbeta))
            out = hs.reshape(slen, bsz, H * DH)
            out = jnp.einsum('sbe,de->sbd', out, out_W)
            return x + out
        return _fast_rnn_forward(x, slow_W, out_W, ln_g, ln_b)

    def _L0_ffn_ref(h, gate_w, gate_b, w1, b1, w2, b2):
        import math
        import jax, jax.numpy as jnp
        import numpy as np
        CAPACITY_FACTOR = 1.25
        B, L, D = h.shape
        E = gate_w.shape[1]
        T = B * L
        C = max(1, math.ceil(CAPACITY_FACTOR * T / E))
        x = h.reshape(T, D)
        logits = x @ gate_w + gate_b
        probs = jax.nn.softmax(logits, axis=-1)
        idx = jnp.argmax(probs, axis=-1)
        prb = jnp.take_along_axis(probs, idx[:, None], axis=1)[:, 0]
        one_hot = jax.nn.one_hot(idx, E, dtype=jnp.float32)
        pos = (jnp.cumsum(one_hot, axis=0) * one_hot).sum(-1).astype(jnp.int32) - 1
        kept = pos < C
        pos_safe = jnp.where(kept, pos, C)
        buf = jnp.zeros((E, C, D), dtype=h.dtype).at[idx, pos_safe].set(x, mode='drop')
        hmid = jax.nn.relu(jnp.einsum('ecd,edf->ecf', buf, w1) + b1[:, None, :])
        ybuf = jnp.einsum('ecf,efd->ecd', hmid, w2) + b2[:, None, :]
        pos_g = jnp.minimum(pos, C - 1)
        y_tok = ybuf[idx, pos_g] * (prb * kept)[:, None]
        y = y_tok.reshape(B, L, D)
        y = jnp.nan_to_num(y, nan=0.0, posinf=10000.0, neginf=-10000.0)
        return y

    def _L1_attn_ref(x, W_K, W_V, W_Q, conv_k, conv_v, conv_q, W_th, b_th, W_et, b_et, W_al, b_al, W1, W2, ln_g, ln_b, W_gate, W_proj):
        import jax, jax.numpy as jnp
        import numpy as np
        B, T, D, DH, C = (2, 512, 64, 256, 64)

        def _dwconv(x, w):
            y = jax.lax.conv_general_dilated(x.transpose(0, 2, 1), w, (1,), ((1, 1),), feature_group_count=x.shape[-1], dimension_numbers=('NCH', 'OIH', 'NCH'))
            return y.transpose(0, 2, 1)

        def _l2norm(z):
            return z / jnp.maximum(jnp.linalg.norm(z, axis=-1, keepdims=True), 1e-12)

        def _combine(e1, e2):
            a1, b1 = e1
            a2, b2 = e2
            return (a1 * a2, a2 * b1 + b2)
        Bq, Tq, Dq = x.shape
        nC = Tq // C
        k = _l2norm(_dwconv(x @ W_K.T, conv_k))
        v = _dwconv(x @ W_V.T, conv_v)
        q = _l2norm(_dwconv(x @ W_Q.T, conv_q))
        theta = jax.nn.sigmoid(x @ W_th.T + b_th).mean(-1)
        eta = jax.nn.sigmoid(x @ W_et.T + b_et).mean(-1)
        alpha = jax.nn.sigmoid(x @ W_al.T + b_al).mean(-1)
        h_k = jax.nn.silu(k @ W1.T)
        h_q = jax.nn.silu(q @ W1.T)
        fast_W0 = jnp.broadcast_to(jax.lax.stop_gradient(W2), (Bq, Dq, DH)) + 0.0
        S0 = jnp.zeros((Bq, Dq, DH), x.dtype)

        def chunked(a):
            return a.reshape(Bq, nC, C, *a.shape[2:]).swapaxes(0, 1)
        xs = (chunked(h_k), chunked(h_q), chunked(v), chunked(theta), chunked(eta), chunked(alpha))

        def step(carry, inp):
            fW, S = carry
            hk, hq, vv, th, et, al = inp
            pred = jnp.einsum('bti,boi->bto', hk, fW)
            res = pred - vv
            u = -th[:, :, None, None] * (res[..., :, None] * hk[..., None, :])
            et_b = jnp.broadcast_to(et[:, :, None, None], (Bq, C, 1, 1))
            u = u.at[:, 0].add(et_b[:, 0] * S)
            S_chunk = jax.lax.associative_scan(_combine, (et_b, u), axis=1)[1]
            S_new = S_chunk[:, -1]
            beta = jnp.broadcast_to((1.0 - al)[:, :, None, None], (Bq, C, 1, 1))
            d0 = S_chunk.at[:, 0].add(beta[:, 0] * fW)
            fW_new = jax.lax.associative_scan(_combine, (beta, d0), axis=1)[1][:, -1]
            ret = jnp.einsum('bti,boi->bto', hq, fW_new)
            return ((fW_new, S_new), ret)
        _, rets = jax.lax.scan(step, (fast_W0, S0), xs)
        retrieved = rets.swapaxes(0, 1).reshape(Bq, Tq, Dq)
        mu = retrieved.mean(-1, keepdims=True)
        var = retrieved.var(-1, keepdims=True)
        out = (retrieved - mu) / jnp.sqrt(var + 1e-05) * ln_g + ln_b
        out = out * jax.nn.sigmoid(x @ W_gate.T)
        return out @ W_proj.T

    def _L1_ffn_ref(x, Wg, bg, W1, b1, W2, b2):
        import jax, jax.numpy as jnp
        import numpy as np
        B, S, D, E, H, K = (4, 1024, 64, 8, 128, 2)
        Bv, Sv, Dv = x.shape
        gate_scores = x @ Wg + bg
        _, idx = jax.lax.top_k(gate_scores, K)
        mask = jax.nn.one_hot(idx, E, dtype=x.dtype).sum(axis=-2)
        xf = x.reshape(-1, Dv)
        mf = mask.reshape(-1, E)
        h = jax.nn.gelu(jnp.einsum('td,edh->teh', xf, W1) + b1[None], approximate=False)
        y = jnp.einsum('teh,ehd->ted', h, W2) + b2[None]
        out = jnp.einsum('ted,te->td', y, mf)
        return out.reshape(Bv, Sv, Dv)

    def _L2_attn_ref(x, qkv_w, qkv_b, proj_w, proj_b):
        import jax, jax.numpy as jnp
        import numpy as np
        NUM_HEADS = 8
        C_SHIFT = 5.0
        B, N, D = x.shape
        H = NUM_HEADS
        dh = D // H
        scale = dh ** (-0.5)
        qkv = x @ qkv_w.T + qkv_b
        qkv = qkv.reshape(B, N, 3, H, dh)
        q, k, v = (qkv[:, :, 0], qkv[:, :, 1], qkv[:, :, 2])
        scores = jnp.einsum('bnhd,bmhd->bhnm', q, k) * scale
        t = jnp.square(scores + C_SHIFT)
        attn = t / jnp.sum(t, axis=-1, keepdims=True)
        out = jnp.einsum('bhnm,bmhd->bnhd', attn, v).reshape(B, N, D)
        return out @ proj_w.T + proj_b

    def _L2_ffn_ref(x, gamma, beta, Wr, br, W1, b1, W2, b2):
        import jax, jax.numpy as jnp
        import numpy as np
        E = 8
        K = 2
        D = 64
        H = 128
        DOUT = 64
        EPS = 1e-05
        mu = jnp.mean(x, axis=-1, keepdims=True)
        var = jnp.mean(jnp.square(x - mu), axis=-1, keepdims=True)
        xn = (x - mu) * jax.lax.rsqrt(var + EPS) * gamma + beta
        logits = jnp.einsum('bsd,de->bse', xn, Wr) + br
        top_vals, top_idx = jax.lax.top_k(logits, K)
        w = jax.nn.softmax(top_vals, axis=-1)
        w_full = jnp.einsum('bsk,bske->bse', w, jax.nn.one_hot(top_idx, E, dtype=w.dtype))
        y = jnp.zeros(x.shape[:-1] + (DOUT,), x.dtype)
        for e in range(E):
            h = jax.nn.gelu(jnp.einsum('bsd,dh->bsh', xn, W1[e]) + b1[e], approximate=False)
            y_e = jnp.einsum('bsh,hd->bsd', h, W2[e]) + b2[e]
            y = y + y_e * w_full[..., e, None]
        return y

    def _L3_attn_ref(nodes, W):
        import jax, jax.numpy as jnp
        import numpy as np
        F = nodes.shape[-1]
        norm_const = 1.0 / jnp.sqrt(jnp.asarray(F, dtype=nodes.dtype))
        x = jnp.einsum('bnf,fg->bng', nodes, W)
        prods = jnp.einsum('bnf,bmf->bnm', x, nodes)
        att_scores = jax.nn.softmax(prods * norm_const, axis=-1)
        messgs = jnp.einsum('bnm,bmf->bnf', att_scores, nodes)
        return messgs

    def _L3_ffn_ref(x, Wr, br, ln_g, ln_b, W1, b1, W2, b2):
        import jax, jax.numpy as jnp
        import numpy as np
        TOP_K = 2
        LN_EPS = 1e-05
        B, S, D = x.shape
        N = B * S
        xt = x.reshape(N, D)
        logits = xt @ Wr + br
        probs = jax.nn.softmax(logits, axis=-1)
        top_p, top_idx = jax.lax.top_k(probs, TOP_K)
        weights = top_p / top_p.sum(axis=-1, keepdims=True)
        mu = xt.mean(axis=-1, keepdims=True)
        var = ((xt - mu) ** 2).mean(axis=-1, keepdims=True)
        xn = (xt - mu) * jax.lax.rsqrt(var + LN_EPS)
        xe = xn[None, :, :] * ln_g[:, None, :] + ln_b[:, None, :]
        h = jax.nn.gelu(jnp.einsum('end,edh->enh', xe, W1) + b1[:, None, :], approximate=False)
        y = jnp.einsum('enh,ehd->end', h, W2) + b2[:, None, :]
        y_tok = jnp.transpose(y, (1, 0, 2))
        sel = jnp.take_along_axis(y_tok, top_idx[:, :, None], axis=1)
        out = (weights[:, :, None] * sel).sum(axis=1)
        return out.reshape(B, S, D)
    h = _L0_tok_ref(x, L0_tok_emb_2, L0_tok_emb_3, L0_tok_emb_4)
    h = h + _L0_attn_ref(_layernorm(h, axis=-1), L0_attn_slow_W, L0_attn_out_W, L0_attn_ln_g, L0_attn_ln_b)
    h = h + _L0_ffn_ref(_layernorm(h, axis=-1), L0_ffn_gate_w, L0_ffn_gate_b, L0_ffn_w1, L0_ffn_b1, L0_ffn_w2, L0_ffn_b2)
    h = h + _L1_attn_ref(_layernorm(h, axis=-1), L1_attn_W_K, L1_attn_W_V, L1_attn_W_Q, L1_attn_conv_k, L1_attn_conv_v, L1_attn_conv_q, L1_attn_W_th, L1_attn_b_th, L1_attn_W_et, L1_attn_b_et, L1_attn_W_al, L1_attn_b_al, L1_attn_W1, L1_attn_W2, L1_attn_ln_g, L1_attn_ln_b, L1_attn_W_gate, L1_attn_W_proj)
    h = h + _L1_ffn_ref(_layernorm(h, axis=-1), L1_ffn_Wg, L1_ffn_bg, L1_ffn_W1, L1_ffn_b1, L1_ffn_W2, L1_ffn_b2)
    h = h + _L2_attn_ref(_layernorm(h, axis=-1), L2_attn_qkv_w, L2_attn_qkv_b, L2_attn_proj_w, L2_attn_proj_b)
    h = h + _L2_ffn_ref(_layernorm(h, axis=-1), L2_ffn_gamma, L2_ffn_beta, L2_ffn_Wr, L2_ffn_br, L2_ffn_W1, L2_ffn_b1, L2_ffn_W2, L2_ffn_b2)
    h = h + _L3_attn_ref(_layernorm(h, axis=-1), L3_attn_W)
    h = h + _L3_ffn_ref(_layernorm(h, axis=-1), L3_ffn_Wr, L3_ffn_br, L3_ffn_ln_g, L3_ffn_ln_b, L3_ffn_W1, L3_ffn_b1, L3_ffn_W2, L3_ffn_b2)
    return h

_drawn_inputs = setup_inputs


def setup_inputs(seed=0):
    import zlib

    import numpy as np

    out = dict(_drawn_inputs(seed))
    spreads = {'L0_attn_ln_g': (1.0, 0.6),
     'L0_attn_ln_b': (0.0, 0.548),
     'L0_ffn_gate_b': (0.0, 0.1),
     'L0_ffn_b1': (0.0, 0.328),
     'L0_ffn_b2': (0.0, 0.1),
     'L1_attn_b_th': (0.0, 2.0),
     'L1_attn_b_et': (0.0, 0.8),
     'L1_attn_b_al': (0.0, 0.694),
     'L1_attn_ln_g': (1.0, 0.2),
     'L1_attn_ln_b': (0.0, 0.1),
     'L1_ffn_bg': (0.0, 0.1),
     'L1_ffn_b1': (0.0, 0.1),
     'L1_ffn_b2': (0.0, 0.1),
     'L2_attn_qkv_b': (0.0, 0.1),
     'L2_attn_proj_b': (0.0, 0.1),
     'L2_ffn_br': (0.0, 0.1),
     'L3_ffn_br': (0.0, 0.1),
     'L3_ffn_ln_g': (1.0, 0.2),
     'L3_ffn_ln_b': (0.0, 0.327),
     'L3_ffn_b1': (0.0, 0.277),
     'L3_ffn_b2': (0.0, 0.1)}
    factors = {'L0_attn_slow_W': 4.08,
     'L0_attn_out_W': 4.219,
     'L1_attn_W_et': 2.843,
     'L1_attn_W_al': 2.744,
     'L2_ffn_gamma': 7.155,
     'L2_ffn_beta': 5.881,
     'L2_ffn_W1': 3.056,
     'L2_ffn_b1': 5.049,
     'L2_ffn_W2': 2.717,
     'L2_ffn_b2': 3.231}
    for name, (base, spread) in spreads.items():
        noise = np.random.default_rng([zlib.crc32(name.encode()), seed]).standard_normal(out[name].shape)
        drawn = base * np.exp(spread * noise) if base else spread * noise
        out[name] = jnp.asarray(drawn.astype(out[name].dtype))
    for name, factor in factors.items():
        out[name] = (out[name] * factor).astype(out[name].dtype)
    return out
```

```python
from contextlib import ExitStack

import numpy as np

import concourse.bass as bass
from concourse import mybir

F32 = mybir.dt.float32
F32R = mybir.dt.float32r
I32 = mybir.dt.int32
U32 = mybir.dt.uint32
ALU = mybir.AluOpType
ACT = mybir.ActivationFunctionType
X = mybir.AxisListType.X

P = 128
B, T, D = 8, 512, 64
N = B * T
TILES = N // P
CT = T // P
E = 8
EPS = 1e-5


class Chain:

    def __init__(self, engine, done):
        self.engine, self.done, self.count = engine, done, 0

    def restart(self):
        self.engine.sem_clear(self.done)
        self.count = 0

    def __call__(self, instruction):
        self.count += 1
        instruction.then_inc(self.done, 1)
        self.engine.wait_ge(self.done, self.count)


class Stage:

    def __init__(self, nc, ctx, name):
        self.nc, self.ctx, self.name = nc, ctx, name
        self.sems = []

    def sb(self, name, shape, dt=F32):
        return self.ctx.enter_context(self.nc.sbuf_tensor(f"{self.name}_{name}", shape, dt))

    def ps(self, name, shape, dt=F32):
        return self.ctx.enter_context(self.nc.psum_tensor(f"{self.name}_{name}", shape, dt))

    def sem(self, name):
        self.sems.append(self.ctx.enter_context(self.nc.semaphore(f"{self.name}_{name}")))
        return self.sems[-1]

    def clear(self):
        numbers = sorted(sem.num for sem in self.sems)
        runs = []
        for n in numbers:
            if runs and n == runs[-1][1]:
                runs[-1][1] = n + 1
            else:
                runs.append([n, n + 1])
        with self.nc.Block() as block:
            @block.gpsimd
            def _(pool):
                for first, end in runs:
                    pool.sem_clear(range(first, end))


def spread(ap, n):
    return ap.unsqueeze(len(ap.shape)).to_broadcast([*ap.shape, n])


def pow_minus_half(pool, out, in_, minus_half):
    return pool.tensor_tensor(out, in_, minus_half, ALU.pow)


def constants(nc, g):
    s = Stage(nc, g["ctx"], "const")
    ident = s.sb("ident", [P, P])
    upto = s.sb("upto", [P, P])
    ones = s.sb("ones", [P, P])
    minus_half = s.sb("minus_half", [P, TILES])
    before = s.sb("before", [P, CT, E, E])
    filled, done = s.sem("filled"), s.sem("done")
    with nc.Block() as block:
        @block.gpsimd
        def _(pool):
            pool.memset(ident[:, :], 0.0).then_inc(filled, 1)
            pool.memset(upto[:, :], 1.0).then_inc(filled, 1)
            pool.memset(before[:, :, :, :], 1.0).then_inc(filled, 1)
            pool.memset(ones[:, :], 1.0).then_inc(done, 1)
            pool.memset(minus_half[:, :], -0.5).then_inc(done, 1)
            pool.wait_ge(filled, 3)
            pool.affine_select(out=ident[:, :], in_=ident[:, :], compare_op=ALU.not_equal, fill=1.0,
                               base=0, pattern=[[-1, P]], channel_multiplier=1).then_inc(done, 1)
            pool.affine_select(out=upto[:, :], in_=upto[:, :], compare_op=ALU.is_ge, fill=0.0,
                               base=0, pattern=[[1, P]], channel_multiplier=-1).then_inc(done, 1)
            pool.affine_select(out=before[:, :, :, :], in_=before[:, :, :, :], compare_op=ALU.is_ge,
                               fill=0.0, base=-1, pattern=[[0, CT], [1, E], [-1, E]],
                               channel_multiplier=0).then_inc(done, 1)
            pool.wait_ge(done, 5)
    s.clear()
    g.update(ident=ident, upto=upto, ones=ones, minus_half=minus_half, before=before)


class Norm:

    def __init__(self, s, g, count=1):
        self.g = g
        self.stat = s.sb("norm_stat", [P, TILES])
        self.square = s.sb("norm_square", [P, TILES, D])
        self.var_ready, self.rstd_ready = s.sem("var_ready"), s.sem("rstd_ready")
        self.count = count
        self.done = 0

    def vector(self, dve, link, x, out, gamma=None, beta=None):
        stat, square = self.stat, self.square
        link(dve.tensor_reduce(stat[:, :], x, X, ALU.add))
        link(dve.scalar_tensor_tensor(out=out, in0=spread(stat[:, :], D), scalar=-1.0 / D, in1=x,
                                      op0=ALU.mult, op1=ALU.add))
        link(dve.tensor_tensor(square[:, :, :], out, out, ALU.mult))
        link(dve.tensor_reduce(stat[:, :], square[:, :, :], X, ALU.add))
        dve.tensor_scalar(stat[:, :], stat[:, :], 1.0 / D, EPS, ALU.mult, ALU.add)\
            .then_inc(self.var_ready, 1)
        self.done += 1
        dve.wait_ge(self.rstd_ready, self.done)
        link(dve.tensor_tensor(out, out, spread(stat[:, :], D), ALU.mult))
        if gamma is not None:
            rows = lambda v: v.unsqueeze(1).to_broadcast([P, TILES, D])
            link(dve.tensor_tensor(out, out, rows(gamma), ALU.mult))
            link(dve.tensor_tensor(out, out, rows(beta), ALU.add))

    def gpsimd(self, pool):
        for n in range(self.count):
            pool.wait_ge(self.var_ready, n + 1)
            pool.tensor_tensor(self.stat[:, :], self.stat[:, :], self.g["minus_half"][:, :], ALU.pow)\
                .then_inc(self.rstd_ready, 1)


def row_bc(ap, n):
    flat = ap if len(ap.shape) == 1 else ap.rearrange("a b -> (a b)")
    return flat.unsqueeze(0).to_broadcast([n, flat.shape[0]])


def turn_pairs(pe, out, rows, ident, count):
    for k in range(count // 2):
        last = pe.transpose(out[:, k * P:(k + 1) * P],
                            rows[:, 2 * k:2 * k + 2, :].rearrange("p a d -> p (a d)"), ident[:, :])
    return last


def take_pairs(copy, xT, turned, count):
    pairs = xT.rearrange("d (k a q) -> d k a q", a=2, q=P)
    for a in range(2):
        last = copy(pairs[:, :, a, :], turned[a * D:(a + 1) * D, 0:count // 2 * P]
                    .rearrange("d (k q) -> d k q", q=P))
    return last


PRIME, VOCAB = 31, 125000
GRAMS = (2, 3, 4)
BACK = GRAMS[-1] - 1


def token_stage(nc, g, ids, tables):
    h = g["h"]
    W = P + BACK
    with ExitStack() as ctx:
        s = Stage(nc, ctx, "tok")
        ids_row = s.sb("ids_row", [TILES, W], I32)
        ids_f = s.sb("ids_f", [TILES, W])
        hashes = s.sb("hashes", [TILES, len(GRAMS), W])
        quot_i = s.sb("quot_i", [TILES, W], I32)
        quot = s.sb("quot", [TILES, W])
        index = s.sb("index", [P, len(GRAMS), TILES], U32)
        rows = [s.sb(f"rows{n}", [P, TILES, D]) for n in GRAMS]
        index_ps = s.ps("index_ps", [P, len(GRAMS), TILES])
        cleared, loaded, hashed = s.sem("cleared"), s.sem("loaded"), s.sem("hashed")
        turned, indexed, chained = s.sem("turned"), s.sem("indexed"), s.sem("chained")
        gathered = g["ctx"].enter_context(nc.semaphore("tok_gathered"))
        flat = ids.rearrange("b t -> (b t)")
        with nc.Block() as block:
            @block.sync
            def _(sp):
                sp.wait_ge(cleared, 1)
                sp.dma_start(ids_row[0:1, BACK:W], flat[0:P].unsqueeze(0)).then_inc(loaded, 16)
                for k in range(0, W, P):
                    width = min(P, W - k)
                    rows_of = flat[P - BACK:N - BACK].rearrange("(j c) -> j c", c=P) if k == 0 else \
                        ids.rearrange("b t -> (b t)").rearrange("(j c) -> j c", c=P)[1:TILES, P - BACK:P]
                    sp.dma_start(ids_row[1:TILES, k:k + width], rows_of[:, 0:width]).then_inc(loaded, 16)

            @block.gpsimd
            def _(pool):
                pool.wait_ge(indexed, 1)
                for n, table in enumerate(tables):
                    for j in range(TILES):
                        pool.indirect_dma_start(
                            rows[n][:, j, :], None, table,
                            bass.IndirectOffsetOnAxis(ap=index[:, n, j:j + 1], axis=0)).then_inc(gathered, 16)

            @block.tensor
            def _(pe):
                pe.wait_ge(hashed, 1)
                for n in range(len(GRAMS)):
                    last = pe.transpose(index_ps[:, n, :], hashes[:, n, BACK:W], g["ident"][0:TILES, 0:TILES])
                last.then_inc(turned, 1)

            @block.vector
            def _(dve):
                link = Chain(dve, chained)
                dve.memset(ids_row[:, :], 0).then_inc(cleared, 1)
                dve.wait_ge(loaded, 48)
                link(dve.tensor_copy(ids_f[:, :], ids_row[:, :]))
                link(dve.memset(hashes[:, :, :], 0.0))
                before = ids_f[:, :]
                for n in range(len(GRAMS)):
                    v = hashes[:, n, n + 1:W]
                    q, qi = quot[:, n + 1:W], quot_i[:, n + 1:W]
                    link(dve.scalar_tensor_tensor(out=v, in0=before[:, n:W - 1], scalar=float(PRIME),
                                                  in1=ids_f[:, n + 1:W], op0=ALU.mult, op1=ALU.add))
                    link(dve.tensor_scalar(qi, v, 1.0 / VOCAB, None, ALU.mult))
                    link(dve.tensor_copy(q, qi))
                    link(dve.scalar_tensor_tensor(out=v, in0=q, scalar=-float(VOCAB), in1=v,
                                                  op0=ALU.mult, op1=ALU.add))
                    link(dve.tensor_scalar(q, v, 0.0, float(VOCAB), ALU.is_lt, ALU.mult))
                    link(dve.tensor_tensor(v, v, q, ALU.add))
                    link(dve.tensor_scalar(q, v, float(VOCAB), -float(VOCAB), ALU.is_ge, ALU.mult))
                    link(dve.tensor_tensor(v, v, q, ALU.add))
                    before = hashes[:, n, :]
                dve.sem_inc(hashed, 1)
                dve.wait_ge(turned, 1)
                dve.tensor_copy(index[:, :, :], index_ps[:, :, :]).then_inc(indexed, 1)
                dve.wait_ge(gathered, 16 * len(GRAMS) * TILES)
                for n in range(len(GRAMS)):
                    link(dve.memset(rows[n][0:n + 1, 0:TILES:CT, :], 0.0))
                link(dve.tensor_tensor(h[:, :, :], rows[0][:, :, :], rows[1][:, :, :], ALU.add))
                link(dve.tensor_tensor(h[:, :, :], h[:, :, :], rows[2][:, :, :], ALU.add))
                link(dve.tensor_scalar(h[:, :, :], h[:, :, :], 1.0 / (len(GRAMS) + 1), None, ALU.mult))
        s.clear()


RNN_HEADS, RNN_DH = 8, 32
RNN_C = RNN_HEADS * RNN_DH
STEPS = B


def recurrent_stage(nc, g, w):
    h, ident = g["h"], g["ident"]
    with ExitStack() as ctx:
        s = Stage(nc, ctx, "rnn")
        wide = 5 * RNN_C + 2 * RNN_HEADS
        w_in = s.sb("w_in", [D, wide])
        w_out = s.sb("w_out", [P, 2, D])
        gb = s.sb("gb", [P, 2, D])
        x = s.sb("x", [P, TILES, D])
        x_rows = s.sb("x_rows", [P, STEPS, D])
        xT = s.sb("xT", [D, STEPS, P])
        qk = s.sb("qk", [P, STEPS, 2 * RNN_C])
        pos = s.sb("pos", [P, STEPS, 2 * RNN_C])
        val = s.sb("val", [P, STEPS, RNN_C])
        rkey = s.sb("rkey", [P, STEPS, RNN_C])
        rval = s.sb("rval", [P, STEPS, RNN_C])
        rate = s.sb("rate", [P, STEPS, 2, RNN_HEADS])
        u = s.sb("u", [P, STEPS, RNN_C])
        z = s.sb("z", [P, STEPS, RNN_C])
        prod = s.sb("prod", [P, STEPS, RNN_C])
        dots = s.sb("dots", [P, STEPS, RNN_HEADS])
        query = s.sb("query", [P, RNN_C])
        old = s.sb("old", [P, RNN_C])
        stat = s.sb("stat", [P, STEPS * 2 * RNN_HEADS])
        zT = s.sb("zT", [P, 2, P])
        turn_ps = [s.ps(f"turn_ps{n}", [P, T]) for n in range(2)]
        in_ps = [[s.ps(f"in_ps{n}{k}", [P, T]) for k in range(3)] for n in range(2)]
        norm = Norm(s, g, 2)
        names = ["loaded", "chained", "x_ready", "rows_ready", "rows_turned", "xT_ready", "projected",
                 "qk_taken", "rest_taken", "neg_ready", "neg_exp", "rkey_ready", "rkey_exp", "rate_exp",
                 "h_ready", "h_exp", "z_ready", "z_turned", "zT_ready", "z_out", "out_taken"]
        (loaded, chained, x_ready, rows_ready, rows_turned, xT_ready, projected, qk_taken, rest_taken,
         neg_ready, neg_exp, rkey_ready, rkey_exp, rate_exp, h_ready, h_exp, z_ready, z_turned, zT_ready,
         z_out, out_taken) = [s.sem(n) for n in names]
        heads = lambda v: v.rearrange("p s (h d) -> p (s h) d", d=RNN_DH)

        with nc.Block() as block:
            @block.sync
            def _(sp):
                sp.dma_start(w_in[:, :], w["w_in"]).then_inc(loaded, 16)
                sp.dma_start(w_out[:, :, :], w["w_out"]).then_inc(loaded, 16)
                sp.dma_start(gb[:, 0, :], row_bc(w["ln_g"], P)).then_inc(loaded, 16)
                sp.dma_start(gb[:, 1, :], row_bc(w["ln_b"], P)).then_inc(loaded, 16)

            @block.gpsimd
            def _(pool):
                norm.gpsimd(pool)
                pool.wait_ge(x_ready, 1)
                with pool.Fori(0, CT) as i:
                    pool.wait_ge(rows_turned, i + 1)
                    pool.tensor_copy(x_rows[:, :, :], x[:, bass.ds(i, STEPS, step=CT), :])\
                        .then_inc(rows_ready, 1)

            @block.tensor
            def _(pe):
                pe.wait_ge(loaded, 64)
                pe.sem_inc(rows_turned, 1)
                with pe.Fori(0, CT) as i:
                    pe.wait_ge(rows_ready, i + 1)
                    turn_pairs(pe, turn_ps[0], x_rows, ident, STEPS).then_inc(rows_turned, 1)
                    pe.wait_ge(xT_ready, i + 1)
                    for t in range(STEPS):
                        pe.wait_ge(qk_taken, i * STEPS + (t + 1))
                        pe.wait_ge(rest_taken, i * STEPS + (t + 1))
                        for k in range(3):
                            width = min(2 * RNN_C, wide - 2 * RNN_C * k)
                            last = pe.matmul(in_ps[t % 2][k][:, 0:width], xT[:, t, :],
                                             w_in[:, 2 * RNN_C * k:2 * RNN_C * k + width], start=True, stop=True)
                        last.then_inc(projected, 1)
                    pe.wait_ge(z_ready, i + 1)
                    for t in range(STEPS):
                        pe.wait_ge(zT_ready, i * STEPS + (t + 1))
                        for k in range(2):
                            last = pe.transpose(turn_ps[0][:, k * P:(k + 1) * P], z[:, t, k * P:(k + 1) * P],
                                                ident[:, :])
                        last.then_inc(z_turned, 1)
                        pe.wait_ge(zT_ready, i * STEPS + (t + 2))
                        for k in range(2):
                            last = pe.matmul(turn_ps[1][:, t * D:(t + 1) * D], zT[:, k, :], w_out[:, k, :],
                                             start=(k == 0), stop=(k == 1))
                        last.then_inc(z_out, 1)
                    pe.wait_ge(out_taken, i + 1)

            @block.scalar
            def _(a):
                a.wait_ge(loaded, 64)
                a.sem_inc(rest_taken, 2)
                a.sem_inc(zT_ready, 1)
                with a.Fori(0, CT) as i:
                    a.wait_ge(rows_turned, i + 2)
                    take_pairs(lambda o, i_: a.activation(o, i_, ACT.Copy),
                               xT[:, :, :].rearrange("d s q -> d (s q)"), turn_ps[0], STEPS).then_inc(xT_ready, 1)
                    for t in range(STEPS):
                        a.wait_ge(projected, i * STEPS + (t + 1))
                        _, b, c = in_ps[t % 2]
                        a.activation(val[:, t, :], b[:, 0:RNN_C], ACT.Copy)
                        a.activation(rkey[:, t, :], b[:, RNN_C:2 * RNN_C], ACT.Copy)
                        a.activation(rval[:, t, :], c[:, 0:RNN_C], ACT.Copy)
                        a.activation(rate[:, t, :, :],
                                     c[:, RNN_C:RNN_C + 2 * RNN_HEADS].rearrange("p (a h) -> p a h", a=2),
                                     ACT.Exp, scale=-1.0).then_inc(rest_taken, 1)
                    a.wait_ge(neg_ready, i + 1)
                    a.activation(qk[:, :, :], qk[:, :, :], ACT.Exp).then_inc(neg_exp, 1)
                    a.wait_ge(rkey_ready, i + 1)
                    a.activation(rkey[:, :, :], rkey[:, :, :], ACT.Exp).then_inc(rkey_exp, 1)
                    for t in range(1, STEPS):
                        a.wait_ge(h_ready, i * (STEPS - 1) + t)
                        a.activation(query[:, :], query[:, :], ACT.Exp).then_inc(h_exp, 1)
                    for t in range(STEPS):
                        a.wait_ge(z_turned, i * STEPS + (t + 1))
                        a.wait_ge(z_out, i * STEPS + (t + 1))
                        a.activation(zT[:, :, :], turn_ps[0][:, 0:2 * P].rearrange("p (k q) -> p k q", k=2),
                                     ACT.Copy).then_inc(zT_ready, 1)

            @block.vector
            def _(dve):
                link = Chain(dve, chained)
                dve.wait_ge(loaded, 64)
                norm.vector(dve, link, h[:, :, :], x[:, :, :])
                link(dve.tensor_tensor(h[:, :, :], h[:, :, :], x[:, :, :], ALU.add))
                norm.vector(dve, link, x[:, :, :], x[:, :, :], gb[:, 0, :], gb[:, 1, :])
                dve.sem_inc(x_ready, 1)
                dve.sem_inc(qk_taken, 2)
                dve.sem_inc(z_out, 1)
                with dve.Fori(0, CT) as i:
                    link.restart()
                    for t in range(STEPS):
                        dve.wait_ge(projected, i * STEPS + (t + 1))
                        a = in_ps[t % 2][0]
                        dve.tensor_scalar(pos[:, t, :], a[:, :], 0.0, None, ALU.max)
                        dve.tensor_scalar(qk[:, t, :], a[:, :], 0.0, None, ALU.min).then_inc(qk_taken, 1)
                    dve.wait_ge(qk_taken, i * STEPS + (STEPS + 2))
                    dve.sem_inc(neg_ready, 1)
                    dve.wait_ge(rest_taken, i * STEPS + (STEPS + 2))
                    r = heads(rkey[:, :, :])
                    small = stat[:, 0:STEPS * RNN_HEADS]
                    link(dve.tensor_reduce(small, r, X, ALU.max))
                    link(dve.tensor_tensor(r, r, spread(small, RNN_DH), ALU.subtract))
                    dve.sem_inc(rkey_ready, 1)
                    link(dve.tensor_scalar(rate[:, :, :, :], rate[:, :, :, :], 1.0, None, ALU.add))
                    link(dve.reciprocal(rate[:, :, :, :], rate[:, :, :, :]))
                    dve.wait_ge(neg_exp, i + 1)
                    link(dve.tensor_tensor(qk[:, :, :], qk[:, :, :], pos[:, :, :], ALU.add))
                    v = heads(qk[:, :, :])
                    link(dve.tensor_reduce(stat[:, :], v, X, ALU.add))
                    link(dve.reciprocal(stat[:, :], stat[:, :]))
                    link(dve.tensor_tensor(v, v, spread(stat[:, :], RNN_DH), ALU.mult))
                    dve.wait_ge(rkey_exp, i + 1)
                    link(dve.tensor_reduce(small, r, X, ALU.add))
                    link(dve.reciprocal(small, small))
                    link(dve.tensor_tensor(r, r, spread(small, RNN_DH), ALU.mult))

                    def recall(keys, values, by, count, out):
                        if not count:
                            return
                        pr = prod[:, 0:count, :]
                        link(dve.tensor_tensor(pr, keys, by.unsqueeze(1).to_broadcast([P, count, RNN_C]), ALU.mult))
                        dt = dots[:, 0:count, :].rearrange("p s h -> p (s h)")
                        link(dve.tensor_reduce(dt, heads(pr), X, ALU.add))
                        link(dve.tensor_tensor(heads(pr), heads(values), spread(dt, RNN_DH), ALU.mult))
                        link(dve.tensor_reduce(out, pr.rearrange("p s c -> p c s"), X, ALU.add))

                    def write(t, values, gate):
                        rate_t = spread(rate[:, t, gate, :], RNN_DH)
                        if t:
                            link(dve.tensor_tensor(old[:, :], values[:, t, :], old[:, :], ALU.subtract))
                        src = old[:, :] if t else values[:, t, :]
                        link(dve.tensor_tensor(u[:, t, :].rearrange("p (h d) -> p h d", d=RNN_DH),
                                               src.rearrange("p (h d) -> p h d", d=RNN_DH), rate_t, ALU.mult))

                    for t in range(STEPS):
                        recall(qk[:, 0:t, RNN_C:2 * RNN_C], u[:, 0:t, :], qk[:, t, RNN_C:2 * RNN_C], t, old[:, :])
                        write(t, val, 0)
                        recall(qk[:, 0:t + 1, RNN_C:2 * RNN_C], u[:, 0:t + 1, :], qk[:, t, 0:RNN_C], t + 1, z[:, t, :])
                    one_head = query[:, :].rearrange("p (h d) -> p h d", d=RNN_DH)
                    few = stat[:, 0:RNN_HEADS]
                    for t in range(STEPS):
                        if t == 0:
                            link(dve.memset(query[:, :], 1.0 / RNN_DH))
                        else:
                            zp = z[:, t - 1, :].rearrange("p (h d) -> p h d", d=RNN_DH)
                            link(dve.tensor_reduce(few, zp, X, ALU.max))
                            dve.tensor_tensor(one_head, zp, spread(few, RNN_DH), ALU.subtract).then_inc(h_ready, 1)
                        recall(rkey[:, 0:t, :], u[:, 0:t, :], rkey[:, t, :], t, old[:, :])
                        write(t, rval, 1)
                        if t:
                            dve.wait_ge(h_exp, i * (STEPS - 1) + t)
                            link(dve.tensor_reduce(few, one_head, X, ALU.add))
                            link(dve.reciprocal(few, few))
                            link(dve.tensor_tensor(one_head, one_head, spread(few, RNN_DH), ALU.mult))
                        recall(rkey[:, 0:t + 1, :], u[:, 0:t + 1, :], query[:, :], t + 1, old[:, :])
                        link(dve.tensor_tensor(z[:, t, :], z[:, t, :], old[:, :], ALU.add))
                    dve.sem_inc(z_ready, 1)
                    dve.wait_ge(z_out, i * STEPS + (STEPS + 1))
                    h_rows = h[:, bass.ds(i, STEPS, step=CT), :]
                    dve.tensor_tensor(h_rows, h_rows, turn_ps[1][:, :].rearrange("p (s d) -> p s d", s=STEPS),
                                      ALU.add).then_inc(out_taken, 1)
        s.clear()


PAIRS = E // 2


def expert_stage(nc, g, name, w, act, per_expert, gating, top, capacity=None, norms=1,
                 gamma_beta=None, expert_norm=None, limit_infinite=False):
    h, ident, ones = g["h"], g["ident"], g["ones"]
    blocks = E * per_expert
    pair = 2 * per_expert
    with ExitStack() as ctx:
        s = Stage(nc, ctx, name)
        w1 = s.sb("w1", [P, blocks * P])
        w1_high = s.sb("w1_high", [P, blocks * P], F32R)
        w1_low = s.sb("w1_low", [P, blocks * P], F32R)
        w2 = s.sb("w2", [P, blocks, D])
        b1 = s.sb("b1", [P, blocks])
        b2 = s.sb("b2", [P, PAIRS])
        wg = s.sb("wg", [P, E])
        wg_high = s.sb("wg_high", [P, E], F32R)
        wg_low = s.sb("wg_low", [P, E], F32R)
        bg = s.sb("bg", [P, E])
        x = s.sb("x", [P, TILES + CT, D])
        x_now = s.sb("x_now", [P, CT, D])
        x_chunk = s.sb("x_chunk", [P, CT, 2, D], F32R)
        xT = s.sb("xT", [P, T], F32R)
        hidden = s.sb("hidden", [P, 2, T])
        logit = s.sb("logit", [P, CT, E])
        share = s.sb("share", [P, CT, E])
        gate = s.sb("gate", [P, CT, E])
        stat = s.sb("stat", [P, CT])
        pairs = s.sb("pairs", [P, CT, E, E])
        ties = s.sb("ties", [P, CT, E, E])
        rank = s.sb("rank", [P, CT, E])
        yT = s.sb("yT", [P, 2, T])
        y = s.sb("y", [P, CT, E * D])
        warm = s.sb("warm", [P, 1])
        total = s.sb("total", [P, CT, D])
        xT_ps = s.ps("xT_ps", [P, T])
        small_ps = s.ps("small_ps", [P, T])
        hid_ps = [s.ps(f"hid_ps{n}", [P, T]) for n in range(2)]
        y_ps = [s.ps(f"y_ps{n}", [P, T]) for n in range(2)]
        back_ps = [s.ps(f"back_ps{n}", [P, T]) for n in range(2)]
        norm = Norm(s, g, norms)
        loaded, chained = s.sem("loaded"), s.sem("chained")
        w_split, x_high, past_end = s.sem("w_split"), s.sem("x_high"), s.sem("past_end")
        x_ready, chunk_ready, chunk_turned = s.sem("x_ready"), s.sem("chunk_ready"), s.sem("chunk_turned")
        xT_ready, logits_ready, shifted = s.sem("xT_ready"), s.sem("logits_ready"), s.sem("shifted")
        exp_ready = s.sem("exp_ready")
        hid_ready, act_done, y_done = s.sem("hid_ready"), s.sem("act_done"), s.sem("y_done")
        yT_ready, y_back, back_taken = s.sem("yT_ready"), s.sem("y_back"), s.sem("back_taken")
        small_taken = s.sem("small_taken")
        gb = None
        loads = 8
        if gamma_beta:
            gb = s.sb("gamma_beta", [P, 2, D])
            loads += 2
        if expert_norm:
            eg, eb = s.sb("expert_g", [P, E]), s.sb("expert_b", [D, E])
            bias_ready, scaled = s.sem("bias_ready"), s.sem("scaled")
            loads += 3
        if capacity:
            picked, counted = s.sem("picked"), s.sem("counted")
            base = s.sb("base", [P, CT + 1, E])
            place = s.sb("place", [P, CT, E])
        if limit_infinite:
            odd = s.sb("odd", [P, CT * D], U32)
            filler = s.sb("filler", [P, 3, CT * D])

        with nc.Block() as block:
            @block.sync
            def _(sp):
                for half in (slice(0, D), slice(D, P)):
                    sp.dma_start(w1[half, :], w["w1"]).then_inc(loaded, 16)
                    sp.dma_start(wg[half, :], w["wg"]).then_inc(loaded, 16)
                sp.dma_start(w2[:, :, :], w["w2"]).then_inc(loaded, 16)
                sp.dma_start(b1[:, :], w["b1"]).then_inc(loaded, 16)
                sp.dma_start(b2[:, :], w["b2"]).then_inc(loaded, 16)
                sp.dma_start(bg[:, :], row_bc(w["bg"], P)).then_inc(loaded, 16)
                if gamma_beta:
                    sp.dma_start(gb[:, 0, :], row_bc(gamma_beta[0], P)).then_inc(loaded, 16)
                    sp.dma_start(gb[:, 1, :], row_bc(gamma_beta[1], P)).then_inc(loaded, 16)
                if expert_norm:
                    sp.dma_start(eg[0:D, :], expert_norm[0]).then_inc(loaded, 16)
                    sp.dma_start(eg[D:P, :], expert_norm[0]).then_inc(loaded, 16)
                    sp.dma_start(eb[:, :], expert_norm[1]).then_inc(loaded, 16)

            @block.gpsimd
            def _(pool):
                pool.memset(x[:, TILES:, :], 0.0).then_inc(past_end, 1)
                pool.wait_ge(loaded, 16 * loads)
                if expert_norm:
                    pool.wait_ge(scaled, 1)
                pool.tensor_copy(w1_high[:, :], w1[:, :]).then_inc(w_split, 1)
                pool.tensor_copy(wg_high[:, :], wg[:, :]).then_inc(w_split, 1)
                pool.wait_ge(w_split, 2)
                pool.tensor_tensor(w1_low[:, :], w1[:, :], w1_high[:, :], ALU.subtract).then_inc(w_split, 1)
                pool.tensor_tensor(wg_low[:, :], wg[:, :], wg_high[:, :], ALU.subtract).then_inc(w_split, 1)
                norm.gpsimd(pool)
                pool.wait_ge(x_ready, 1)
                pool.wait_ge(past_end, 1)
                with pool.Fori(0, B + 1) as i:
                    pool.wait_ge(chunk_turned, i + 1)
                    pool.tensor_copy(x_now[:, :, :], x[:, bass.ds(i * CT, CT), :]).then_inc(x_high, 1)
                    pool.wait_ge(x_high, 1)
                    pool.tensor_copy(x_chunk[:, :, 0, :], x_now[:, :, :]).then_inc(x_high, 1)
                    pool.wait_ge(x_high, 2)
                    pool.tensor_tensor(x_chunk[:, :, 1, :], x_now[:, :, :], x_chunk[:, :, 0, :], ALU.subtract)\
                        .then_inc(chunk_ready, 1)
                    pool.sem_clear(x_high)

            @block.tensor
            def _(pe):
                pe.wait_ge(loaded, 16 * loads)
                if expert_norm:
                    for n in range(blocks):
                        last = pe.matmul(small_ps[:, 64 + n:65 + n], w1[0:D, n * P:(n + 1) * P],
                                         eb[:, n // per_expert:n // per_expert + 1], start=True, stop=True)
                    last.then_inc(bias_ready, 1)
                pe.wait_ge(w_split, 4)
                pe.sem_inc(chunk_turned, 1)
                pe.sem_inc(y_done, 2)

                def turn_chunk():
                    for j in range(CT):
                        last = pe.transpose(xT_ps[:, j * P:(j + 1) * P],
                                            x_chunk[:, j, :, :].rearrange("p a d -> p (a d)").bitcast(F32),
                                            ident[:, :])
                    last.then_inc(chunk_turned, 1)

                pe.wait_ge(chunk_ready, 1)
                turn_chunk()

                def hidden_block(n, freed):
                    pe.wait_ge(act_done, freed)
                    pe.matmul(hid_ps[n % 2][:, :], w1_high[:, n * P:(n + 1) * P], xT[:, :],
                              start=True, stop=False)
                    pe.matmul(hid_ps[n % 2][:, :], w1_low[:, n * P:(n + 1) * P], xT[:, :],
                              start=False, stop=True).then_inc(hid_ready, 1)

                pe.wait_ge(xT_ready, 1)
                hidden_block(0, 1)
                with pe.Fori(0, B) as i:
                    def turn_back(q):
                        pe.wait_ge(yT_ready, i * PAIRS + (q + 3))
                        pe.wait_ge(back_taken, i * PAIRS + (q + 1))
                        for j in range(CT):
                            last = pe.transpose(back_ps[q % 2][:, j * P:(j + 1) * P],
                                                yT[:, q % 2, j * P:(j + 1) * P], ident[:, :])
                        last.then_inc(y_back, 1)

                    pe.wait_ge(small_taken, i + 1)
                    for j in range(CT):
                        for part in (wg_high, wg_low):
                            last = pe.matmul(small_ps[:, j * E:(j + 1) * E], xT[:, j * P:(j + 1) * P],
                                             part[:, :], start=(part is wg_high), stop=(part is wg_low))
                    last.then_inc(logits_ready, 1)
                    for n in range(blocks):
                        if n + 1 < blocks:
                            hidden_block(n + 1, i * blocks + (n + 2))
                        if n == blocks // 2 + 1 and capacity:
                            pe.wait_ge(picked, i + 1)
                            pe.matmul(small_ps[:, 32:64], g["upto"][:, :], rank[:, :, :], start=True, stop=True)
                            pe.matmul(small_ps[:, 64:96], g["ones"][:, :], rank[:, :, :], start=True, stop=True)\
                                .then_inc(counted, 1)
                        if n == 2:
                            pe.wait_ge(chunk_ready, i + 2)
                            turn_chunk()
                        e, part = n // per_expert, n % per_expert
                        q, side = e // 2, e % 2 * D
                        if n % pair == 0:
                            pe.wait_ge(yT_ready, i * PAIRS + (q + 1))
                        pe.wait_ge(act_done, i * blocks + (n + 3))
                        pe.matmul(y_ps[q % 2][side:side + D, :], w2[:, n, :], hidden[:, n % 2, :],
                                  start=(part == 0), stop=(part == per_expert - 1)).then_inc(y_done, 1)
                        if n % pair == 1 and q:
                            turn_back(q - 1)
                    pe.wait_ge(xT_ready, i + 2)
                    hidden_block(0, i * blocks + (blocks + 1))
                    turn_back(PAIRS - 1)

            @block.scalar
            def _(act_engine):
                a = act_engine
                a.sem_inc(act_done, 2)
                a.wait_ge(loaded, 16 * loads)
                if expert_norm:
                    a.wait_ge(scaled, 1)
                a.activation(warm[:, :], ones[:, 0:1], ACT.Exp if capacity else act)
                a.sem_inc(yT_ready, 2)
                a.wait_ge(chunk_turned, 2)
                a.activation(xT[:, :], xT_ps[:, :], ACT.Copy).then_inc(xT_ready, 1)
                with a.Fori(0, B) as i:
                    def take_pair(q):
                        a.wait_ge(y_done, i * blocks + ((q + 1) * pair + 2))
                        a.wait_ge(y_back, i * PAIRS + (q + 1))
                        a.activation(yT[:, q % 2, :], y_ps[q % 2][:, :], ACT.Identity, bias=b2[:, q:q + 1])\
                            .then_inc(yT_ready, 1)

                    for n in range(blocks):
                        a.wait_ge(hid_ready, i * blocks + (n + 1))
                        a.wait_ge(y_done, i * blocks + (n + 1))
                        a.activation(hidden[:, n % 2, :], hid_ps[n % 2][:, :], act, bias=b1[:, n:n + 1])\
                            .then_inc(act_done, 1)
                        if n and n % pair == 0:
                            take_pair(n // pair - 1)
                        if n == 3 and gating != "mask":
                            a.wait_ge(shifted, i + 1)
                            a.activation(share[:, :, :], logit[:, :, :], ACT.Exp).then_inc(exp_ready, 1)
                    a.wait_ge(chunk_turned, i + 3)
                    a.activation(xT[:, :], xT_ps[:, :], ACT.Copy).then_inc(xT_ready, 1)
                    take_pair(PAIRS - 1)

            @block.vector
            def _(dve):
                link = Chain(dve, chained)
                dve.wait_ge(loaded, 16 * loads)
                if expert_norm:
                    dve.wait_ge(bias_ready, 1)
                    link(dve.tensor_tensor(b1[:, :], b1[:, :], small_ps[:, 64:64 + blocks], ALU.add))
                    for e in range(E):
                        part = w1[:, e * per_expert * P:(e + 1) * per_expert * P]
                        link(dve.tensor_scalar(part, part, eg[:, e:e + 1], None, ALU.mult))
                    dve.sem_inc(scaled, 1)
                if capacity:
                    link(dve.memset(base[:, :, :], 0.0))
                if limit_infinite:
                    link(dve.memset(filler[:, 0, :], 1e4))
                    link(dve.memset(filler[:, 1, :], -1e4))
                    link(dve.memset(filler[:, 2, :], 0.0))
                for n in range(norms):
                    last_norm = n == norms - 1
                    norm.vector(dve, link, h[:, :, :] if n == 0 else x[:, 0:TILES, :], x[:, 0:TILES, :],
                                *((gb[:, 0, :], gb[:, 1, :]) if gamma_beta and last_norm else ()))
                dve.sem_inc(x_ready, 1)
                dve.sem_inc(back_taken, 2)
                dve.sem_inc(small_taken, 1)
                dve.sem_inc(y_back, 2)
                with dve.Fori(0, B) as i:
                    link.restart()
                    dve.wait_ge(logits_ready, i + 1)
                    link(dve.tensor_tensor(logit[:, :, :],
                                           small_ps[:, 0:CT * E].rearrange("p (j e) -> p j e", j=CT),
                                           bg[:, :].unsqueeze(1).to_broadcast([P, CT, E]), ALU.add))
                    key = logit
                    if gating != "mask":
                        link(dve.tensor_reduce(stat[:, :], logit[:, :, :], X, ALU.max))
                        dve.tensor_tensor(pairs[:, :, 0, :], logit[:, :, :], spread(stat[:, :], E),
                                          ALU.subtract).then_inc(chained, 1)
                        link.count += 1
                        dve.wait_ge(chained, link.count)
                        dve.tensor_copy(logit[:, :, :], pairs[:, :, 0, :]).then_inc(shifted, 1)
                        dve.wait_ge(exp_ready, i + 1)
                        if gating in ("top", "renormed"):
                            link(dve.tensor_reduce(stat[:, :], share[:, :, :], X, ALU.add))
                            link(dve.reciprocal(stat[:, :], stat[:, :]))
                            link(dve.tensor_tensor(share[:, :, :], share[:, :, :], spread(stat[:, :], E), ALU.mult))
                            key = share
                    k = key[:, :, :]
                    link(dve.tensor_tensor(pairs[:, :, :, :], k.unsqueeze(2).to_broadcast([P, CT, E, E]),
                                           spread(k, E), ALU.subtract))
                    flat = lambda v: v[:, :, :, :].rearrange("p j e f -> p (j e f)")
                    link(dve.scalar_tensor_tensor(out=flat(ties), in0=flat(pairs), scalar=0.0,
                                                  in1=flat(g["before"]), op0=ALU.is_equal, op1=ALU.mult))
                    link(dve.scalar_tensor_tensor(out=flat(pairs), in0=flat(pairs), scalar=0.0,
                                                  in1=flat(ties), op0=ALU.is_gt, op1=ALU.add))
                    link(dve.tensor_reduce(rank[:, :, :], pairs[:, :, :, :], X, ALU.add))
                    if gating == "mask":
                        link(dve.tensor_scalar(gate[:, :, :], rank[:, :, :], float(top), None, ALU.is_lt))
                    else:
                        link(dve.scalar_tensor_tensor(out=gate[:, :, :], in0=rank[:, :, :], scalar=float(top),
                                                      in1=share[:, :, :], op0=ALU.is_lt, op1=ALU.mult))
                    if gating in ("renormed", "softmax"):
                        link(dve.tensor_reduce(stat[:, :], gate[:, :, :], X, ALU.add))
                        link(dve.reciprocal(stat[:, :], stat[:, :]))
                        link(dve.tensor_tensor(gate[:, :, :], gate[:, :, :], spread(stat[:, :], E), ALU.mult))
                    if capacity:
                        link(dve.tensor_scalar(rank[:, :, :], rank[:, :, :], float(top), None, ALU.is_lt))
                        dve.sem_inc(picked, 1)
                        dve.wait_ge(counted, i + 1)
                        for j in range(CT):
                            link(dve.tensor_tensor(base[:, j + 1, :], base[:, j, :],
                                                   small_ps[:, 64 + j * E:64 + (j + 1) * E], ALU.add))
                        link(dve.tensor_tensor(place[:, :, :], base[:, 0:CT, :],
                                               small_ps[:, 32:64].rearrange("p (j e) -> p j e", j=CT), ALU.add))
                        link(dve.tensor_copy(base[:, 0, :], base[:, CT, :]))
                        link(dve.scalar_tensor_tensor(out=gate[:, :, :], in0=place[:, :, :], scalar=float(capacity),
                                                      in1=gate[:, :, :], op0=ALU.is_le, op1=ALU.mult))
                    dve.sem_inc(small_taken, 1)
                    for q in range(PAIRS):
                        dve.wait_ge(y_back, i * PAIRS + (q + 3))
                        dve.tensor_tensor(y[:, :, q * P:(q + 1) * P].rearrange("p j (a d) -> p j a d", a=2),
                                          back_ps[q % 2][:, :].rearrange("p (j a d) -> p j a d", j=CT, a=2),
                                          spread(gate[:, :, 2 * q:2 * q + 2], D), ALU.mult)\
                            .then_inc(back_taken, 1)
                    dve.wait_ge(back_taken, i * PAIRS + (PAIRS + 2))
                    link(dve.tensor_reduce(total[:, :, :], y[:, :, :].rearrange("p j (e d) -> p j d e", e=E),
                                           X, ALU.add))
                    if limit_infinite:
                        flat_total = total[:, :, :].rearrange("p j d -> p (j d)")
                        for n, (test, bound) in enumerate(((ALU.is_gt, 3.4028235e38), (ALU.is_lt, -3.4028235e38))):
                            link(dve.tensor_scalar(odd[:, :], flat_total, bound, None, test))
                            link(dve.copy_predicated(flat_total, odd[:, :], filler[:, n, :]))
                        link(dve.tensor_tensor(odd[:, :], flat_total, flat_total, ALU.not_equal))
                        link(dve.copy_predicated(flat_total, odd[:, :], filler[:, 2, :]))
                    h_chunk = h[:, bass.ds(i * CT, CT), :]
                    link(dve.tensor_tensor(h_chunk, h_chunk, total[:, :, :], ALU.add))
        s.clear()


MEM_DH = 256
BLK = MEM_DH // P
CHUNK = 64
NORM_MIN = 1e-12


def memory_stage(nc, g, w):
    with ExitStack() as ctx:
        s = Stage(nc, ctx, "mem")
        kept = dict(
            hkT=s.sb("hkT", [P, BLK, N]), hqT=s.sb("hqT", [P, BLK, N]), hk=s.sb("hk", [P, TILES, MEM_DH]),
            v=s.sb("v", [P, TILES, D]), gate=s.sb("gate", [P, TILES, D]), rates=s.sb("rates", [P, 3, TILES]))
        kept["retrieved"] = kept["v"]
        project(nc, g, w, kept)
        recur(nc, g, w, kept)
        give_back(nc, g, w, kept)


def project(nc, g, w, kept):
    h, ident, ones = g["h"], g["ident"], g["ones"]
    lower, upper = slice(0, D), slice(D, P)
    with ExitStack() as ctx:
        s = Stage(nc, ctx, "memp")
        maps = s.sb("maps", [D, 7, D])
        w1 = s.sb("w1", [P, MEM_DH])
        taps = s.sb("taps", [P, 2, 3])
        shift = s.sb("shift", [P, 2])
        pair_ones = s.sb("pair_ones", [P, P])
        x = s.sb("x", [P, TILES, D])
        x_chunk = s.sb("x_chunk", [P, CT, D])
        xT = s.sb("xT", [D, T])
        raw = s.sb("raw", [P, 2, T + 2])
        conv = s.sb("conv", [P, 2, T])
        square = s.sb("square", [P, T])
        length = s.sb("length", [P, T])
        sig = s.sb("sig", [P, 2, T])
        turn_ps = s.ps("turn_ps", [P, T])
        banks = [s.ps(f"job_ps{n}", [P, T]) for n in range(4)]
        norm = Norm(s, g)
        names = ["loaded", "chained", "x_ready", "chunk_ready", "chunk_turned", "xT_ready", "made", "taken",
                 "squared", "scaled", "v_ready", "paired"]
        (loaded, chained, x_ready, chunk_ready, chunk_turned, xT_ready, made, taken, squared, scaled,
         v_ready, paired) = [s.sem(n) for n in names]
        KQ, VT, EA, GATE, LENGTH, HKT, HK, HQT, VALUES, MEANS, JOBS = 0, 1, 2, 3, 4, 5, 7, 9, 11, 12, 13
        LOADS = 7 + 2 + 3 + 3

        with nc.Block() as block:
            @block.sync
            def _(sp):
                for n, name in enumerate(("W_K", "W_Q", "W_V", "W_th", "W_et", "W_al", "W_gate")):
                    sp.dma_start(maps[:, n, :], w[name]).then_inc(loaded, 16)
                for rows in (lower, upper):
                    sp.dma_start(w1[rows, :], w["W1"]).then_inc(loaded, 16)
                for rows, n, name in ((lower, 0, "conv_k"), (upper, 0, "conv_q"), (lower, 1, "conv_v")):
                    sp.dma_start(taps[rows, n, :], w[name]).then_inc(loaded, 16)
                for rows, n, name in ((upper, 0, "b_th"), (lower, 1, "b_et"), (upper, 1, "b_al")):
                    sp.dma_start(shift[rows, n:n + 1], w[name]).then_inc(loaded, 16)

            @block.gpsimd
            def _(pool):
                pool.memset(pair_ones[lower, lower], 1.0).then_inc(paired, 1)
                pool.memset(pair_ones[upper, upper], 1.0).then_inc(paired, 1)
                pool.memset(pair_ones[lower, upper], 0.0).then_inc(paired, 1)
                pool.memset(pair_ones[upper, lower], 0.0).then_inc(paired, 1)
                pool.wait_ge(paired, 4)
                norm.gpsimd(pool)
                pool.wait_ge(x_ready, 1)
                with pool.Fori(0, B) as i:
                    pool.wait_ge(chunk_turned, i + 1)
                    pool.tensor_copy(x_chunk[:, :, :], x[:, bass.ds(i * CT, CT), :])\
                        .then_inc(chunk_ready, 1)

            @block.tensor
            def _(pe):
                pe.wait_ge(loaded, 16 * LOADS)
                pe.wait_ge(paired, 4)
                pe.sem_inc(chunk_turned, 1)
                with pe.Fori(0, B) as i:
                    pe.wait_ge(chunk_ready, i + 1)
                    turn_pairs(pe, turn_ps, x_chunk, ident, CT).then_inc(chunk_turned, 1)
                    pe.wait_ge(xT_ready, i + 1)

                    def bank(n, ahead=0):
                        pe.wait_ge(taken, i * JOBS + (1 if n < 4 else n - 2 + ahead))
                        return banks[n % 4]

                    tile = lambda v, j: v[:, j * P:(j + 1) * P]
                    for n in (KQ, VT, EA):
                        b = bank(n)
                        pe.matmul(b[:, :], maps[:, 2 * n:2 * n + 2, :].rearrange("d a e -> d (a e)"), xT[:, :],
                                  start=True, stop=True).then_inc(made, 1)
                    b = bank(GATE)
                    for j in range(CT):
                        last = pe.matmul(b[:, j * D:(j + 1) * D], tile(xT, j), maps[:, 6, :],
                                         start=True, stop=True)
                    last.then_inc(made, 1)
                    b = bank(LENGTH)
                    pe.wait_ge(squared, i + 1)
                    pe.matmul(b[:, :], pair_ones[:, :], square[:, :], start=True, stop=True).then_inc(made, 1)
                    pe.wait_ge(scaled, i + 2)
                    for k in range(BLK):
                        b = bank(HKT + k)
                        pe.matmul(b[:, :], w1[lower, k * P:(k + 1) * P], conv[lower, 0, :], start=True, stop=True)\
                            .then_inc(made, 1)
                    for k in range(CT // 2):
                        b = bank(HK + k)
                        for j in range(2):
                            last = pe.matmul(b[:, j * MEM_DH:(j + 1) * MEM_DH], tile(conv[lower, 0, :], 2 * k + j),
                                             w1[lower, :], start=True, stop=True)
                        last.then_inc(made, 1)
                    pe.wait_ge(v_ready, i + 1)
                    for k in range(BLK):
                        b = bank(HQT + k, ahead=k)
                        pe.matmul(b[:, :], w1[upper, k * P:(k + 1) * P], conv[upper, 0, :], start=True, stop=True)\
                            .then_inc(made, 1)
                    b = banks[VALUES % 4]
                    for j in range(CT):
                        last = pe.transpose(b[:, j * D:(j + 1) * D], tile(conv[lower, 1, :], j), ident[lower, lower])
                    last.then_inc(made, 1)
                    b = bank(MEANS)
                    for j in range(CT):
                        pe.matmul(b[:, 2 * CT + j:2 * CT + j + 1], tile(sig[upper, 0, :], j), ones[upper, 0:1],
                                  start=True, stop=True)
                        last = pe.matmul(b[:, 2 * j:2 * j + 2], tile(sig[:, 1, :], j), pair_ones[:, 0:P:D],
                                         start=True, stop=True)
                    last.then_inc(made, 1)

            @block.scalar
            def _(a):
                a.sem_inc(taken, 1)
                a.wait_ge(loaded, 16 * LOADS)
                with a.Fori(0, B) as i:
                    tiles = bass.ds(i * CT, CT)
                    tokens = bass.ds(i * T, T)
                    a.wait_ge(chunk_turned, i + 2)
                    take_pairs(lambda o, i_: a.activation(o, i_, ACT.Copy), xT[:, :], turn_ps, CT)\
                        .then_inc(xT_ready, 1)

                    def made_by(n):
                        a.wait_ge(made, i * JOBS + (n + 1))
                        return banks[n % 4]

                    a.wait_ge(scaled, i + 1)
                    a.activation(raw[:, 0, 1:T + 1], made_by(KQ)[:, :], ACT.Copy).then_inc(taken, 1)
                    b = made_by(VT)
                    a.activation(raw[lower, 1, 1:T + 1], b[lower, :], ACT.Copy)
                    a.activation(sig[upper, 0, :], b[upper, :], ACT.Sigmoid, bias=shift[upper, 0:1]).then_inc(taken, 1)
                    a.activation(sig[:, 1, :], made_by(EA)[:, :], ACT.Sigmoid, bias=shift[:, 1:2]).then_inc(taken, 1)
                    a.activation(kept["gate"][:, tiles, :],
                                 made_by(GATE)[:, 0:CT * D].rearrange("p (j d) -> p j d", d=D), ACT.Sigmoid)\
                        .then_inc(taken, 1)
                    a.activation(length[:, :], made_by(LENGTH)[:, :], ACT.Sqrt).then_inc(taken, 1)
                    for k in range(BLK):
                        a.activation(kept["hkT"][:, k, tokens], made_by(HKT + k)[:, :], ACT.Silu).then_inc(taken, 1)
                    for k in range(CT // 2):
                        a.activation(kept["hk"][:, bass.ds(i * CT + 2 * k, 2), :],
                                     made_by(HK + k)[:, :].rearrange("p (j f) -> p j f", f=MEM_DH), ACT.Silu)\
                            .then_inc(taken, 1)
                    for k in range(BLK):
                        a.activation(kept["hqT"][:, k, tokens], made_by(HQT + k)[:, :], ACT.Silu).then_inc(taken, 1)
                    a.activation(kept["v"][:, tiles, :],
                                 made_by(VALUES)[:, 0:CT * D].rearrange("p (j d) -> p j d", d=D), ACT.Copy)\
                        .then_inc(taken, 1)
                    b = made_by(MEANS)
                    a.activation(kept["rates"][:, 0, tiles], b[:, 2 * CT:3 * CT], ACT.Copy, scale=1.0 / D)
                    a.activation(kept["rates"][:, 1:3, tiles], b[:, 0:2 * CT].rearrange("p (j k) -> p k j", k=2),
                                 ACT.Copy, scale=1.0 / D).then_inc(taken, 1)

            @block.vector
            def _(dve):
                link = Chain(dve, chained)
                norm.vector(dve, link, h[:, :, :], x[:, :, :])
                dve.sem_inc(x_ready, 1)
                dve.wait_ge(loaded, 16 * LOADS)
                link(dve.memset(raw[:, :, :], 0.0))
                dve.sem_inc(scaled, 1)
                with dve.Fori(0, B) as i:
                    link.restart()

                    def convolve(n, rows):
                        y = conv[rows, n, :]
                        link(dve.tensor_scalar(y, raw[rows, n, 0:T], taps[rows, n, 0:1], None, ALU.mult))
                        for k in (1, 2):
                            link(dve.scalar_tensor_tensor(out=y, in0=raw[rows, n, k:T + k],
                                                          scalar=taps[rows, n, k:k + 1], in1=y,
                                                          op0=ALU.mult, op1=ALU.add))

                    dve.wait_ge(taken, i * JOBS + (VT + 2))
                    convolve(0, slice(0, P))
                    dve.tensor_tensor(square[:, :], conv[:, 0, :], conv[:, 0, :], ALU.mult).then_inc(squared, 1)
                    convolve(1, lower)
                    dve.sem_inc(v_ready, 1)
                    dve.wait_ge(taken, i * JOBS + (LENGTH + 2))
                    link(dve.tensor_scalar(length[:, :], length[:, :], NORM_MIN, None, ALU.max))
                    link(dve.reciprocal(length[:, :], length[:, :]))
                    dve.tensor_tensor(conv[:, 0, :], conv[:, 0, :], length[:, :], ALU.mult).then_inc(scaled, 1)
        s.clear()


def recur(nc, g, w, kept):
    ident, ones = g["ident"], g["ones"]
    PAIRS = CT
    TH, ET, AL = 0, 1, 2
    TOT = 3
    with ExitStack() as ctx:
        s = Stage(nc, ctx, "memr")
        flip = s.sb("flip", [P, P])
        first = s.sb("first", [P, BLK, D])
        row = s.sb("row", [TILES, 3, P])
        shifted = s.sb("shifted", [TILES, 2, 2, CHUNK])
        zeros = s.sb("zeros", [TILES, CHUNK])
        prods = s.sb("prods", [TILES, 3, 2, CHUNK])
        total = s.sb("total", [TILES, 2, TOT])
        spread_total = s.sb("spread_total", [TILES, 2 * TOT, TILES])
        coef_row = s.sb("coef_row", [TILES, 2, P])
        coef_rev = s.sb("coef_rev", [P, 2 * TILES])
        coef = s.sb("coef", [P, 2, TILES])
        tot = s.sb("tot", [P, 2, TOT, TILES])
        hkT_s = [s.sb(f"hkT_s{n}", [P, BLK, B, P]) for n in range(2)]
        hqT_s = [s.sb(f"hqT_s{n}", [P, BLK, B, P]) for n in range(2)]
        hk_s = [s.sb(f"hk_s{n}", [P, B, MEM_DH]) for n in range(2)]
        memory = s.sb("memory", [P, BLK, B, D])
        momentum = s.sb("momentum", [P, BLK, B, D])
        old = s.sb("old", [P, BLK, B, D])
        push = s.sb("push", [P, BLK, B, D])
        error = s.sb("error", [P, B, D])
        wide = s.sb("wide", [P, B, 2, D])
        row_ps = s.ps("row_ps", [P, T])
        pred_ps, ret_ps = s.ps("pred_ps", [P, T]), s.ps("ret_ps", [P, T])
        up_ps = s.ps("up_ps", [P, 4 * T])
        names = ["loaded", "chained", "flipped", "rows_ready", "rows_taken", "rev_ready", "rev_taken",
                 "coef_ready", "start", "staged0", "staged1", "predicted", "wide_ready", "updated",
                 "memory_ready", "momentum_ready", "returned", "kept_ret", "pushed"]
        (loaded, chained, flipped, rows_ready, rows_taken, rev_ready, rev_taken, coef_ready, start,
         staged0, staged1, predicted, wide_ready, updated, memory_ready, momentum_ready, returned,
         kept_ret, pushed) = [s.sem(n) for n in names]
        staged = (staged0, staged1)
        HALVES = 2 * PAIRS // 2
        ROUNDS = PAIRS // 2

        with nc.Block() as block:
            @block.sync
            def _(sp):
                sp.dma_start(first[:, :, :], w["W2"]).then_inc(loaded, 16)
                with sp.Fori(0, ROUNDS) as i:
                    for p in range(2):
                        sp.wait_ge(returned, i * HALVES + (2 * p + 2))
                        at = (i * 2 + p)
                        for k in range(BLK):
                            for to, of in ((hkT_s, kept["hkT"]), (hqT_s, kept["hqT"])):
                                sp.dma_start(to[p][:, k, :, :],
                                             of[:, k, :].rearrange("p (b c q) -> p b c q", b=B, q=P)
                                             [:, :, bass.ds(at, 1), :].rearrange("p b c q -> p (b c) q"))\
                                    .then_inc(staged[p], 16)
                        sp.dma_start(hk_s[p][:, :, :], kept["hk"][:, bass.ds(at, B, step=PAIRS), :])\
                            .then_inc(staged[p], 16)

            @block.gpsimd
            def _(pool):
                pool.memset(flip[:, :], 0.0).then_inc(flipped, 1)
                pool.wait_ge(flipped, 1)
                pool.affine_select(out=flip[:, :].rearrange("p (a c) -> p a c", c=CHUNK),
                                   in_=flip[:, :].rearrange("p (a c) -> p a c", c=CHUNK),
                                   compare_op=ALU.not_equal, fill=1.0, base=-(CHUNK - 1),
                                   pattern=[[-CHUNK, 2], [1, CHUNK]], channel_multiplier=1).then_inc(flipped, 1)

            @block.tensor
            def _(pe):
                pe.wait_ge(flipped, 2)
                for k in range(3):
                    last = pe.matmul(row_ps[0:TILES, k * P:(k + 1) * P], kept["rates"][:, k, :], flip[:, :],
                                     start=True, stop=True)
                last.then_inc(rows_ready, 1)
                pe.wait_ge(rows_taken, 1)
                for k in range(2):
                    last = pe.matmul(ret_ps[:, k * TILES:(k + 1) * TILES], coef_row[:, k, :],
                                     ident[0:TILES, 0:TILES], start=True, stop=True)
                last = pe.matmul(ret_ps[:, 4 * TILES:4 * TILES + 2 * TOT * TILES], ones[0:TILES, :],
                                 spread_total[:, :, :], start=True, stop=True)
                last.then_inc(rev_ready, 1)
                pe.wait_ge(rev_taken, 1)
                pe.matmul(ret_ps[:, 2 * TILES:4 * TILES], flip[:, :], coef_rev[:, :], start=True, stop=True)\
                    .then_inc(coef_ready, 1)
                pe.wait_ge(start, 1)
                pe.sem_inc(returned, 4)
                with pe.Fori(0, ROUNDS) as i:

                    def predict(n):
                        p, half = n // 2, n % 2 * CHUNK
                        if n % 2 == 0:
                            pe.wait_ge(staged[p], i * 80 + 80)
                        pe.wait_ge(memory_ready, i * HALVES + (n + 1))
                        pe.wait_ge(loaded, 16)
                        for b in range(B):
                            for k in range(BLK):
                                last = pe.matmul(pred_ps[half:half + CHUNK, b * D:(b + 1) * D],
                                                 hkT_s[p][:, k, b, half:half + CHUNK], memory[:, k, b, :],
                                                 start=(k == 0), stop=(k == BLK - 1))
                        last.then_inc(predicted, 1)

                    def update(n):
                        p, half = n // 2, n % 2 * CHUNK
                        pe.wait_ge(momentum_ready, i * HALVES + (n + 1))
                        pe.wait_ge(wide_ready, i * HALVES + (n + 1))
                        for k in range(BLK):
                            for b in range(B):
                                at = (k * B + b) * 2 * D
                                last = pe.matmul(up_ps[:, at:at + 2 * D],
                                                 hk_s[p][half:half + CHUNK, b, k * P:(k + 1) * P],
                                                 wide[half:half + CHUNK, b, :, :].rearrange("p a d -> p (a d)"),
                                                 start=True, stop=True)
                        last.then_inc(updated, 1)

                    def give(n):
                        p, half = n // 2, n % 2 * CHUNK
                        pe.wait_ge(kept_ret, i * HALVES + (n + 1))
                        pe.wait_ge(memory_ready, i * HALVES + (n + 2))
                        pe.wait_ge(loaded, 16)
                        for b in range(B):
                            for k in range(BLK):
                                last = pe.matmul(ret_ps[half:half + CHUNK, b * D:(b + 1) * D],
                                                 hqT_s[p][:, k, b, half:half + CHUNK], memory[:, k, b, :],
                                                 start=(k == 0), stop=(k == BLK - 1))
                        last.then_inc(returned, 1)

                    for n in range(HALVES):
                        predict(n)
                        if n:
                            give(n - 1)
                        update(n)
                    give(HALVES - 1)

            @block.scalar
            def _(a):
                a.sem_inc(kept_ret, 1)
                a.activation(zeros[0:1, 0:1], ones[0:1, 0:1], ACT.Copy).then_inc(pushed, 1)
                with a.Fori(0, ROUNDS) as i:
                    for n in range(HALVES):
                        half = n % 2 * CHUNK
                        a.wait_ge(returned, i * HALVES + (n + 5))
                        a.activation(kept["retrieved"][half:half + CHUNK, bass.ds(i * 2 + n // 2, B, step=PAIRS), :],
                                     ret_ps[half:half + CHUNK, :].rearrange("p (b d) -> p b d", d=D), ACT.Copy)\
                            .then_inc(kept_ret, 1)

            @block.vector
            def _(dve):
                link = Chain(dve, chained)
                dve.wait_ge(rows_ready, 1)
                link(dve.tensor_copy(row[:, :, :], row_ps[0:TILES, 0:3 * P].rearrange("p (k c) -> p k c", c=P)))
                link(dve.tensor_scalar(row[:, AL, :], row[:, AL, :], -1.0, 1.0, ALU.mult, ALU.add))
                dve.wait_ge(pushed, 1)
                link(dve.memset(zeros[:, :], 0.0))
                link(dve.memset(shifted[:, :, :, :], 1.0))
                halves = lambda k: row[:, k, :].rearrange("p (a c) -> p a c", c=CHUNK)
                for k, of in enumerate((ET, AL)):
                    link(dve.tensor_copy(shifted[:, k, :, 1:CHUNK], halves(of)[:, :, 0:CHUNK - 1]))
                PB, WT, PE_ = 0, 1, 2
                for a in range(2):
                    link(dve.tensor_tensor_scan(prods[:, PB, a, :], shifted[:, 1, a, :], zeros[:, :], 1.0,
                                                ALU.mult, ALU.add))
                    link(dve.tensor_tensor_scan(prods[:, PE_, a, :], shifted[:, 0, a, :], zeros[:, :], 1.0,
                                                ALU.mult, ALU.add))
                    link(dve.tensor_tensor_scan(prods[:, WT, a, :], shifted[:, 0, a, :], prods[:, PB, a, :], 0.0,
                                                ALU.mult, ALU.add))
                end = slice(CHUNK - 1, CHUNK)
                for k, (of, by) in enumerate(((PB, AL), (WT, ET), (PE_, ET))):
                    link(dve.tensor_tensor(total[:, :, k:k + 1], prods[:, of, :, end], halves(by)[:, :, end], ALU.mult))
                flat = lambda v: v.rearrange("p a c -> p (a c)")
                for k, of in enumerate((WT, PE_)):
                    link(dve.scalar_tensor_tensor(out=coef_row[:, k, :], in0=flat(prods[:, of, :, :]), scalar=-1.0,
                                                  in1=row[:, TH, :], op0=ALU.mult, op1=ALU.mult))
                link(dve.tensor_tensor(spread_total[:, :, :], spread(flat(total[:, :, :]), TILES),
                                       ident[0:TILES, 0:TILES].unsqueeze(1).to_broadcast([TILES, 2 * TOT, TILES]),
                                       ALU.mult))
                dve.sem_inc(rows_taken, 1)
                dve.wait_ge(rev_ready, 1)
                link(dve.tensor_copy(coef_rev[:, :], ret_ps[:, 0:2 * TILES]))
                link(dve.tensor_copy(tot[:, :, :, :],
                                     ret_ps[:, 4 * TILES:4 * TILES + 2 * TOT * TILES]
                                     .rearrange("p (a k j) -> p a k j", a=2, k=TOT)))
                dve.sem_inc(rev_taken, 1)
                dve.wait_ge(coef_ready, 1)
                link(dve.tensor_copy(coef[:, :, :], ret_ps[:, 2 * TILES:4 * TILES].rearrange("p (k j) -> p k j", k=2)))
                dve.wait_ge(loaded, 16)
                link(dve.tensor_copy(memory[:, :, :, :], first[:, :, :].unsqueeze(2).to_broadcast([P, BLK, B, D])))
                link(dve.memset(momentum[:, :, :, :], 0.0))
                dve.sem_inc(start, 1)
                dve.sem_inc(memory_ready, 1)
                dve.sem_inc(momentum_ready, 1)
                up = up_ps[:, :].rearrange("p (n a d) -> p n a d", a=2, d=D)
                merged = lambda v: v[:, :, :, :].rearrange("p k b d -> p (k b) d")
                with dve.Fori(0, ROUNDS) as i:
                    link.restart()
                    for n in range(HALVES):
                        lo = n % 2 * CHUNK
                        tiles = bass.ds(i * 2 + n // 2, B, step=PAIRS)

                        def by(k):
                            return spread(tot[:, n % 2, k, tiles], D).unsqueeze(1).to_broadcast([P, BLK, B, D])

                        link(dve.tensor_tensor(old[:, :, :, :], memory[:, :, :, :], by(0), ALU.mult))
                        link(dve.tensor_tensor(push[:, :, :, :], momentum[:, :, :, :], by(1), ALU.mult))
                        link(dve.tensor_tensor(old[:, :, :, :], old[:, :, :, :], push[:, :, :, :], ALU.add))
                        link(dve.tensor_tensor(momentum[:, :, :, :], momentum[:, :, :, :], by(2), ALU.mult))
                        part = slice(lo, lo + CHUNK)
                        dve.wait_ge(predicted, i * HALVES + (n + 1))
                        link(dve.tensor_tensor(error[part, :, :], pred_ps[part, :].rearrange("p (b d) -> p b d", d=D),
                                               kept["v"][part, tiles, :], ALU.subtract))
                        for k in range(2):
                            link(dve.tensor_tensor(wide[part, :, k, :], error[part, :, :],
                                                   spread(coef[part, k, tiles], D), ALU.mult))
                        dve.sem_inc(wide_ready, 1)
                        dve.wait_ge(updated, i * HALVES + (n + 1))
                        link(dve.tensor_tensor(merged(memory), merged(old), up[:, :, 0, :], ALU.add))
                        dve.sem_inc(memory_ready, 1)
                        link(dve.tensor_tensor(merged(momentum), merged(momentum), up[:, :, 1, :], ALU.add))
                        dve.sem_inc(momentum_ready, 1)
        s.clear()


def give_back(nc, g, w, kept):
    h, ident, got = g["h"], g["ident"], kept["retrieved"]
    with ExitStack() as ctx:
        s = Stage(nc, ctx, "memo")
        proj = s.sb("proj", [D, D])
        gb = s.sb("gb", [P, 2, D])
        o_chunk = s.sb("o_chunk", [P, CT, D])
        oT = s.sb("oT", [D, T])
        turn_ps, out_ps = s.ps("turn_ps", [P, T]), s.ps("out_ps", [P, T])
        norm = Norm(s, g)
        names = ["loaded", "chained", "o_ready", "chunk_ready", "chunk_turned", "oT_ready", "projected", "out_taken"]
        loaded, chained, o_ready, chunk_ready, chunk_turned, oT_ready, projected, out_taken = \
            [s.sem(n) for n in names]
        with nc.Block() as block:
            @block.sync
            def _(sp):
                sp.dma_start(proj[:, :], w["W_proj"]).then_inc(loaded, 16)
                sp.dma_start(gb[:, 0, :], row_bc(w["ln_g"], P)).then_inc(loaded, 16)
                sp.dma_start(gb[:, 1, :], row_bc(w["ln_b"], P)).then_inc(loaded, 16)

            @block.gpsimd
            def _(pool):
                norm.gpsimd(pool)
                pool.wait_ge(o_ready, 1)
                with pool.Fori(0, B) as i:
                    pool.wait_ge(chunk_turned, i + 1)
                    pool.tensor_copy(o_chunk[:, :, :], got[:, bass.ds(i * CT, CT), :]).then_inc(chunk_ready, 1)

            @block.tensor
            def _(pe):
                pe.wait_ge(loaded, 48)
                pe.sem_inc(chunk_turned, 1)
                with pe.Fori(0, B) as i:
                    pe.wait_ge(chunk_ready, i + 1)
                    turn_pairs(pe, turn_ps, o_chunk, ident, CT).then_inc(chunk_turned, 1)
                    pe.wait_ge(out_taken, i + 1)
                    pe.wait_ge(oT_ready, i + 1)
                    for j in range(CT):
                        last = pe.matmul(out_ps[:, j * D:(j + 1) * D], oT[:, j * P:(j + 1) * P], proj[:, :],
                                         start=True, stop=True)
                    last.then_inc(projected, 1)

            @block.scalar
            def _(a):
                with a.Fori(0, B) as i:
                    a.wait_ge(chunk_turned, i + 2)
                    take_pairs(lambda o, i_: a.activation(o, i_, ACT.Copy), oT[:, :], turn_ps, CT)\
                        .then_inc(oT_ready, 1)

            @block.vector
            def _(dve):
                link = Chain(dve, chained)
                dve.wait_ge(loaded, 48)
                norm.vector(dve, link, got[:, :, :], got[:, :, :], gb[:, 0, :], gb[:, 1, :])
                link(dve.tensor_tensor(got[:, :, :], got[:, :, :], kept["gate"][:, :, :], ALU.mult))
                dve.sem_inc(o_ready, 1)
                dve.sem_inc(out_taken, 1)
                with dve.Fori(0, B) as i:
                    dve.wait_ge(projected, i + 1)
                    h_chunk = h[:, bass.ds(i * CT, CT), :]
                    dve.tensor_tensor(h_chunk, h_chunk, out_ps[:, 0:CT * D].rearrange("p (j d) -> p j d", d=D),
                                      ALU.add).then_inc(out_taken, 1)
        s.clear()


SQ_HEADS, SQ_DH = 8, 8


def square_stage(nc, g, w):
    h, ident = g["h"], g["ident"]
    PAIRS = SQ_HEADS // 2
    WV = SQ_HEADS + D
    WK = D + WV
    with ExitStack() as ctx:
        s = Stage(nc, ctx, "sq")
        q_i, q_j = s.sb("q_i", [D, PAIRS, P]), s.sb("q_j", [D, PAIRS, P])
        qb_i, qb_j = s.sb("qb_i", [P, PAIRS]), s.sb("qb_j", [P, PAIRS])
        qb = s.sb("qb", [D, 1])
        wt = s.sb("wt", [D, 3 * D])
        kvb = s.sb("kvb", [P, 2 * D])
        proj_w, proj_b = s.sb("proj_w", [D, D]), s.sb("proj_b", [P, D])
        blocks = s.sb("blocks", [P, PAIRS + 1, WV])
        x = s.sb("x", [P, TILES, D])
        x_chunk = s.sb("x_chunk", [P, CT, D])
        xT = s.sb("xT", [D, T])
        kv = s.sb("kv", [P, CT, WK])
        kk = s.sb("kk", [P, CT, SQ_HEADS, SQ_DH * SQ_DH])
        sums = s.sb("sums", [P, PAIRS + 1, WV])
        left = s.sb("left", [P, 2, T])
        qq = s.sb("qq", [P, PAIRS, T])
        q1 = s.sb("q1", [D + 1, T])
        recip = s.sb("recip", [P, CT, SQ_HEADS])
        mix = s.sb("mix", [P, CT, D])
        mixT = s.sb("mixT", [D, T])
        part = s.sb("part", [P, CT, D])
        turn_ps, kv_ps, q1_ps, sum_ps = [s.ps(n, [P, T]) for n in ("turn_ps", "kv_ps", "q1_ps", "sum_ps")]
        left_ps, right_ps, mix_ps, proj_ps = [s.ps(n, [P, T]) for n in ("left_ps", "right_ps", "mix_ps", "proj_ps")]
        norm = Norm(s, g)
        names = ["loaded", "chained", "x_ready", "chunk_ready", "chunk_turned", "xT_ready", "kv_projected",
                 "kk_ready", "summed", "sums_ready", "q1_projected", "q1_ready", "paired", "left_ready",
                 "qq_ready", "mixed", "mix_ready", "mix_turned", "mixT_ready", "projected", "out_taken"]
        (loaded, chained, x_ready, chunk_ready, chunk_turned, xT_ready, kv_projected, kk_ready, summed,
         sums_ready, q1_projected, q1_ready, paired, left_ready, qq_ready, mixed, mix_ready, mix_turned,
         mixT_ready, projected, out_taken) = [s.sem(n) for n in names]
        LOADS = 10

        with nc.Block() as block:
            @block.sync
            def _(sp):
                for to, of in ((q_i, w["q_i"].rearrange("d (a p) -> d a p", p=P)),
                               (q_j, w["q_j"].rearrange("d (a p) -> d a p", p=P)),
                               (blocks, w["blocks"])):
                    sp.dma_start(to[:, :, :], of).then_inc(loaded, 16)
                for to, of in ((qb_i, w["qb_i"]), (qb_j, w["qb_j"]), (qb, w["qb"]), (wt, w["w"]),
                               (proj_w, w["proj_w"]), (proj_b, row_bc(w["proj_b"], P)),
                               (kvb, row_bc(w["b"][D:3 * D], P))):
                    sp.dma_start(to[:, :], of).then_inc(loaded, 16)

            @block.gpsimd
            def _(pool):
                norm.gpsimd(pool)
                pool.wait_ge(x_ready, 1)
                with pool.Fori(0, B) as i:
                    pool.wait_ge(chunk_turned, i + 1)
                    pool.tensor_copy(x_chunk[:, :, :], x[:, bass.ds(i * CT, CT), :])\
                        .then_inc(chunk_ready, 1)

            @block.tensor
            def _(pe):
                pe.wait_ge(loaded, 16 * LOADS)
                pe.sem_inc(chunk_turned, 1)
                with pe.Fori(0, B) as i:
                    pe.wait_ge(chunk_ready, i + 1)
                    turn_pairs(pe, turn_ps, x_chunk, ident, CT).then_inc(chunk_turned, 1)
                    pe.wait_ge(xT_ready, i + 1)
                    for j in range(CT):
                        last = pe.matmul(kv_ps[:, j * 2 * D:(j + 1) * 2 * D], xT[:, j * P:(j + 1) * P],
                                         wt[:, D:3 * D], start=True, stop=True)
                    last.then_inc(kv_projected, 1)
                    pe.matmul(q1_ps[0:D, :], wt[:, 0:D], xT[:, :], start=True, stop=True)\
                        .then_inc(q1_projected, 1)
                    for a in range(PAIRS):
                        pe.wait_ge(qq_ready, i * PAIRS + (a + 1))
                        pe.matmul(left_ps[:, :], q_i[:, a, :], xT[:, :], start=True, stop=True)
                        pe.matmul(right_ps[:, :], q_j[:, a, :], xT[:, :], start=True, stop=True)\
                            .then_inc(paired, 1)
                    pe.wait_ge(kk_ready, i + 1)
                    for a in range(PAIRS):
                        for j in range(CT):
                            pe.matmul(sum_ps[:, a * WV:(a + 1) * WV],
                                      kk[:, j, 2 * a:2 * a + 2, :].rearrange("p a f -> p (a f)"),
                                      kv[:, j, D:WK], start=(j == 0), stop=(j == CT - 1))
                    for j in range(CT):
                        last = pe.matmul(sum_ps[0:D + 1, PAIRS * WV:(PAIRS + 1) * WV], kv[:, j, 0:D + 1],
                                         kv[:, j, D:WK], start=(j == 0), stop=(j == CT - 1))
                    last.then_inc(summed, 1)
                    pe.wait_ge(sums_ready, i + 1)
                    pe.wait_ge(qq_ready, i * PAIRS + (PAIRS + 1))
                    pe.wait_ge(q1_ready, i + 1)
                    for j in range(CT):
                        out = mix_ps[:, j * WV:(j + 1) * WV]
                        for a in range(PAIRS):
                            pe.matmul(out, qq[:, a, j * P:(j + 1) * P], sums[:, a, :], start=(a == 0), stop=False)
                        last = pe.matmul(out, q1[:, j * P:(j + 1) * P], sums[0:D + 1, PAIRS, :],
                                         start=False, stop=True)
                    last.then_inc(mixed, 1)
                    pe.wait_ge(mix_ready, i + 1)
                    turn_pairs(pe, turn_ps, mix, ident, CT).then_inc(mix_turned, 1)
                    pe.wait_ge(mixT_ready, i + 1)
                    for j in range(CT):
                        last = pe.matmul(proj_ps[:, j * D:(j + 1) * D], mixT[:, j * P:(j + 1) * P],
                                         proj_w[:, :], start=True, stop=True)
                    last.then_inc(projected, 1)
                    pe.wait_ge(out_taken, i + 1)

            @block.scalar
            def _(a_):
                a = a_
                copy = lambda o, i_: a.activation(o, i_, ACT.Copy)
                a.wait_ge(loaded, 16 * LOADS)
                a.activation(left[0:1, 0, 0:1], g["ones"][0:1, 0:1], ACT.Copy)
                with a.Fori(0, B) as i:
                    a.wait_ge(chunk_turned, i + 2)
                    take_pairs(copy, xT[:, :], turn_ps, CT).then_inc(xT_ready, 1)
                    a.wait_ge(q1_projected, i + 1)
                    a.activation(q1[0:D, :], q1_ps[0:D, :], ACT.Identity, bias=qb[:, 0:1]).then_inc(q1_ready, 1)
                    for n in range(PAIRS):
                        a.wait_ge(paired, i * PAIRS + (n + 1))
                        a.activation(left[:, n % 2, :], left_ps[:, :], ACT.Identity, bias=qb_i[:, n:n + 1])\
                            .then_inc(left_ready, 1)
                    a.wait_ge(mix_turned, i + 1)
                    take_pairs(copy, mixT[:, :], turn_ps, CT).then_inc(mixT_ready, 1)

            @block.vector
            def _(dve):
                link = Chain(dve, chained)
                norm.vector(dve, link, h[:, :, :], x[:, :, :])
                dve.sem_inc(x_ready, 1)
                dve.sem_inc(qq_ready, 1)
                dve.wait_ge(loaded, 16 * LOADS)
                link(dve.memset(kv[:, :, D:D + SQ_HEADS], 1.0))
                link(dve.memset(q1[D:D + 1, :], 1.0))
                with dve.Fori(0, B) as i:
                    link.restart()
                    dve.wait_ge(kv_projected, i + 1)
                    raw = kv_ps[:, :].rearrange("p (j c) -> p j c", j=CT)
                    bias = lambda a: kvb[:, a * D:(a + 1) * D].unsqueeze(1).to_broadcast([P, CT, D])
                    link(dve.tensor_tensor(kv[:, :, 0:D], raw[:, :, 0:D], bias(0), ALU.add))
                    link(dve.tensor_tensor(kv[:, :, D + SQ_HEADS:WK], raw[:, :, D:2 * D], bias(1), ALU.add))
                    for j in range(CT):
                        k = kv[:, j, 0:D].rearrange("p (h i) -> p h i", i=SQ_DH)
                        last = dve.tensor_tensor(kk[:, j, :, :].rearrange("p h (i j) -> p h i j", j=SQ_DH),
                                                 spread(k, SQ_DH), k.unsqueeze(2).to_broadcast([P, SQ_HEADS, SQ_DH, SQ_DH]),
                                                 ALU.mult)
                    last.then_inc(kk_ready, 1)
                    for n in range(PAIRS):
                        dve.wait_ge(left_ready, i * PAIRS + (n + 1))
                        dve.scalar_tensor_tensor(out=qq[:, n, :], in0=right_ps[:, :], scalar=qb_j[:, n:n + 1],
                                                 in1=left[:, n % 2, :], op0=ALU.add, op1=ALU.mult)\
                            .then_inc(qq_ready, 1)
                    dve.wait_ge(summed, i + 1)
                    full = sum_ps[:, 0:(PAIRS + 1) * WV].rearrange("p (a c) -> p a c", c=WV)
                    link(dve.tensor_tensor(sums[:, 0:PAIRS, :], full[:, 0:PAIRS, :], blocks[:, 0:PAIRS, :], ALU.mult))
                    dve.tensor_tensor(sums[0:D + 1, PAIRS, :], full[0:D + 1, PAIRS, :], blocks[0:D + 1, PAIRS, :],
                                      ALU.mult).then_inc(sums_ready, 1)
                    dve.wait_ge(mixed, i + 1)
                    got = mix_ps[:, 0:CT * WV].rearrange("p (j c) -> p j c", c=WV)
                    link(dve.reciprocal(recip[:, :, :], got[:, :, 0:SQ_HEADS]))
                    dve.tensor_tensor(mix[:, :, :].rearrange("p j (h e) -> p j h e", e=SQ_DH),
                                      got[:, :, SQ_HEADS:WV].rearrange("p j (h e) -> p j h e", e=SQ_DH),
                                      spread(recip[:, :, :], SQ_DH), ALU.mult).then_inc(mix_ready, 1)
                    dve.wait_ge(projected, i + 1)
                    link(dve.tensor_tensor(part[:, :, :], proj_ps[:, 0:CT * D].rearrange("p (j d) -> p j d", d=D),
                                           proj_b[:, :].unsqueeze(1).to_broadcast([P, CT, D]), ALU.add))
                    dve.sem_inc(out_taken, 1)
                    h_chunk = h[:, bass.ds(i * CT, CT), :]
                    link(dve.tensor_tensor(h_chunk, h_chunk, part[:, :, :], ALU.add))
        s.clear()


def softmax_stage(nc, g, w):
    h, ident = g["h"], g["ident"]
    SCALE = float(D) ** -0.5
    with ExitStack() as ctx:
        s = Stage(nc, ctx, "soft")
        wt = s.sb("wt", [D, 2 * D])
        x = s.sb("x", [P, TILES, D])
        x_chunk = s.sb("x_chunk", [P, CT, D])
        xT = s.sb("xT", [D, T])
        yT = s.sb("yT", [D, T])
        top = s.sb("top", [P, CT])
        total = s.sb("total", [P, CT])
        prob = s.sb("prob", [P, 2, T])
        probT = s.sb("probT", [P, 2, CT, P])
        part = s.sb("part", [P, CT, D])
        xT_ps, y_ps, out_ps = s.ps("xT_ps", [P, T]), s.ps("y_ps", [P, T]), s.ps("out_ps", [P, T])
        score_ps = [s.ps(f"score_ps{n}", [P, T]) for n in range(2)]
        turn_ps = [s.ps(f"turn_ps{n}", [P, T]) for n in range(2)]
        norm = Norm(s, g)
        names = ["loaded", "chained", "x_ready", "chunk_ready", "chunk_turned", "xT_ready", "y_ready",
                 "yT_ready", "scored", "top_ready", "prob_ready", "prob_turned", "probT_ready",
                 "mixed", "out_taken"]
        (loaded, chained, x_ready, chunk_ready, chunk_turned, xT_ready, y_ready, yT_ready, scored,
         top_ready, prob_ready, prob_turned, probT_ready, mixed, out_taken) = [s.sem(n) for n in names]

        with nc.Block() as block:
            @block.sync
            def _(sp):
                sp.dma_start(wt[:, 0:D], w["W"]).then_inc(loaded, 16)
                sp.dma_start(wt[:, D:2 * D], w["W"]).then_inc(loaded, 16)

            @block.gpsimd
            def _(pool):
                norm.gpsimd(pool)
                pool.wait_ge(x_ready, 1)
                with pool.Fori(0, B) as i:
                    pool.wait_ge(mixed, i * CT + CT)
                    pool.tensor_copy(x_chunk[:, :, :], x[:, bass.ds(i * CT, CT), :])\
                        .then_inc(chunk_ready, 1)

            @block.tensor
            def _(pe):
                pe.wait_ge(loaded, 32)
                pe.sem_inc(mixed, CT)
                with pe.Fori(0, B) as i:
                    pe.wait_ge(chunk_ready, i + 1)
                    turn_pairs(pe, xT_ps, x_chunk, ident, CT).then_inc(chunk_turned, 1)
                    pe.wait_ge(xT_ready, i + 1)
                    pe.wait_ge(loaded, 32)
                    pe.matmul(y_ps[:, :], wt[:, :], xT[:, :], start=True, stop=True).then_inc(y_ready, 1)
                    pe.wait_ge(yT_ready, i + 1)

                    def score(j):
                        pe.wait_ge(prob_ready, i * CT + (j + 1))
                        pe.matmul(score_ps[j % 2][:, :], yT[:, j * P:(j + 1) * P], xT[:, :],
                                  start=True, stop=True).then_inc(scored, 1)

                    def turn(j):
                        pe.wait_ge(prob_ready, i * CT + (j + 3))
                        pe.wait_ge(probT_ready, i * CT + (j + 1))
                        for m in range(CT):
                            last = pe.transpose(turn_ps[j % 2][:, m * P:(m + 1) * P],
                                                prob[:, j % 2, m * P:(m + 1) * P], ident[:, :])
                        last.then_inc(prob_turned, 1)

                    def mix(j):
                        pe.wait_ge(probT_ready, i * CT + (j + 3))
                        if j == 0:
                            pe.wait_ge(out_taken, i + 1)
                        for m in range(CT):
                            last = pe.matmul(out_ps[:, j * D:(j + 1) * D], probT[:, j % 2, m, :],
                                             x_chunk[:, m, :], start=(m == 0), stop=(m == CT - 1))
                        last.then_inc(mixed, 1)

                    score(0)
                    for j in range(CT):
                        if j + 1 < CT:
                            score(j + 1)
                        turn(j)
                        if j:
                            mix(j - 1)
                    mix(CT - 1)

            @block.scalar
            def _(a):
                a.sem_inc(prob_ready, 2)
                a.activation(prob[0:1, 0, 0:1], g["ones"][0:1, 0:1], ACT.Exp)
                with a.Fori(0, B) as i:
                    a.wait_ge(chunk_turned, i + 1)
                    a.wait_ge(mixed, i * CT + CT)
                    take_pairs(lambda o, i_: a.activation(o, i_, ACT.Copy), xT[:, :], xT_ps, CT)\
                        .then_inc(xT_ready, 1)
                    a.wait_ge(y_ready, i + 1)
                    a.activation(yT[:, :], y_ps[0:D, :], ACT.Copy).then_inc(yT_ready, 1)
                    for j in range(CT):
                        a.wait_ge(top_ready, i * CT + (j + 1))
                        a.wait_ge(prob_turned, i * CT + (j + 1))
                        a.activation(prob[:, j % 2, :], score_ps[j % 2][:, :], ACT.Exp, bias=top[:, j:j + 1],
                                     scale=SCALE, accum_out=total[:, j:j + 1]).then_inc(prob_ready, 1)

            @block.vector
            def _(dve):
                link = Chain(dve, chained)
                norm.vector(dve, link, h[:, :, :], x[:, :, :])
                dve.sem_inc(x_ready, 1)
                dve.sem_inc(prob_turned, 2)
                dve.sem_inc(probT_ready, 2)
                dve.sem_inc(out_taken, 1)
                with dve.Fori(0, B) as i:
                    link.restart()

                    def maximum(j):
                        dve.wait_ge(scored, i * CT + (j + 1))
                        link(dve.tensor_reduce(top[:, j:j + 1], score_ps[j % 2][:, :], X, ALU.max))
                        dve.tensor_scalar(top[:, j:j + 1], top[:, j:j + 1], -SCALE, None, ALU.mult)\
                            .then_inc(top_ready, 1)

                    maximum(0)
                    for j in range(CT):
                        if j + 1 < CT:
                            maximum(j + 1)
                        dve.wait_ge(prob_turned, i * CT + (j + 3))
                        dve.wait_ge(mixed, i * CT + (j - 1 + CT))
                        dve.tensor_copy(probT[:, j % 2, :, :],
                                        turn_ps[j % 2][:, :].rearrange("p (m q) -> p m q", m=CT))\
                            .then_inc(probT_ready, 1)
                    dve.wait_ge(mixed, i * CT + 2 * CT)
                    link(dve.reciprocal(total[:, :], total[:, :]))
                    link(dve.tensor_tensor(part[:, :, :], out_ps[:, 0:CT * D].rearrange("p (j d) -> p j d", d=D),
                                           spread(total[:, :], D), ALU.mult))
                    dve.sem_inc(out_taken, 1)
                    h_chunk = h[:, bass.ds(i * CT, CT), :]
                    link(dve.tensor_tensor(h_chunk, h_chunk, part[:, :, :], ALU.add))
        s.clear()


def named(arrays, prefix):
    return {k[len(prefix) + 1:]: a for k, a in arrays.items() if k.startswith(prefix + "_")}


def tower(nc, arrays, out):
    capacity = -(-5 * N // (4 * E))
    with ExitStack() as ctx:
        h = ctx.enter_context(nc.sbuf_tensor("h", [P, TILES, D], F32))
        stored = ctx.enter_context(nc.semaphore("stored"))
        g = {"ctx": ctx, "h": h}
        constants(nc, g)
        token_stage(nc, g, arrays["ids"], [arrays[f"emb_{n}"] for n in GRAMS])
        recurrent_stage(nc, g, named(arrays, "L0_attn"))
        expert_stage(nc, g, "L0_ffn", named(arrays, "L0_ffn"), ACT.Relu, 2, "top", 1,
                     capacity=capacity, limit_infinite=True)
        memory_stage(nc, g, named(arrays, "L1_attn"))
        expert_stage(nc, g, "L1_ffn", named(arrays, "L1_ffn"), ACT.Gelu, 1, "mask", 2)
        square_stage(nc, g, named(arrays, "L2_attn"))
        w = named(arrays, "L2_ffn")
        expert_stage(nc, g, "L2_ffn", w, ACT.Gelu, 1, "softmax", 2, norms=2,
                     gamma_beta=(w["gamma"], w["beta"]))
        softmax_stage(nc, g, named(arrays, "L3_attn"))
        w = named(arrays, "L3_ffn")
        expert_stage(nc, g, "L3_ffn", w, ACT.Gelu, 2, "renormed", 2, norms=2,
                     expert_norm=(w["ln_g"], w["ln_b"]))
        with nc.Block() as block:
            @block.sync
            def _(sp):
                sp.dma_start(out.rearrange("b t d -> (b t) d").rearrange("(j p) d -> p j d", p=P), h[:, :, :])\
                    .then_inc(stored, 16)
                sp.wait_ge(stored, 16)


def square_blocks():
    column = np.concatenate([np.arange(8), np.repeat(np.arange(8), 8)])
    out = np.zeros((128, 5, 72), np.float32)
    row = np.arange(128)
    for pair in range(4):
        out[:, pair] = np.where((2 * pair + row // 64)[:, None] == column, 1 / 8, 0)
    out[0:64, 4] = np.where((row[0:64] // 8)[:, None] == column, 10 / np.sqrt(8), 0)
    out[64, 4] = 25
    return out


def lay_out(v):
    c = np.ascontiguousarray
    out = {"ids": c(v["x"])}
    for n in (2, 3, 4):
        out[f"emb_{n}"] = c(v[f"L0_tok_emb_{n}"])

    def experts(name, w1, b1, w2, b2, wg, bg):
        w1, b1, w2 = v[w1], v[b1], v[w2]
        blocks = b1.size // 128
        out[f"{name}_w1"] = c(w1.transpose(1, 0, 2).reshape(w1.shape[1], -1))
        out[f"{name}_b1"] = c(b1.reshape(blocks, 128).T)
        out[f"{name}_w2"] = c(w2.reshape(blocks, 128, -1).transpose(1, 0, 2))
        out[f"{name}_b2"] = c(v[b2].reshape(4, 128).T)
        out[f"{name}_wg"] = c(v[wg])
        out[f"{name}_bg"] = c(v[bg])

    experts("L0_ffn", "L0_ffn_w1", "L0_ffn_b1", "L0_ffn_w2", "L0_ffn_b2", "L0_ffn_gate_w", "L0_ffn_gate_b")
    experts("L1_ffn", "L1_ffn_W1", "L1_ffn_b1", "L1_ffn_W2", "L1_ffn_b2", "L1_ffn_Wg", "L1_ffn_bg")
    experts("L2_ffn", "L2_ffn_W1", "L2_ffn_b1", "L2_ffn_W2", "L2_ffn_b2", "L2_ffn_Wr", "L2_ffn_br")
    experts("L3_ffn", "L3_ffn_W1", "L3_ffn_b1", "L3_ffn_W2", "L3_ffn_b2", "L3_ffn_Wr", "L3_ffn_br")
    out["L2_ffn_gamma"], out["L2_ffn_beta"] = c(v["L2_ffn_gamma"]), c(v["L2_ffn_beta"])
    out["L3_ffn_ln_g"], out["L3_ffn_ln_b"] = c(v["L3_ffn_ln_g"].T), c(v["L3_ffn_ln_b"].T)

    w = v["L0_attn_slow_W"].reshape(8, 162, 64)
    kinds = [w[:, a:b].reshape(-1, 64) for a, b in zip((0, 32, 64, 96, 128, 160, 161), (32, 64, 96, 128, 160, 161, 162))]
    out["L0_attn_w_in"] = c(np.concatenate(kinds).T)
    out["L0_attn_w_out"] = c(v["L0_attn_out_W"].T.reshape(2, 128, 64).transpose(1, 0, 2))
    out["L0_attn_ln_g"], out["L0_attn_ln_b"] = c(v["L0_attn_ln_g"]), c(v["L0_attn_ln_b"])

    for n in ("W_K", "W_V", "W_Q", "W_th", "W_et", "W_al", "W_gate", "W_proj", "W1"):
        out[f"L1_attn_{n}"] = c(v[f"L1_attn_{n}"].T)
    out["L1_attn_W2"] = c(v["L1_attn_W2"].T.reshape(2, 128, 64).transpose(1, 0, 2))
    for n in ("conv_k", "conv_v", "conv_q"):
        out[f"L1_attn_{n}"] = c(v[f"L1_attn_{n}"].reshape(64, 3))
    for n in ("b_th", "b_et", "b_al"):
        out[f"L1_attn_{n}"] = c(v[f"L1_attn_{n}"].reshape(64, 1))
    out["L1_attn_ln_g"], out["L1_attn_ln_b"] = c(v["L1_attn_ln_g"]), c(v["L1_attn_ln_b"])

    w, b = v["L2_attn_qkv_w"], v["L2_attn_qkv_b"]
    q, qb = w[0:64].reshape(8, 8, 64), b[0:64].reshape(8, 8)
    out["L2_attn_q_i"] = c(np.repeat(q, 8, axis=1).reshape(512, 64).T)
    out["L2_attn_q_j"] = c(np.tile(q, (1, 8, 1)).reshape(512, 64).T)
    out["L2_attn_qb_i"] = c(np.repeat(qb, 8, axis=1).reshape(4, 128).T)
    out["L2_attn_qb_j"] = c(np.tile(qb, (1, 8)).reshape(4, 128).T)
    out["L2_attn_w"] = c(w.T)
    out["L2_attn_qb"] = c(b[0:64].reshape(64, 1))
    out["L2_attn_b"] = c(b)
    out["L2_attn_proj_w"] = c(v["L2_attn_proj_w"].T)
    out["L2_attn_proj_b"] = c(v["L2_attn_proj_b"])
    out["L3_attn_W"] = c(v["L3_attn_W"])
    out["L2_attn_blocks"] = square_blocks()
    return out


def kernel(**inputs):
    import concourse.bacc as bacc
    from concourse.bass_utils import run_bass_kernel_spmd

    nc = bacc.Bacc("TRN2", target_bir_lowering=False, num_devices=1)
    laid = lay_out({k: np.asarray(a) for k, a in inputs.items()})
    arrays = {k: nc.dram_tensor(f"in_{k}", a.shape, mybir.dt.from_np(a.dtype), kind="ExternalInput").ap()
              for k, a in laid.items()}
    out = nc.dram_tensor("out", (B, T, D), F32, kind="ExternalOutput").ap()
    tower(nc, arrays, out)
    r = run_bass_kernel_spmd(nc, [{f"in_{k}": a for k, a in laid.items()}], core_ids=[0])
    return r.results[0]["out"]
```

```python
from contextlib import ExitStack

import numpy as np

import concourse.bass as bass
from concourse import mybir

F32 = mybir.dt.float32
F32R = mybir.dt.float32r
I32 = mybir.dt.int32
U32 = mybir.dt.uint32
ALU = mybir.AluOpType
ACT = mybir.ActivationFunctionType
X = mybir.AxisListType.X

P = 128
B, T, D = 8, 512, 64
N = B * T
TILES = N // P
CT = T // P
E = 8
EPS = 1e-5


class Chain:

    def __init__(self, engine, done):
        self.engine, self.done, self.count = engine, done, 0

    def restart(self):
        self.engine.sem_clear(self.done)
        self.count = 0

    def __call__(self, instruction):
        self.count += 1
        instruction.then_inc(self.done, 1)
        self.engine.wait_ge(self.done, self.count)


class Stage:

    def __init__(self, nc, ctx, name):
        self.nc, self.ctx, self.name = nc, ctx, name
        self.sems = []

    def sb(self, name, shape, dt=F32):
        return self.ctx.enter_context(self.nc.sbuf_tensor(f"{self.name}_{name}", shape, dt))

    def ps(self, name, shape, dt=F32):
        return self.ctx.enter_context(self.nc.psum_tensor(f"{self.name}_{name}", shape, dt))

    def sem(self, name):
        self.sems.append(self.ctx.enter_context(self.nc.semaphore(f"{self.name}_{name}")))
        return self.sems[-1]

    def clear(self):
        numbers = sorted(sem.num for sem in self.sems)
        runs = []
        for n in numbers:
            if runs and n == runs[-1][1]:
                runs[-1][1] = n + 1
            else:
                runs.append([n, n + 1])
        with self.nc.Block() as block:
            @block.gpsimd
            def _(pool):
                for first, end in runs:
                    pool.sem_clear(range(first, end))


def spread(ap, n):
    return ap.unsqueeze(len(ap.shape)).to_broadcast([*ap.shape, n])


def pow_minus_half(pool, out, in_, minus_half):
    return pool.tensor_tensor(out, in_, minus_half, ALU.pow)


def constants(nc, g):
    s = Stage(nc, g["ctx"], "const")
    ident = s.sb("ident", [P, P])
    upto = s.sb("upto", [P, P])
    ones = s.sb("ones", [P, P])
    minus_half = s.sb("minus_half", [P, TILES])
    before = s.sb("before", [P, CT, E, E])
    filled, done = s.sem("filled"), s.sem("done")
    with nc.Block() as block:
        @block.gpsimd
        def _(pool):
            pool.memset(ident[:, :], 0.0).then_inc(filled, 1)
            pool.memset(upto[:, :], 1.0).then_inc(filled, 1)
            pool.memset(before[:, :, :, :], 1.0).then_inc(filled, 1)
            pool.memset(ones[:, :], 1.0).then_inc(done, 1)
            pool.memset(minus_half[:, :], -0.5).then_inc(done, 1)
            pool.wait_ge(filled, 3)
            pool.affine_select(out=ident[:, :], in_=ident[:, :], compare_op=ALU.not_equal, fill=1.0,
                               base=0, pattern=[[-1, P]], channel_multiplier=1).then_inc(done, 1)
            pool.affine_select(out=upto[:, :], in_=upto[:, :], compare_op=ALU.is_ge, fill=0.0,
                               base=0, pattern=[[1, P]], channel_multiplier=-1).then_inc(done, 1)
            pool.affine_select(out=before[:, :, :, :], in_=before[:, :, :, :], compare_op=ALU.is_ge,
                               fill=0.0, base=-1, pattern=[[0, CT], [1, E], [-1, E]],
                               channel_multiplier=0).then_inc(done, 1)
            pool.wait_ge(done, 5)
    s.clear()
    g.update(ident=ident, upto=upto, ones=ones, minus_half=minus_half, before=before)


class Norm:

    def __init__(self, s, g, count=1, square=None, halves=None, name="norm"):
        self.g = g
        self.stat = s.sb(f"{name}_stat", [P, TILES])
        self.square = s.sb("norm_square", [P, TILES, D])[:, :, :] if square is None else square
        self.centred, self.squared = s.sem(f"{name}_centred"), s.sem(f"{name}_squared")
        self.var_ready, self.rstd_ready = s.sem(f"{name}_var_ready"), s.sem(f"{name}_rstd_ready")
        self.count = count
        self.tiles = TILES // 4 if halves else TILES // 2
        self.done = self.squares = 0
        self.halves = halves or [slice(a * TILES // 2, (a + 1) * TILES // 2) for a in range(2)]

    def vector(self, dve, link, x, out, gamma=None, beta=None, meanwhile=None):
        stat, square = self.stat, self.square
        for half in self.halves:
            link(dve.tensor_reduce(stat[:, half], x[:, half, :], X, ALU.add))
            link(dve.scalar_tensor_tensor(out=out[:, half, :], in0=spread(stat[:, half], D), scalar=-1.0 / D,
                                          in1=x[:, half, :], op0=ALU.mult, op1=ALU.add))
            dve.sem_inc(self.centred, 1)
        for n, half in enumerate(self.halves):
            dve.wait_ge(self.squared, self.done + n + 1)
            link(dve.tensor_reduce(stat[:, half], square[:, half, :], X, ALU.add))
            dve.tensor_scalar(stat[:, half], stat[:, half], 1.0 / D, EPS, ALU.mult, ALU.add)\
                .then_inc(self.var_ready, 1)
        if meanwhile:
            meanwhile()
        for n, half in enumerate(self.halves):
            dve.wait_ge(self.rstd_ready, self.done + n + 1)
            link(dve.tensor_tensor(out[:, half, :], out[:, half, :], spread(stat[:, half], D), ALU.mult))
            if gamma is not None:
                rows = lambda v: v.unsqueeze(1).to_broadcast([P, self.tiles, D])
                link(dve.tensor_tensor(out[:, half, :], out[:, half, :], rows(gamma), ALU.mult))
                link(dve.tensor_tensor(out[:, half, :], out[:, half, :], rows(beta), ALU.add))
        self.done += 2

    def scalar(self, act, out):
        for half in self.halves:
            self.squares += 1
            act.wait_ge(self.centred, self.squares)
            act.activation(self.square[:, half, :], out[:, half, :], ACT.Square).then_inc(self.squared, 1)

    def gpsimd(self, pool, after_first=None):
        for n in range(2 * self.count):
            if n == 2 and after_first:
                after_first()
            half = self.halves[n % 2]
            pool.wait_ge(self.var_ready, n + 1)
            pool.tensor_tensor(self.stat[:, half], self.stat[:, half], self.g["minus_half"][:, 0:self.tiles], ALU.pow)\
                .then_inc(self.rstd_ready, 1)


def row_bc(ap, n):
    flat = ap if len(ap.shape) == 1 else ap.rearrange("a b -> (a b)")
    return flat.unsqueeze(0).to_broadcast([n, flat.shape[0]])


def turn_pairs(pe, out, rows, ident, count):
    for k in range(count // 2):
        last = pe.transpose(out[:, k * P:(k + 1) * P],
                            rows[:, 2 * k:2 * k + 2, :].rearrange("p a d -> p (a d)"), ident[:, :])
    return last


def take_pairs(copy, xT, turned, count):
    pairs = xT.rearrange("d (k a q) -> d k a q", a=2, q=P)
    for a in range(2):
        last = copy(pairs[:, :, a, :], turned[a * D:(a + 1) * D, 0:count // 2 * P]
                    .rearrange("d (k q) -> d k q", q=P))
    return last


PRIME, VOCAB = 31, 125000
GRAMS = (2, 3, 4)
BACK = GRAMS[-1] - 1


def token_stage(nc, g, ids, tables):
    h = g["h"]
    W = P + BACK
    with ExitStack() as ctx:
        s = Stage(nc, ctx, "tok")
        ids_row = s.sb("ids_row", [TILES, W], I32)
        ids_f = s.sb("ids_f", [TILES, W])
        hashes = s.sb("hashes", [TILES, len(GRAMS), W])
        quot_i = s.sb("quot_i", [TILES, W], I32)
        quot = s.sb("quot", [TILES, W])
        index = s.sb("index", [P, len(GRAMS), TILES], U32)
        rows = [s.sb(f"rows{n}", [P, TILES, D]) for n in GRAMS]
        index_ps = s.ps("index_ps", [P, len(GRAMS), TILES])
        cleared, loaded, hashed = s.sem("cleared"), s.sem("loaded"), s.sem("hashed")
        turned, indexed, chained = s.sem("turned"), s.sem("indexed"), s.sem("chained")
        gathered = g["ctx"].enter_context(nc.semaphore("tok_gathered"))
        flat = ids.rearrange("b t -> (b t)")
        with nc.Block() as block:
            @block.sync
            def _(sp):
                sp.wait_ge(cleared, 1)
                sp.dma_start(ids_row[0:1, BACK:W], flat[0:P].unsqueeze(0)).then_inc(loaded, 16)
                for k in range(0, W, P):
                    width = min(P, W - k)
                    rows_of = flat[P - BACK:N - BACK].rearrange("(j c) -> j c", c=P) if k == 0 else \
                        ids.rearrange("b t -> (b t)").rearrange("(j c) -> j c", c=P)[1:TILES, P - BACK:P]
                    sp.dma_start(ids_row[1:TILES, k:k + width], rows_of[:, 0:width]).then_inc(loaded, 16)

            @block.gpsimd
            def _(pool):
                pool.wait_ge(indexed, 1)
                for n, table in enumerate(tables):
                    for j in range(TILES):
                        pool.indirect_dma_start(
                            rows[n][:, j, :], None, table,
                            bass.IndirectOffsetOnAxis(ap=index[:, n, j:j + 1], axis=0)).then_inc(gathered, 16)

            @block.tensor
            def _(pe):
                pe.wait_ge(hashed, 1)
                for n in range(len(GRAMS)):
                    last = pe.transpose(index_ps[:, n, :], hashes[:, n, BACK:W], g["ident"][0:TILES, 0:TILES])
                last.then_inc(turned, 1)

            @block.vector
            def _(dve):
                link = Chain(dve, chained)
                dve.memset(ids_row[:, :], 0).then_inc(cleared, 1)
                dve.wait_ge(loaded, 48)
                link(dve.tensor_copy(ids_f[:, :], ids_row[:, :]))
                link(dve.memset(hashes[:, :, :], 0.0))
                before = ids_f[:, :]
                for n in range(len(GRAMS)):
                    v = hashes[:, n, n + 1:W]
                    q, qi = quot[:, n + 1:W], quot_i[:, n + 1:W]
                    link(dve.scalar_tensor_tensor(out=v, in0=before[:, n:W - 1], scalar=float(PRIME),
                                                  in1=ids_f[:, n + 1:W], op0=ALU.mult, op1=ALU.add))
                    link(dve.tensor_scalar(qi, v, 1.0 / VOCAB, None, ALU.mult))
                    link(dve.tensor_copy(q, qi))
                    link(dve.scalar_tensor_tensor(out=v, in0=q, scalar=-float(VOCAB), in1=v,
                                                  op0=ALU.mult, op1=ALU.add))
                    link(dve.tensor_scalar(q, v, 0.0, float(VOCAB), ALU.is_lt, ALU.mult))
                    link(dve.tensor_tensor(v, v, q, ALU.add))
                    link(dve.tensor_scalar(q, v, float(VOCAB), -float(VOCAB), ALU.is_ge, ALU.mult))
                    link(dve.tensor_tensor(v, v, q, ALU.add))
                    before = hashes[:, n, :]
                dve.sem_inc(hashed, 1)
                dve.wait_ge(turned, 1)
                dve.tensor_copy(index[:, :, :], index_ps[:, :, :]).then_inc(indexed, 1)
                dve.wait_ge(gathered, 16 * len(GRAMS) * TILES)
                for n in range(len(GRAMS)):
                    link(dve.memset(rows[n][0:n + 1, 0:TILES:CT, :], 0.0))
                link(dve.tensor_tensor(h[:, :, :], rows[0][:, :, :], rows[1][:, :, :], ALU.add))
                link(dve.tensor_tensor(h[:, :, :], h[:, :, :], rows[2][:, :, :], ALU.add))
                link(dve.tensor_scalar(h[:, :, :], h[:, :, :], 1.0 / (len(GRAMS) + 1), None, ALU.mult))
        s.clear()


RNN_HEADS, RNN_DH = 8, 32
RNN_C = RNN_HEADS * RNN_DH
STEPS = B


def recurrent_stage(nc, g, w):
    h, ident = g["h"], g["ident"]
    with ExitStack() as ctx:
        s = Stage(nc, ctx, "rnn")
        wide = 5 * RNN_C + 2 * RNN_HEADS
        pair = 2 * RNN_C
        w_high = s.sb("w_high", [P, wide], F32R)
        w_low = s.sb("w_low", [P, wide], F32R)
        w_out = s.sb("w_out", [P, 2, D])
        gb = s.sb("gb", [P, 2, D])
        x = s.sb("x", [P, TILES + 1, D])
        x_now = s.sb("x_now", [P, STEPS, D])
        x_rows = s.sb("x_rows", [P, STEPS, 2, D], F32R)
        xT = s.sb("xT", [P, STEPS, P], F32R)
        exp_qk = s.sb("exp_qk", [P, STEPS, pair])
        query = [s.sb(f"query{n}", [P, STEPS, RNN_C]) for n in range(2)]
        keys = [s.sb(f"keys{n}", [P, STEPS, 2, RNN_C]) for n in range(2)]
        values = [s.sb(f"values{n}", [P, STEPS, 2, RNN_C]) for n in range(2)]
        rate = [s.sb(f"rate{n}", [P, STEPS, 2, RNN_HEADS]) for n in range(2)]
        u = s.sb("u", [P, STEPS, 2, RNN_C])
        w_in = u[:, :, :, :].rearrange("p s a c -> p (s a c)")[:, 0:wide]
        scratch = s.sb("scratch", [P, STEPS, pair])
        old_prod = s.sb("old_prod", [P, STEPS, pair])
        z_prod = s.sb("z_prod", [P, 2, STEPS, RNN_C])
        hid = old_prod[:, :, RNN_C:pair]
        soft = s.sb("soft", [P, RNN_C])
        dots = s.sb("dots", [P, STEPS, 2 * RNN_HEADS])
        z_dots = s.sb("z_dots", [P, STEPS, RNN_HEADS])
        old = s.sb("old", [P, 2, RNN_C])
        stat = s.sb("stat", [P, 2 * STEPS * RNN_HEADS])
        hidT = s.sb("hidT", [P, 2, P])
        turn_ps = s.ps("turn_ps", [P, T])
        old_ps = out_ps = s.ps("old_out_ps", [P, T])
        in_ps = [s.ps(f"in_ps{n}", [P, T]) for n in range(2)]
        z_ps = [s.ps(f"z_ps{n}", [P, T]) for n in range(4)]
        turns = [slice(n, TILES, CT) for n in range(CT)]
        norms = [Norm(s, g, 2, name=f"norm{n}", halves=turns[2 * n:2 * n + 2], square=scratch[:, :, :].rearrange("p s c -> p (s c)")[:, 0:TILES * D]
                      .rearrange("p (j d) -> p j d", j=TILES)) for n in range(2)]
        names = ["loaded", "chained", "x_ready", "past_end", "w_split", "x_high", "rows_ready", "rows_turned",
                 "xT_ready", "projected", "in_taken", "prepared", "rkey_ready", "rkey_exp",
                 "z_prod_ready", "z_ready", "h_ready", "h_exp", "hid_ready", "hid_turned", "hidT_ready",
                 "out_ready", "out_taken", "old_prod_ready", "old_ready"]
        (loaded, chained, x_ready, past_end, w_split, x_high, rows_ready, rows_turned,
         xT_ready, projected, in_taken, prepared, rkey_ready, rkey_exp,
         z_prod_ready, z_ready, h_ready, h_exp, hid_ready, hid_turned, hidT_ready,
         out_ready, out_taken, old_prod_ready, old_ready) = [s.sem(n) for n in names]
        heads = lambda v: v.rearrange("p s (h d) -> p (s h) d", d=RNN_DH)
        parts = ((0, pair), (pair, pair), (2 * pair, wide - 2 * pair))
        banks = STEPS * len(parts)

        with nc.Block() as block:
            @block.sync
            def _(sp):
                for half in (slice(0, D), slice(D, P)):
                    sp.dma_start(w_in[half, :], w["w_in"]).then_inc(loaded, 16)
                sp.dma_start(w_out[:, :, :], w["w_out"]).then_inc(loaded, 16)
                sp.dma_start(gb[:, 0, :], row_bc(w["ln_g"], P)).then_inc(loaded, 16)
                sp.dma_start(gb[:, 1, :], row_bc(w["ln_b"], P)).then_inc(loaded, 16)

            @block.gpsimd
            def _(pool):
                pool.memset(x[:, TILES:, :], 0.0).then_inc(past_end, 1)

                def split_weights():
                    pool.wait_ge(loaded, 80)
                    pool.tensor_copy(w_high[:, :], w_in[:, :]).then_inc(w_split, 1)
                    pool.wait_ge(w_split, 1)
                    pool.tensor_tensor(w_low[:, :], w_in[:, :], w_high[:, :], ALU.subtract).then_inc(w_split, 1)

                def split_rows(turn):
                    pool.wait_ge(rows_turned, turn * 2 + 2)
                    pool.tensor_copy(x_now[:, :, :], x[:, bass.ds(turn, STEPS, step=CT), :]).then_inc(x_high, 1)
                    pool.wait_ge(x_high, 1)
                    pool.tensor_copy(x_rows[:, :, 0, :], x_now[:, :, :]).then_inc(x_high, 1)
                    pool.wait_ge(x_high, 2)
                    pool.tensor_tensor(x_rows[:, :, 1, :], x_now[:, :, :], x_rows[:, :, 0, :], ALU.subtract)\
                        .then_inc(rows_ready, 1)
                    pool.sem_clear(x_high)

                norms[0].gpsimd(pool, after_first=split_weights)
                pool.wait_ge(past_end, 1)
                pool.wait_ge(x_ready, 1)
                split_rows(0)
                norms[1].gpsimd(pool)
                pool.wait_ge(x_ready, 2)
                with pool.Fori(0, CT) as i:
                    split_rows(i + 1)

            @block.tensor
            def _(pe):
                def turn_rows(turn, half):
                    pe.wait_ge(rows_ready, turn + 1)
                    pe.wait_ge(xT_ready, turn * 2 + (half + 1))
                    for k in range(4):
                        last = pe.transpose(turn_ps[:, k * P:(k + 1) * P],
                                            x_rows[:, 4 * half + k, :, :].rearrange("p a d -> p (a d)").bitcast(F32),
                                            ident[:, :])
                    last.then_inc(rows_turned, 1)

                def project(turn, t):
                    if t % 4 == 0:
                        pe.wait_ge(xT_ready, turn * 2 + (t // 4 + 2))
                    for k, (first, width) in enumerate(parts):
                        m = 3 * t + k
                        pe.wait_ge(in_taken, turn * banks + (m + 1))
                        out = in_ps[m % 2][:, 0:width]
                        pe.matmul(out, xT[:, t, :], w_high[:, first:first + width], start=True, stop=False)
                        pe.matmul(out, xT[:, t, :], w_low[:, first:first + width], start=False, stop=True)\
                            .then_inc(projected, 1)

                pe.wait_ge(loaded, 80)
                pe.wait_ge(w_split, 2)
                pe.sem_inc(rows_turned, 2)
                turn_rows(0, 0)
                for t in range(STEPS):
                    project(0, t)
                    if t == 0:
                        turn_rows(0, 1)
                with pe.Fori(0, CT // 2) as i:
                    for n in range(2):
                        turn = i * 2 + n
                        pe.wait_ge(hidT_ready, turn * STEPS + 1)
                        turn_rows(turn + 1, 0)
                        for t in range(STEPS + 1):
                            if 0 < t < STEPS:
                                if t == 1:
                                    pe.wait_ge(out_taken, turn + 1)
                                pe.wait_ge(old_prod_ready, turn * (STEPS - 1) + t)
                                for step in range(t):
                                    last = pe.matmul(old_ps[:, :], ident[:, :], old_prod[:, step, :],
                                                     start=(step == 0), stop=(step == t - 1))
                                last.then_inc(old_ready, 1)
                            if t < STEPS:
                                project(turn + 1, t)
                            if t == 0:
                                turn_rows(turn + 1, 1)
                            else:
                                z = t - 1
                                pe.wait_ge(z_prod_ready, turn * STEPS + t)
                                for step in range(t):
                                    last = pe.matmul(z_ps[z // 2][:, z % 2 * RNN_C:(z % 2 + 1) * RNN_C], ident[:, :],
                                                     z_prod[:, z % 2, step, :], start=(step == 0), stop=(step == z))
                                last.then_inc(z_ready, 1)
                        for t in range(STEPS):
                            pe.wait_ge(hid_ready, turn * STEPS + (t + 1))
                            pe.wait_ge(xT_ready, turn * 2 + 5)
                            pe.wait_ge(hidT_ready, turn * STEPS + (t + 1))
                            for k in range(2):
                                last = pe.transpose(turn_ps[:, k * P:(k + 1) * P], hid[:, t, k * P:(k + 1) * P],
                                                    ident[:, :])
                            last.then_inc(hid_turned, 1)
                            pe.wait_ge(hidT_ready, turn * STEPS + (t + 2))
                            for k in range(2):
                                last = pe.matmul(out_ps[:, t * D:(t + 1) * D], hidT[:, k, :], w_out[:, k, :],
                                                 start=(k == 0), stop=(k == 1))
                            last.then_inc(out_ready, 1)

            @block.scalar
            def _(a):
                def take_xT(turn, half):
                    a.wait_ge(rows_turned, turn * 2 + (half + 3))
                    a.activation(xT[:, 4 * half:4 * half + 4, :].rearrange("p s q -> p (s q)"), turn_ps[:, :],
                                 ACT.Copy).then_inc(xT_ready, 1)

                def take_step(turn, n, t):
                    m = 3 * t
                    a.wait_ge(projected, turn * banks + (m + 1))
                    bank = in_ps[m % 2]
                    a.activation(exp_qk[:, t, :], bank[:, :], ACT.Exp)
                    a.activation(query[n][:, t, :], bank[:, 0:RNN_C], ACT.Relu)
                    a.activation(keys[n][:, t, 0, :], bank[:, RNN_C:pair], ACT.Relu).then_inc(in_taken, 1)
                    a.wait_ge(projected, turn * banks + (m + 2))
                    a.activation(values[n][:, t, :, :].rearrange("p a c -> p (a c)"), in_ps[(m + 1) % 2][:, :],
                                 ACT.Copy).then_inc(in_taken, 1)
                    a.wait_ge(projected, turn * banks + (m + 3))
                    bank = in_ps[(m + 2) % 2]
                    a.activation(keys[n][:, t, 1, :], bank[:, 0:RNN_C], ACT.Copy)
                    a.activation(rate[n][:, t, :, :],
                                 bank[:, RNN_C:RNN_C + 2 * RNN_HEADS].rearrange("p (a h) -> p a h", a=2),
                                 ACT.Exp, scale=-1.0).then_inc(in_taken, 1)

                a.sem_inc(xT_ready, 1)
                a.sem_inc(in_taken, 2)
                a.sem_inc(hidT_ready, 1)
                a.sem_inc(out_taken, 1)
                for n in (0, 0, 1):
                    norms[n].scalar(a, x[:, 0:TILES, :])
                take_xT(0, 0)
                for t in range(STEPS):
                    if t == STEPS // 2:
                        norms[1].scalar(a, x[:, 0:TILES, :])
                    take_step(0, 0, t)
                    if t == 0:
                        take_xT(0, 1)
                with a.Fori(0, CT // 2) as i:
                    for n in range(2):
                        turn = i * 2 + n
                        a.wait_ge(rkey_ready, turn + 1)
                        a.activation(keys[n][:, :, 1, :], keys[n][:, :, 1, :], ACT.Exp).then_inc(rkey_exp, 1)
                        take_xT(turn + 1, 0)
                        a.wait_ge(prepared, turn + 1)
                        for t in range(STEPS):
                            take_step(turn + 1, 1 - n, t)
                            if t == 0:
                                take_xT(turn + 1, 1)
                        for t in range(STEPS):
                            if t + 1 < STEPS:
                                a.wait_ge(h_ready, turn * (STEPS - 1) + (t + 1))
                                a.activation(soft[:, :], soft[:, :], ACT.Exp).then_inc(h_exp, 1)
                            a.wait_ge(hid_turned, turn * STEPS + (t + 2))
                            a.wait_ge(out_ready, turn * STEPS + (t + 1))
                            a.activation(hidT[:, :, :], turn_ps[:, 0:2 * P].rearrange("p (k q) -> p k q", k=2),
                                         ACT.Copy).then_inc(hidT_ready, 1)
                        a.wait_ge(out_ready, turn * STEPS + (STEPS + 1))
                        a.activation(x[:, bass.ds(turn, STEPS, step=CT), :],
                                     out_ps[:, :].rearrange("p (s d) -> p s d", s=STEPS), ACT.Copy)\
                            .then_inc(out_taken, 1)

            @block.vector
            def _(dve):
                link = Chain(dve, chained)
                dve.wait_ge(loaded, 80)
                for n, norm in enumerate(norms):
                    norm.vector(dve, link, h[:, 0:TILES, :], x[:, 0:TILES, :])
                    for tiles in turns[2 * n:2 * n + 2]:
                        link(dve.tensor_tensor(h[:, tiles, :], h[:, tiles, :], x[:, tiles, :], ALU.add))
                    norm.vector(dve, link, x[:, 0:TILES, :], x[:, 0:TILES, :], gb[:, 0, :], gb[:, 1, :])
                    dve.sem_inc(x_ready, 1)
                dve.sem_inc(out_ready, 1)
                dve.sem_inc(z_ready, 2)
                dve.sem_inc(hid_turned, 1)
                one_head = soft[:, :].rearrange("p (h d) -> p h d", d=RNN_DH)
                few = stat[:, 0:RNN_HEADS]
                dve.wait_ge(w_split, 2)
                with dve.Fori(0, CT // 2) as i:
                    for n in range(2):
                        turn = i * 2 + n
                        link.restart()
                        q, key, value = query[n], keys[n], values[n]
                        dve.wait_ge(in_taken, turn * banks + (banks + 2))
                        small = stat[:, 0:STEPS * RNN_HEADS]
                        grouped = lambda v: v.rearrange("p (s h) -> p s h", h=RNN_HEADS)
                        split = lambda v: v.rearrange("p s (h d) -> p s h d", d=RNN_DH)
                        r = split(key[:, :, 1, :])
                        link(dve.tensor_reduce(grouped(small), r, X, ALU.max))
                        link(dve.tensor_tensor(r, r, spread(grouped(small), RNN_DH), ALU.subtract))
                        dve.sem_inc(rkey_ready, 1)
                        for half, v in ((0, q[:, :, :]), (1, key[:, :, 0, :])):
                            link(dve.scalar_tensor_tensor(out=v, in0=exp_qk[:, :, half * RNN_C:(half + 1) * RNN_C],
                                                          scalar=1.0, in1=v, op0=ALU.min, op1=ALU.add))
                        dve.sem_inc(prepared, 1)
                        rates = rate[n][:, :, :, :]
                        link(dve.tensor_scalar(rates, rates, 1.0, None, ALU.add))
                        link(dve.reciprocal(rates, rates))
                        for k, v in enumerate((q[:, :, :], key[:, :, 0, :], key[:, :, 1, :])):
                            if k == 2:
                                dve.wait_ge(rkey_exp, turn + 1)
                            link(dve.tensor_reduce(grouped(small), split(v), X, ALU.add))
                            link(dve.reciprocal(small, small))
                            link(dve.tensor_tensor(split(v), split(v), spread(grouped(small), RNN_DH), ALU.mult))

                        def score(pr, ks, by, dt, count):
                            width = by.shape[-1]
                            link(dve.tensor_tensor(pr, ks, by.unsqueeze(1).to_broadcast([P, count, width]), ALU.mult))
                            link(dve.tensor_reduce(dt, split(pr), X, ALU.add))

                        both = lambda v: v.rearrange("p s a c -> p s (a c)")
                        by_head = lambda v: v.rearrange("p a (h d) -> p a h d", d=RNN_DH)

                        def write_u(t, src):
                            link(dve.tensor_tensor(by_head(u[:, t, :, :]), by_head(src),
                                                   spread(rate[n][:, t, :, :], RNN_DH), ALU.mult))

                        def score_old(t):
                            score(scratch[:, 0:t, :], both(key[:, 0:t, :, :]),
                                  key[:, t, :, :].rearrange("p a c -> p (a c)"), dots[:, 0:t, :], t)

                        def z_products(t):
                            dve.wait_ge(z_ready, turn * STEPS + (t + 1))
                            pr, dt = z_prod[:, t % 2, 0:t + 1, :], z_dots[:, 0:t + 1, :]
                            score(pr, key[:, 0:t + 1, 0, :], q[:, t, :], dt, t + 1)
                            link(dve.tensor_tensor(split(pr), split(u[:, 0:t + 1, 0, :]), spread(dt, RNN_DH), ALU.mult))
                            dve.sem_inc(z_prod_ready, 1)

                        write_u(0, value[:, 0, :, :])
                        score_old(1)
                        dve.wait_ge(hid_turned, turn * STEPS + 1)
                        for t in range(1, STEPS):
                            pr = old_prod[:, 0:t, :]
                            link(dve.tensor_tensor(split(pr), split(both(u[:, 0:t, :, :])), spread(dots[:, 0:t, :], RNN_DH),
                                                   ALU.mult))
                            dve.sem_inc(old_prod_ready, 1)
                            z_products(t - 1)
                            if t + 1 < STEPS:
                                score_old(t + 1)
                            dve.wait_ge(old_ready, turn * (STEPS - 1) + t)
                            link(dve.tensor_tensor(old[:, :, :], value[:, t, :, :],
                                                   old_ps[:, :].rearrange("p (a c) -> p a c", a=2), ALU.subtract))
                            write_u(t, old[:, :, :])
                        z_products(STEPS - 1)

                        for t in range(STEPS):
                            dt = dots[:, 0:t + 1, 0:RNN_HEADS]
                            pr = scratch[:, 0:t + 1, 0:RNN_C]
                            if t == 0:
                                link(dve.memset(soft[:, :], 1.0 / RNN_DH))
                            else:
                                last_h = hid[:, t - 1, :].rearrange("p (h d) -> p h d", d=RNN_DH)
                                link(dve.tensor_reduce(few, last_h, X, ALU.max))
                                link(dve.tensor_tensor(one_head, last_h, spread(few, RNN_DH), ALU.subtract))
                                dve.sem_inc(h_ready, 1)
                                dve.wait_ge(h_exp, turn * (STEPS - 1) + t)
                                link(dve.tensor_reduce(few, one_head, X, ALU.add))
                                link(dve.reciprocal(few, few))
                                link(dve.tensor_tensor(one_head, one_head, spread(few, RNN_DH), ALU.mult))
                            score(pr, key[:, 0:t + 1, 1, :], soft[:, :], dt, t + 1)
                            link(dve.tensor_tensor(split(pr), split(u[:, 0:t + 1, 1, :]), spread(dt, RNN_DH), ALU.mult))
                            link(dve.tensor_reduce(old[:, 0, :], pr.rearrange("p s c -> p c s"), X, ALU.add))
                            if t == 0:
                                dve.wait_ge(z_ready, turn * STEPS + (STEPS + 2))
                            link(dve.tensor_tensor(hid[:, t, :], z_ps[t // 2][:, t % 2 * RNN_C:(t % 2 + 1) * RNN_C],
                                                   old[:, 0, :], ALU.add))
                            dve.sem_inc(hid_ready, 1)
                dve.wait_ge(out_taken, CT + 1)
                dve.tensor_tensor(h[:, :, :], h[:, :, :], x[:, 0:TILES, :], ALU.add)
        s.clear()


PAIRS = E // 2
RING = 3


def expert_stage(nc, g, name, w, act, per_expert, gating, top, capacity=None, norms=1,
                 gamma_beta=None, expert_norm=None, limit_infinite=False):
    h, ident, ones = g["h"], g["ident"], g["ones"]
    blocks = E * per_expert
    pair = 2 * per_expert
    exp_at = 6 if capacity else 5 if per_expert > 1 else 3
    with ExitStack() as ctx:
        s = Stage(nc, ctx, name)
        w1 = s.sb("w1", [P, blocks * P])
        w1_high = s.sb("w1_high", [P, blocks * P], F32R)
        w1_low = s.sb("w1_low", [P, blocks * P], F32R)
        w2 = s.sb("w2", [P, blocks, D])
        b1 = s.sb("b1", [P, blocks])
        b2 = s.sb("b2", [P, PAIRS])
        wg = s.sb("wg", [P, E])
        wg_high = s.sb("wg_high", [P, E], F32R)
        wg_low = s.sb("wg_low", [P, E], F32R)
        bg = s.sb("bg", [P, E])
        x = s.sb("x", [P, TILES + CT, D])
        x_now = s.sb("x_now", [P, CT, D])
        x_chunk = s.sb("x_chunk", [P, CT, 2, D], F32R)
        xT = s.sb("xT", [P, T], F32R)
        hidden = s.sb("hidden", [P, RING, T])
        logit = s.sb("logit", [P, CT, E])
        share = s.sb("share", [P, CT, E])
        gate = s.sb("gate", [P, CT, E])
        stat = s.sb("stat", [P, CT])
        pairs = s.sb("pairs", [P, CT, E, E])
        ties = s.sb("ties", [P, CT, E, E])
        rank = s.sb("rank", [P, CT, E])
        yT = s.sb("yT", [P, 2, T])
        y = s.sb("y", [P, CT, E * D])
        warm = s.sb("warm", [P, 1])
        total = s.sb("total", [P, CT, D])
        xT_ps = s.ps("xT_ps", [P, T])
        small_ps = s.ps("small_ps", [P, T])
        hid_ps = [s.ps(f"hid_ps{n}", [P, T]) for n in range(RING)]
        y_ps = [s.ps(f"y_ps{n}", [P, T]) for n in range(2)]
        back_ps = s.ps("back_ps", [P, T])
        norm = Norm(s, g, norms)
        loaded, chained = s.sem("loaded"), s.sem("chained")
        w_split, x_high, past_end = s.sem("w_split"), s.sem("x_high"), s.sem("past_end")
        w_high = s.sem("w_high")
        x_ready, chunk_ready, chunk_turned = s.sem("x_ready"), s.sem("chunk_ready"), s.sem("chunk_turned")
        xT_ready, logits_ready, shifted = s.sem("xT_ready"), s.sem("logits_ready"), s.sem("shifted")
        exp_ready = s.sem("exp_ready")
        hid_ready, act_done, y_done = s.sem("hid_ready"), s.sem("act_done"), s.sem("y_done")
        yT_ready, y_back, back_taken = s.sem("yT_ready"), s.sem("y_back"), s.sem("back_taken")
        small_taken = s.sem("small_taken")
        gb = None
        loads = 8
        if gamma_beta:
            gb = s.sb("gamma_beta", [P, 2, D])
            loads += 2
        if expert_norm:
            eg, eb = s.sb("expert_g", [P, E]), s.sb("expert_b", [D, E])
            bias_ready, scaled = s.sem("bias_ready"), s.sem("scaled")
            loads += 3
        if capacity:
            picked, counted = s.sem("picked"), s.sem("counted")
            base = s.sb("base", [P, CT + 1, E])
            place = s.sb("place", [P, CT, E])
        if limit_infinite:
            odd = s.sb("odd", [P, CT * D], U32)
            filler = s.sb("filler", [P, 3, CT * D])

        with nc.Block() as block:
            @block.sync
            def _(sp):
                for half in (slice(0, D), slice(D, P)):
                    sp.dma_start(w1[half, :], w["w1"]).then_inc(loaded, 16)
                    sp.dma_start(wg[half, :], w["wg"]).then_inc(loaded, 16)
                sp.dma_start(w2[:, :, :], w["w2"]).then_inc(loaded, 16)
                sp.dma_start(b1[:, :], w["b1"]).then_inc(loaded, 16)
                sp.dma_start(b2[:, :], w["b2"]).then_inc(loaded, 16)
                sp.dma_start(bg[:, :], row_bc(w["bg"], P)).then_inc(loaded, 16)
                if gamma_beta:
                    sp.dma_start(gb[:, 0, :], row_bc(gamma_beta[0], P)).then_inc(loaded, 16)
                    sp.dma_start(gb[:, 1, :], row_bc(gamma_beta[1], P)).then_inc(loaded, 16)
                if expert_norm:
                    sp.dma_start(eg[0:D, :], expert_norm[0]).then_inc(loaded, 16)
                    sp.dma_start(eg[D:P, :], expert_norm[0]).then_inc(loaded, 16)
                    sp.dma_start(eb[:, :], expert_norm[1]).then_inc(loaded, 16)

            @block.gpsimd
            def _(pool):
                pool.memset(x[:, TILES:, :], 0.0).then_inc(past_end, 1)
                norm.gpsimd(pool)
                pool.wait_ge(x_ready, 1)
                pool.wait_ge(past_end, 1)
                with pool.Fori(0, B + 1) as i:
                    pool.wait_ge(chunk_turned, i + 1)
                    pool.tensor_copy(x_now[:, :, :], x[:, bass.ds(i * CT, CT), :]).then_inc(x_high, 1)
                    pool.wait_ge(x_high, 1)
                    pool.tensor_copy(x_chunk[:, :, 0, :], x_now[:, :, :]).then_inc(x_high, 1)
                    pool.wait_ge(x_high, 2)
                    pool.tensor_tensor(x_chunk[:, :, 1, :], x_now[:, :, :], x_chunk[:, :, 0, :], ALU.subtract)\
                        .then_inc(chunk_ready, 1)
                    pool.sem_clear(x_high)

            @block.tensor
            def _(pe):
                pe.wait_ge(loaded, 16 * loads)
                if expert_norm:
                    for n in range(blocks):
                        last = pe.matmul(small_ps[:, 64 + n:65 + n], w1[0:D, n * P:(n + 1) * P],
                                         eb[:, n // per_expert:n // per_expert + 1], start=True, stop=True)
                    last.then_inc(bias_ready, 1)
                pe.wait_ge(w_split, 1)
                pe.sem_inc(chunk_turned, 1)
                pe.sem_inc(y_done, 2)

                def turn_chunk():
                    for j in range(CT):
                        last = pe.transpose(xT_ps[:, j * P:(j + 1) * P],
                                            x_chunk[:, j, :, :].rearrange("p a d -> p (a d)").bitcast(F32),
                                            ident[:, :])
                    last.then_inc(chunk_turned, 1)

                pe.wait_ge(chunk_ready, 1)
                turn_chunk()

                def hidden_block(n, freed):
                    pe.wait_ge(act_done, freed)
                    pe.matmul(hid_ps[n % RING][:, :], w1_high[:, n * P:(n + 1) * P], xT[:, :],
                              start=True, stop=False)
                    pe.matmul(hid_ps[n % RING][:, :], w1_low[:, n * P:(n + 1) * P], xT[:, :],
                              start=False, stop=True).then_inc(hid_ready, 1)

                pe.wait_ge(xT_ready, 1)
                for n in range(RING - 1):
                    hidden_block(n, 2)
                with pe.Fori(0, B) as i:
                    def turn_back(q):
                        pe.wait_ge(yT_ready, i * PAIRS + (q + 3))
                        pe.wait_ge(back_taken, i * PAIRS + (q + 2))
                        for j in range(CT):
                            last = pe.transpose(back_ps[:, j * P:(j + 1) * P],
                                                yT[:, q % 2, j * P:(j + 1) * P], ident[:, :])
                        last.then_inc(y_back, 1)

                    pe.wait_ge(small_taken, i + 1)
                    for j in range(CT):
                        for part in (wg_high, wg_low):
                            last = pe.matmul(small_ps[:, j * E:(j + 1) * E], xT[:, j * P:(j + 1) * P],
                                             part[:, :], start=(part is wg_high), stop=(part is wg_low))
                    last.then_inc(logits_ready, 1)
                    for n in range(blocks):
                        if n + RING - 1 < blocks:
                            hidden_block(n + RING - 1, i * blocks + (n + 2))
                        if n == blocks // 2 + 1 and capacity:
                            pe.wait_ge(picked, i + 1)
                            pe.matmul(small_ps[:, 32:64], g["upto"][:, :], rank[:, :, :], start=True, stop=True)
                            pe.matmul(small_ps[:, 64:96], g["ones"][:, :], rank[:, :, :], start=True, stop=True)\
                                .then_inc(counted, 1)
                        if n == 2:
                            pe.wait_ge(chunk_ready, i + 2)
                            turn_chunk()
                        e, part = n // per_expert, n % per_expert
                        q, side = e // 2, e % 2 * D
                        if n % pair == 0:
                            pe.wait_ge(yT_ready, i * PAIRS + (q + 1))
                        pe.wait_ge(act_done, i * blocks + (n + 3))
                        pe.matmul(y_ps[q % 2][side:side + D, :], w2[:, n, :], hidden[:, n % RING, :],
                                  start=(part == 0), stop=(part == per_expert - 1)).then_inc(y_done, 1)
                        if n % pair == (pair - 1 if capacity else 1) and q:
                            turn_back(q - 1)
                    pe.wait_ge(xT_ready, i + 2)
                    for n in range(RING - 1):
                        hidden_block(n, i * blocks + (blocks + 2))
                    turn_back(PAIRS - 1)

            @block.scalar
            def _(act_engine):
                a = act_engine
                a.sem_inc(act_done, 2)

                def high_parts():
                    a.wait_ge(loaded, 16 * loads)
                    if expert_norm:
                        a.wait_ge(scaled, 1)
                    a.activation(w1_high[:, :], w1[:, :], ACT.Copy).then_inc(w_high, 1)
                    a.activation(wg_high[:, :], wg[:, :], ACT.Copy).then_inc(w_high, 1)

                norm.scalar(a, x[:, 0:TILES, :])
                high_parts()
                if norms > 1:
                    norm.scalar(a, x[:, 0:TILES, :])
                a.activation(warm[:, :], ones[:, 0:1], ACT.Exp if capacity else act)
                a.sem_inc(yT_ready, 2)
                a.wait_ge(chunk_turned, 2)
                a.activation(xT[:, :], xT_ps[:, :], ACT.Copy).then_inc(xT_ready, 1)
                with a.Fori(0, B) as i:
                    def take_pair(q):
                        a.wait_ge(y_done, i * blocks + ((q + 1) * pair + 2))
                        a.wait_ge(y_back, i * PAIRS + (q + 1))
                        a.activation(yT[:, q % 2, :], y_ps[q % 2][:, :], ACT.Identity, bias=b2[:, q:q + 1])\
                            .then_inc(yT_ready, 1)

                    for n in range(blocks):
                        a.wait_ge(hid_ready, i * blocks + (n + 1))
                        a.wait_ge(y_done, i * blocks + max(n, 2))
                        a.activation(hidden[:, n % RING, :], hid_ps[n % RING][:, :], act, bias=b1[:, n:n + 1])\
                            .then_inc(act_done, 1)
                        if n and n % pair == 0:
                            take_pair(n // pair - 1)
                        if n == exp_at and gating != "mask":
                            a.wait_ge(shifted, i + 1)
                            a.activation(share[:, :, :], logit[:, :, :], ACT.Exp).then_inc(exp_ready, 1)
                    a.wait_ge(chunk_turned, i + 3)
                    a.activation(xT[:, :], xT_ps[:, :], ACT.Copy).then_inc(xT_ready, 1)
                    take_pair(PAIRS - 1)

            @block.vector
            def _(dve):
                link = Chain(dve, chained)

                def split_weights():
                    dve.wait_ge(loaded, 16 * loads)
                    if expert_norm:
                        dve.wait_ge(bias_ready, 1)
                        link(dve.tensor_tensor(b1[:, :], b1[:, :], small_ps[:, 64:64 + blocks], ALU.add))
                        for e in range(E):
                            part = w1[:, e * per_expert * P:(e + 1) * per_expert * P]
                            link(dve.tensor_scalar(part, part, eg[:, e:e + 1], None, ALU.mult))
                        dve.sem_inc(scaled, 1)
                    dve.wait_ge(w_high, 2)
                    link(dve.tensor_tensor(w1_low[:, :], w1[:, :], w1_high[:, :], ALU.subtract))
                    link(dve.tensor_tensor(wg_low[:, :], wg[:, :], wg_high[:, :], ALU.subtract))
                    dve.sem_inc(w_split, 1)

                if capacity:
                    link(dve.memset(base[:, :, :], 0.0))
                if limit_infinite:
                    link(dve.memset(filler[:, 0, :], 1e4))
                    link(dve.memset(filler[:, 1, :], -1e4))
                    link(dve.memset(filler[:, 2, :], 0.0))
                for n in range(norms):
                    last_norm = n == norms - 1
                    norm.vector(dve, link, h[:, :, :] if n == 0 else x[:, 0:TILES, :], x[:, 0:TILES, :],
                                *((gb[:, 0, :], gb[:, 1, :]) if gamma_beta and last_norm else ()),
                                meanwhile=split_weights if n == 0 else None)
                dve.sem_inc(x_ready, 1)
                dve.sem_inc(back_taken, 2)
                dve.sem_inc(small_taken, 1)
                dve.sem_inc(y_back, 2)
                with dve.Fori(0, B) as i:
                    link.restart()
                    dve.wait_ge(logits_ready, i + 1)
                    link(dve.tensor_tensor(logit[:, :, :],
                                           small_ps[:, 0:CT * E].rearrange("p (j e) -> p j e", j=CT),
                                           bg[:, :].unsqueeze(1).to_broadcast([P, CT, E]), ALU.add))
                    key = logit
                    if gating != "mask":
                        link(dve.tensor_reduce(stat[:, :], logit[:, :, :], X, ALU.max))
                        dve.tensor_tensor(pairs[:, :, 0, :], logit[:, :, :], spread(stat[:, :], E),
                                          ALU.subtract).then_inc(chained, 1)
                        link.count += 1
                        dve.wait_ge(chained, link.count)
                        dve.tensor_copy(logit[:, :, :], pairs[:, :, 0, :]).then_inc(shifted, 1)
                        dve.wait_ge(exp_ready, i + 1)
                        if gating in ("top", "renormed"):
                            link(dve.tensor_reduce(stat[:, :], share[:, :, :], X, ALU.add))
                            link(dve.reciprocal(stat[:, :], stat[:, :]))
                            link(dve.tensor_tensor(share[:, :, :], share[:, :, :], spread(stat[:, :], E), ALU.mult))
                            key = share
                    k = key[:, :, :]
                    link(dve.tensor_tensor(pairs[:, :, :, :], k.unsqueeze(2).to_broadcast([P, CT, E, E]),
                                           spread(k, E), ALU.subtract))
                    flat = lambda v: v[:, :, :, :].rearrange("p j e f -> p (j e f)")
                    link(dve.scalar_tensor_tensor(out=flat(ties), in0=flat(pairs), scalar=0.0,
                                                  in1=flat(g["before"]), op0=ALU.is_equal, op1=ALU.mult))
                    link(dve.scalar_tensor_tensor(out=flat(pairs), in0=flat(pairs), scalar=0.0,
                                                  in1=flat(ties), op0=ALU.is_gt, op1=ALU.add))
                    link(dve.tensor_reduce(rank[:, :, :], pairs[:, :, :, :], X, ALU.add))
                    if gating == "mask":
                        link(dve.tensor_scalar(gate[:, :, :], rank[:, :, :], float(top), None, ALU.is_lt))
                    else:
                        link(dve.scalar_tensor_tensor(out=gate[:, :, :], in0=rank[:, :, :], scalar=float(top),
                                                      in1=share[:, :, :], op0=ALU.is_lt, op1=ALU.mult))
                    if gating in ("renormed", "softmax"):
                        link(dve.tensor_reduce(stat[:, :], gate[:, :, :], X, ALU.add))
                        link(dve.reciprocal(stat[:, :], stat[:, :]))
                        link(dve.tensor_tensor(gate[:, :, :], gate[:, :, :], spread(stat[:, :], E), ALU.mult))
                    if capacity:
                        link(dve.tensor_scalar(rank[:, :, :], rank[:, :, :], float(top), None, ALU.is_lt))
                        dve.sem_inc(picked, 1)
                        dve.wait_ge(counted, i + 1)
                        for j in range(CT):
                            link(dve.tensor_tensor(base[:, j + 1, :], base[:, j, :],
                                                   small_ps[:, 64 + j * E:64 + (j + 1) * E], ALU.add))
                        link(dve.tensor_tensor(place[:, :, :], base[:, 0:CT, :],
                                               small_ps[:, 32:64].rearrange("p (j e) -> p j e", j=CT), ALU.add))
                        link(dve.tensor_copy(base[:, 0, :], base[:, CT, :]))
                        link(dve.scalar_tensor_tensor(out=gate[:, :, :], in0=place[:, :, :], scalar=float(capacity),
                                                      in1=gate[:, :, :], op0=ALU.is_le, op1=ALU.mult))
                    dve.sem_inc(small_taken, 1)
                    for q in range(PAIRS):
                        dve.wait_ge(y_back, i * PAIRS + (q + 3))
                        dve.tensor_tensor(y[:, :, q * P:(q + 1) * P].rearrange("p j (a d) -> p j a d", a=2),
                                          back_ps[:, :].rearrange("p (j a d) -> p j a d", j=CT, a=2),
                                          spread(gate[:, :, 2 * q:2 * q + 2], D), ALU.mult)\
                            .then_inc(back_taken, 1)
                    dve.wait_ge(back_taken, i * PAIRS + (PAIRS + 2))
                    link(dve.tensor_reduce(total[:, :, :], y[:, :, :].rearrange("p j (e d) -> p j d e", e=E),
                                           X, ALU.add))
                    if limit_infinite:
                        flat_total = total[:, :, :].rearrange("p j d -> p (j d)")
                        for n, (test, bound) in enumerate(((ALU.is_gt, 3.4028235e38), (ALU.is_lt, -3.4028235e38))):
                            link(dve.tensor_scalar(odd[:, :], flat_total, bound, None, test))
                            link(dve.copy_predicated(flat_total, odd[:, :], filler[:, n, :]))
                        link(dve.tensor_tensor(odd[:, :], flat_total, flat_total, ALU.not_equal))
                        link(dve.copy_predicated(flat_total, odd[:, :], filler[:, 2, :]))
                    h_chunk = h[:, bass.ds(i * CT, CT), :]
                    link(dve.tensor_tensor(h_chunk, h_chunk, total[:, :, :], ALU.add))
        s.clear()


MEM_DH = 256
BLK = MEM_DH // P
CHUNK = 64
NORM_MIN = 1e-12


def memory_stage(nc, g, w):
    with ExitStack() as ctx:
        s = Stage(nc, ctx, "mem")
        kept = dict(
            hkT=s.sb("hkT", [P, BLK, N]), hqT=s.sb("hqT", [P, BLK, N]), hk=s.sb("hk", [P, TILES, MEM_DH]),
            v=s.sb("v", [P, TILES, D]), gate=s.sb("gate", [P, TILES + CT, D]), rates=s.sb("rates", [P, 3, TILES]))
        kept["retrieved"] = kept["v"]
        project(nc, g, w, kept)
        recur(nc, g, w, kept)
        give_back(nc, g, w, kept)


def project(nc, g, w, kept):
    h, ident, ones = g["h"], g["ident"], g["ones"]
    lower, upper = slice(0, D), slice(D, P)
    with ExitStack() as ctx:
        s = Stage(nc, ctx, "memp")
        maps = s.sb("maps", [P, 7, D])
        maps_parts = [s.sb(f"maps_{n}", [P, 7, D], F32R) for n in ("high", "low")]
        w1_k, w1_q = s.sb("w1_k", [P, MEM_DH]), s.sb("w1_q", [P, MEM_DH])
        taps = s.sb("taps", [P, 2, 3])
        shift = s.sb("shift", [P, 2])
        pair_ones = s.sb("pair_ones", [P, P])
        x = s.sb("x", [P, TILES + CT, D])
        x_now = s.sb("x_now", [P, CT, D])
        x_chunk = s.sb("x_chunk", [P, CT, 2, D], F32R)
        xT = s.sb("xT", [P, T], F32R)
        raw = s.sb("raw", [P, 2, T + 2])
        conv = s.sb("conv", [P, 2, T])
        unit = s.sb("unit", [P, T])
        square = s.sb("square", [P, T])
        length = s.sb("length", [P, T])
        sig = s.sb("sig", [P, 2, T])
        turn_ps = s.ps("turn_ps", [P, T])
        banks = [s.ps(f"job_ps{n}", [P, T]) for n in range(4)]
        norm = Norm(s, g)
        names = ["loaded", "chained", "x_ready", "chunk_ready", "chunk_turned", "xT_ready", "made", "taken",
                 "squared", "scaled", "v_ready", "paired", "raw_ready", "w_split", "x_high", "past_end"]
        (loaded, chained, x_ready, chunk_ready, chunk_turned, xT_ready, made, taken, squared, scaled,
         v_ready, paired, raw_ready, w_split, x_high, past_end) = [s.sem(n) for n in names]
        LENGTH, VALUES, MEANS, KQ, VT, EA, GATE, HKT, HK, HQT, JOBS = 0, 1, 2, 3, 4, 5, 6, 7, 9, 11, 13
        LOADS = 2 * 7 + 2 + 3 + 3

        with nc.Block() as block:
            @block.sync
            def _(sp):
                for n, name in enumerate(("W_K", "W_Q", "W_V", "W_th", "W_et", "W_al", "W_gate")):
                    for rows in (lower, upper):
                        sp.dma_start(maps[rows, n, :], w[name]).then_inc(loaded, 16)
                for rows, to in ((lower, w1_k), (upper, w1_q)):
                    sp.dma_start(to[rows, :], w["W1"]).then_inc(loaded, 16)
                for rows, n, name in ((lower, 0, "conv_k"), (upper, 0, "conv_q"), (lower, 1, "conv_v")):
                    sp.dma_start(taps[rows, n, :], w[name]).then_inc(loaded, 16)
                for rows, n, name in ((upper, 0, "b_th"), (lower, 1, "b_et"), (upper, 1, "b_al")):
                    sp.dma_start(shift[rows, n:n + 1], w[name]).then_inc(loaded, 16)

            @block.gpsimd
            def _(pool):
                pool.memset(pair_ones[lower, lower], 1.0).then_inc(paired, 1)
                pool.memset(pair_ones[upper, upper], 1.0).then_inc(paired, 1)
                pool.memset(pair_ones[lower, upper], 0.0).then_inc(paired, 1)
                pool.memset(pair_ones[upper, lower], 0.0).then_inc(paired, 1)
                pool.wait_ge(paired, 4)
                pool.memset(x[:, TILES:, :], 0.0).then_inc(past_end, 1)
                norm.gpsimd(pool)
                pool.wait_ge(loaded, 16 * LOADS)
                high, low = maps_parts
                pool.tensor_copy(high[:, :, :], maps[:, :, :]).then_inc(w_split, 1)
                pool.wait_ge(w_split, 1)
                pool.tensor_tensor(low[:, :, :], maps[:, :, :], high[:, :, :], ALU.subtract).then_inc(w_split, 1)
                pool.wait_ge(x_ready, 1)
                pool.wait_ge(past_end, 1)
                with pool.Fori(0, B + 1) as i:
                    pool.wait_ge(chunk_turned, i + 1)
                    pool.tensor_copy(x_now[:, :, :], x[:, bass.ds(i * CT, CT), :]).then_inc(x_high, 1)
                    pool.wait_ge(x_high, 1)
                    pool.tensor_copy(x_chunk[:, :, 0, :], x_now[:, :, :]).then_inc(x_high, 1)
                    pool.wait_ge(x_high, 2)
                    pool.tensor_tensor(x_chunk[:, :, 1, :], x_now[:, :, :], x_chunk[:, :, 0, :], ALU.subtract)\
                        .then_inc(chunk_ready, 1)
                    pool.sem_clear(x_high)

            @block.tensor
            def _(pe):
                pe.wait_ge(loaded, 16 * LOADS)
                pe.wait_ge(paired, 4)
                pe.wait_ge(w_split, 2)
                pe.sem_inc(chunk_turned, 1)
                tile = lambda v, j: v[:, j * P:(j + 1) * P]

                def turn_chunk(chunk):
                    pe.wait_ge(chunk_ready, chunk + 1)
                    for j in range(CT):
                        last = pe.transpose(turn_ps[:, j * P:(j + 1) * P],
                                            x_chunk[:, j, :, :].rearrange("p a d -> p (a d)").bitcast(F32), ident[:, :])
                    last.then_inc(chunk_turned, 1)

                def first_maps(chunk, bank):
                    pe.wait_ge(xT_ready, chunk + 1)
                    for n in (KQ, VT, EA):
                        b = bank(n)
                        for k, part in enumerate(maps_parts):
                            first = 2 * (n - KQ)
                            last = pe.matmul(b[:, :], part[:, first:first + 2, :].rearrange("d a e -> d (a e)"),
                                             xT[:, :], start=(k == 0), stop=(k == 1))
                        last.then_inc(made, 1)
                    b = bank(GATE)
                    for j in range(CT):
                        for k, part in enumerate(maps_parts):
                            last = pe.matmul(b[:, j * D:(j + 1) * D], tile(xT, j), part[:, 6, :],
                                             start=(k == 0), stop=(k == 1))
                    last.then_inc(made, 1)

                turn_chunk(0)
                first_maps(0, lambda n: banks[n % 4])
                with pe.Fori(0, B) as i:

                    def bank(n):
                        pe.wait_ge(taken, i * JOBS + (5 if n < 4 else n + 2))
                        return banks[n % 4]

                    turn_chunk(i + 1)
                    b = bank(LENGTH)
                    pe.wait_ge(squared, i + 1)
                    pe.wait_ge(v_ready, i + 1)
                    pe.matmul(b[:, :], pair_ones[:, :], square[:, :], start=True, stop=True).then_inc(made, 1)
                    b = banks[VALUES % 4]
                    for j in range(CT):
                        last = pe.transpose(b[:, j * D:(j + 1) * D], tile(conv[lower, 1, :], j), ident[lower, lower])
                    last.then_inc(made, 1)
                    b = banks[MEANS % 4]
                    for j in range(CT):
                        pe.matmul(b[:, 2 * CT + j:2 * CT + j + 1], tile(sig[upper, 0, :], j), ones[upper, 0:1],
                                  start=True, stop=True)
                        last = pe.matmul(b[:, 2 * j:2 * j + 2], tile(sig[:, 1, :], j), pair_ones[:, 0:P:D],
                                         start=True, stop=True)
                    last.then_inc(made, 1)
                    first_maps(i + 1, bank)
                    pe.wait_ge(scaled, i + 2)
                    for k in range(BLK):
                        b = bank(HKT + k)
                        pe.matmul(b[:, :], w1_k[:, k * P:(k + 1) * P], unit[:, :], start=True, stop=True)\
                            .then_inc(made, 1)
                    for k in range(CT // 2):
                        b = bank(HK + k)
                        for j in range(2):
                            last = pe.matmul(b[:, j * MEM_DH:(j + 1) * MEM_DH], tile(unit, 2 * k + j),
                                             w1_k[:, :], start=True, stop=True)
                        last.then_inc(made, 1)
                    for k in range(BLK):
                        b = bank(HQT + k)
                        pe.matmul(b[:, :], w1_q[:, k * P:(k + 1) * P], unit[:, :], start=True, stop=True)\
                            .then_inc(made, 1)

            @block.scalar
            def _(a):
                a.sem_inc(taken, 1)
                norm.scalar(a, x[:, 0:TILES, :])
                a.wait_ge(loaded, 16 * LOADS)

                def take_xT(chunk):
                    a.wait_ge(chunk_turned, chunk + 2)
                    a.activation(xT[:, :], turn_ps[:, :], ACT.Copy).then_inc(xT_ready, 1)

                def take_first(chunk, made_by):
                    a.activation(raw[:, 0, 1:T + 1], made_by(KQ)[:, :], ACT.Copy).then_inc(taken, 1)
                    b = made_by(VT)
                    a.activation(raw[lower, 1, 1:T + 1], b[lower, :], ACT.Copy).then_inc(raw_ready, 1)
                    a.activation(sig[upper, 0, :], b[upper, :], ACT.Sigmoid, bias=shift[upper, 0:1]).then_inc(taken, 1)
                    a.activation(sig[:, 1, :], made_by(EA)[:, :], ACT.Sigmoid, bias=shift[:, 1:2]).then_inc(taken, 1)
                    a.activation(kept["gate"][:, bass.ds(chunk * CT, CT), :],
                                 made_by(GATE)[:, 0:CT * D].rearrange("p (j d) -> p j d", d=D), ACT.Sigmoid)\
                        .then_inc(taken, 1)

                def made_before(n):
                    a.wait_ge(made, n - KQ + 1)
                    return banks[n % 4]

                take_xT(0)
                a.wait_ge(scaled, 1)
                take_first(0, made_before)
                with a.Fori(0, B) as i:
                    tiles = bass.ds(i * CT, CT)
                    tokens = bass.ds(i * T, T)

                    def made_by(n):
                        a.wait_ge(made, i * JOBS + (n + 5))
                        return banks[n % 4]

                    a.activation(length[:, :], made_by(LENGTH)[:, :], ACT.Sqrt).then_inc(taken, 1)
                    take_xT(i + 1)
                    a.activation(kept["v"][:, tiles, :],
                                 made_by(VALUES)[:, 0:CT * D].rearrange("p (j d) -> p j d", d=D), ACT.Copy)\
                        .then_inc(taken, 1)
                    b = made_by(MEANS)
                    a.activation(kept["rates"][:, 0, tiles], b[:, 2 * CT:3 * CT], ACT.Copy, scale=1.0 / D)
                    a.activation(kept["rates"][:, 1:3, tiles], b[:, 0:2 * CT].rearrange("p (j k) -> p k j", k=2),
                                 ACT.Copy, scale=1.0 / D).then_inc(taken, 1)
                    a.wait_ge(v_ready, i + 1)
                    take_first(i + 1, made_by)
                    for k in range(BLK):
                        a.activation(kept["hkT"][:, k, tokens], made_by(HKT + k)[:, :], ACT.Silu).then_inc(taken, 1)
                    for k in range(CT // 2):
                        a.activation(kept["hk"][:, bass.ds(i * CT + 2 * k, 2), :],
                                     made_by(HK + k)[:, :].rearrange("p (j f) -> p j f", f=MEM_DH), ACT.Silu)\
                            .then_inc(taken, 1)
                    for k in range(BLK):
                        a.activation(kept["hqT"][:, k, tokens], made_by(HQT + k)[:, :], ACT.Silu).then_inc(taken, 1)

            @block.vector
            def _(dve):
                link = Chain(dve, chained)
                norm.vector(dve, link, h[:, :, :], x[:, 0:TILES, :])
                dve.sem_inc(x_ready, 1)
                dve.wait_ge(loaded, 16 * LOADS)
                link(dve.memset(raw[:, :, :], 0.0))
                link(dve.memset(w1_k[upper, :], 0.0))
                link(dve.memset(w1_q[lower, :], 0.0))
                dve.sem_inc(scaled, 1)
                with dve.Fori(0, B) as i:
                    link.restart()

                    def convolve(n, rows):
                        y = conv[rows, n, :]
                        link(dve.tensor_scalar(y, raw[rows, n, 0:T], taps[rows, n, 0:1], None, ALU.mult))
                        for k in (1, 2):
                            link(dve.scalar_tensor_tensor(out=y, in0=raw[rows, n, k:T + k],
                                                          scalar=taps[rows, n, k:k + 1], in1=y,
                                                          op0=ALU.mult, op1=ALU.add))

                    dve.wait_ge(raw_ready, i + 1)
                    convolve(0, slice(0, P))
                    dve.tensor_tensor(square[:, :], conv[:, 0, :], conv[:, 0, :], ALU.mult).then_inc(squared, 1)
                    convolve(1, lower)
                    dve.sem_inc(v_ready, 1)
                    dve.wait_ge(taken, i * JOBS + (LENGTH + 6))
                    link(dve.tensor_scalar(length[:, :], length[:, :], NORM_MIN, None, ALU.max))
                    link(dve.reciprocal(length[:, :], length[:, :]))
                    link(dve.tensor_tensor(unit[:, :], conv[:, 0, :], length[:, :], ALU.mult))
                    dve.sem_inc(scaled, 1)
        s.clear()


def recur(nc, g, w, kept):
    ident, ones = g["ident"], g["ones"]
    PAIRS = CT
    TH, ET, AL = 0, 1, 2
    TOT = 3
    with ExitStack() as ctx:
        s = Stage(nc, ctx, "memr")
        flip = s.sb("flip", [P, P])
        first = s.sb("first", [P, BLK, D])
        row = s.sb("row", [TILES, 3, P])
        shifted = s.sb("shifted", [TILES, 2, 2, CHUNK])
        zeros = s.sb("zeros", [TILES, CHUNK])
        prods = s.sb("prods", [TILES, 3, 2, CHUNK])
        total = s.sb("total", [TILES, 2, TOT])
        spread_total = s.sb("spread_total", [TILES, 2 * TOT, TILES])
        coef_row = s.sb("coef_row", [TILES, 2, P])
        coef_rev = s.sb("coef_rev", [P, 2 * TILES])
        coef = s.sb("coef", [P, 2, TILES])
        tot = s.sb("tot", [P, 2, TOT, TILES])
        hkT_s = [s.sb(f"hkT_s{n}", [P, BLK, B, P]) for n in range(2)]
        hqT_s = [s.sb(f"hqT_s{n}", [P, BLK, B, P]) for n in range(2)]
        hk_s = [s.sb(f"hk_s{n}", [P, B, MEM_DH]) for n in range(2)]
        memory = s.sb("memory", [P, BLK, B, D])
        momentum = s.sb("momentum", [P, BLK, B, D])
        old = s.sb("old", [P, BLK, B, D])
        push = s.sb("push", [P, BLK, B, D])
        error = s.sb("error", [P, B, D])
        wide = [s.sb(f"wide{n}", [P, B, 2, D]) for n in range(2)]
        row_ps = s.ps("row_ps", [P, T])
        pred_ps, ret_ps = s.ps("pred_ps", [P, T]), s.ps("ret_ps", [P, T])
        up_ps = s.ps("up_ps", [P, 4 * T])
        names = ["loaded", "chained", "flipped", "rows_ready", "rows_taken", "rev_ready", "rev_taken",
                 "coef_ready", "start", "staged0", "staged1", "predicted", "wide_ready", "updated",
                 "memory_ready", "momentum_ready", "returned", "kept_ret", "pushed"]
        (loaded, chained, flipped, rows_ready, rows_taken, rev_ready, rev_taken, coef_ready, start,
         staged0, staged1, predicted, wide_ready, updated, memory_ready, momentum_ready, returned,
         kept_ret, pushed) = [s.sem(n) for n in names]
        staged = (staged0, staged1)
        HALVES = 2 * PAIRS // 2
        ROUNDS = PAIRS // 2

        with nc.Block() as block:
            @block.sync
            def _(sp):
                sp.dma_start(first[:, :, :], w["W2"]).then_inc(loaded, 16)
                with sp.Fori(0, ROUNDS) as i:
                    for p in range(2):
                        sp.wait_ge(returned, i * HALVES + (2 * p + 2))
                        at = (i * 2 + p)
                        for k in range(BLK):
                            for to, of in ((hkT_s, kept["hkT"]), (hqT_s, kept["hqT"])):
                                sp.dma_start(to[p][:, k, :, :],
                                             of[:, k, :].rearrange("p (b c q) -> p b c q", b=B, q=P)
                                             [:, :, bass.ds(at, 1), :].rearrange("p b c q -> p (b c) q"))\
                                    .then_inc(staged[p], 16)
                        sp.dma_start(hk_s[p][:, :, :], kept["hk"][:, bass.ds(at, B, step=PAIRS), :])\
                            .then_inc(staged[p], 16)

            @block.gpsimd
            def _(pool):
                pool.memset(flip[:, :], 0.0).then_inc(flipped, 1)
                pool.wait_ge(flipped, 1)
                pool.affine_select(out=flip[:, :].rearrange("p (a c) -> p a c", c=CHUNK),
                                   in_=flip[:, :].rearrange("p (a c) -> p a c", c=CHUNK),
                                   compare_op=ALU.not_equal, fill=1.0, base=-(CHUNK - 1),
                                   pattern=[[-CHUNK, 2], [1, CHUNK]], channel_multiplier=1).then_inc(flipped, 1)

            @block.tensor
            def _(pe):
                pe.wait_ge(flipped, 2)
                for k in range(3):
                    last = pe.matmul(row_ps[0:TILES, k * P:(k + 1) * P], kept["rates"][:, k, :], flip[:, :],
                                     start=True, stop=True)
                last.then_inc(rows_ready, 1)
                pe.wait_ge(rows_taken, 1)
                for k in range(2):
                    last = pe.matmul(ret_ps[:, k * TILES:(k + 1) * TILES], coef_row[:, k, :],
                                     ident[0:TILES, 0:TILES], start=True, stop=True)
                last = pe.matmul(ret_ps[:, 4 * TILES:4 * TILES + 2 * TOT * TILES], ones[0:TILES, :],
                                 spread_total[:, :, :], start=True, stop=True)
                last.then_inc(rev_ready, 1)
                pe.wait_ge(rev_taken, 1)
                pe.matmul(ret_ps[:, 2 * TILES:4 * TILES], flip[:, :], coef_rev[:, :], start=True, stop=True)\
                    .then_inc(coef_ready, 1)
                pe.wait_ge(start, 1)
                pe.sem_inc(returned, 4)
                with pe.Fori(0, ROUNDS) as i:

                    def predict(n):
                        p, half = n // 2, n % 2 * CHUNK
                        if n % 2 == 0:
                            pe.wait_ge(staged[p], i * 80 + 80)
                        pe.wait_ge(memory_ready, i * HALVES + (n + 1))
                        pe.wait_ge(loaded, 16)
                        for b in range(B):
                            for k in range(BLK):
                                last = pe.matmul(pred_ps[half:half + CHUNK, b * D:(b + 1) * D],
                                                 hkT_s[p][:, k, b, half:half + CHUNK], memory[:, k, b, :],
                                                 start=(k == 0), stop=(k == BLK - 1))
                        last.then_inc(predicted, 1)

                    def update(n):
                        p, half = n // 2, n % 2 * CHUNK
                        pe.wait_ge(momentum_ready, i * HALVES + (n + 1))
                        pe.wait_ge(wide_ready, i * HALVES + (n + 1))
                        for k in range(BLK):
                            for b in range(B):
                                at = (k * B + b) * 2 * D
                                last = pe.matmul(up_ps[:, at:at + 2 * D],
                                                 hk_s[p][:, b, k * P:(k + 1) * P],
                                                 wide[n % 2][:, b, :, :].rearrange("p a d -> p (a d)"),
                                                 start=True, stop=True)
                            last.then_inc(updated, 1)

                    def give(n):
                        p, half = n // 2, n % 2 * CHUNK
                        pe.wait_ge(kept_ret, i * HALVES + (n + 1))
                        pe.wait_ge(memory_ready, i * HALVES + (n + 2))
                        pe.wait_ge(loaded, 16)
                        for b in range(B):
                            for k in range(BLK):
                                last = pe.matmul(ret_ps[half:half + CHUNK, b * D:(b + 1) * D],
                                                 hqT_s[p][:, k, b, half:half + CHUNK], memory[:, k, b, :],
                                                 start=(k == 0), stop=(k == BLK - 1))
                        last.then_inc(returned, 1)

                    for n in range(HALVES):
                        predict(n)
                        if n:
                            give(n - 1)
                        update(n)
                    give(HALVES - 1)

            @block.scalar
            def _(a):
                a.sem_inc(kept_ret, 1)
                a.activation(zeros[0:1, 0:1], ones[0:1, 0:1], ACT.Copy).then_inc(pushed, 1)
                with a.Fori(0, ROUNDS) as i:
                    for n in range(HALVES):
                        half = n % 2 * CHUNK
                        a.wait_ge(returned, i * HALVES + (n + 5))
                        a.activation(kept["retrieved"][half:half + CHUNK, bass.ds(i * 2 + n // 2, B, step=PAIRS), :],
                                     ret_ps[half:half + CHUNK, :].rearrange("p (b d) -> p b d", d=D), ACT.Copy)\
                            .then_inc(kept_ret, 1)

            @block.vector
            def _(dve):
                link = Chain(dve, chained)
                dve.wait_ge(rows_ready, 1)
                link(dve.tensor_copy(row[:, :, :], row_ps[0:TILES, 0:3 * P].rearrange("p (k c) -> p k c", c=P)))
                link(dve.tensor_scalar(row[:, AL, :], row[:, AL, :], -1.0, 1.0, ALU.mult, ALU.add))
                dve.wait_ge(pushed, 1)
                link(dve.memset(zeros[:, :], 0.0))
                link(dve.memset(shifted[:, :, :, :], 1.0))
                halves = lambda k: row[:, k, :].rearrange("p (a c) -> p a c", c=CHUNK)
                for k, of in enumerate((ET, AL)):
                    link(dve.tensor_copy(shifted[:, k, :, 1:CHUNK], halves(of)[:, :, 0:CHUNK - 1]))
                PB, WT, PE_ = 0, 1, 2
                for a in range(2):
                    link(dve.tensor_tensor_scan(prods[:, PB, a, :], shifted[:, 1, a, :], zeros[:, :], 1.0,
                                                ALU.mult, ALU.add))
                    link(dve.tensor_tensor_scan(prods[:, PE_, a, :], shifted[:, 0, a, :], zeros[:, :], 1.0,
                                                ALU.mult, ALU.add))
                    link(dve.tensor_tensor_scan(prods[:, WT, a, :], shifted[:, 0, a, :], prods[:, PB, a, :], 0.0,
                                                ALU.mult, ALU.add))
                end = slice(CHUNK - 1, CHUNK)
                for k, (of, by) in enumerate(((PB, AL), (WT, ET), (PE_, ET))):
                    link(dve.tensor_tensor(total[:, :, k:k + 1], prods[:, of, :, end], halves(by)[:, :, end], ALU.mult))
                flat = lambda v: v.rearrange("p a c -> p (a c)")
                for k, of in enumerate((WT, PE_)):
                    link(dve.scalar_tensor_tensor(out=coef_row[:, k, :], in0=flat(prods[:, of, :, :]), scalar=-1.0,
                                                  in1=row[:, TH, :], op0=ALU.mult, op1=ALU.mult))
                link(dve.tensor_tensor(spread_total[:, :, :], spread(flat(total[:, :, :]), TILES),
                                       ident[0:TILES, 0:TILES].unsqueeze(1).to_broadcast([TILES, 2 * TOT, TILES]),
                                       ALU.mult))
                dve.sem_inc(rows_taken, 1)
                dve.wait_ge(rev_ready, 1)
                link(dve.tensor_copy(coef_rev[:, :], ret_ps[:, 0:2 * TILES]))
                link(dve.tensor_copy(tot[:, :, :, :],
                                     ret_ps[:, 4 * TILES:4 * TILES + 2 * TOT * TILES]
                                     .rearrange("p (a k j) -> p a k j", a=2, k=TOT)))
                dve.sem_inc(rev_taken, 1)
                dve.wait_ge(coef_ready, 1)
                link(dve.tensor_copy(coef[:, :, :], ret_ps[:, 2 * TILES:4 * TILES].rearrange("p (k j) -> p k j", k=2)))
                dve.wait_ge(loaded, 16)
                link(dve.tensor_copy(memory[:, :, :, :], first[:, :, :].unsqueeze(2).to_broadcast([P, BLK, B, D])))
                link(dve.memset(momentum[:, :, :, :], 0.0))
                link(dve.memset(wide[0][CHUNK:P, :, :, :], 0.0))
                link(dve.memset(wide[1][0:CHUNK, :, :, :], 0.0))
                dve.sem_inc(start, 1)
                dve.sem_inc(memory_ready, 1)
                dve.sem_inc(momentum_ready, 1)
                up = up_ps[:, :].rearrange("p (n a d) -> p n a d", a=2, d=D)
                merged = lambda v: v[:, :, :, :].rearrange("p k b d -> p (k b) d")
                with dve.Fori(0, ROUNDS) as i:
                    link.restart()
                    for n in range(HALVES):
                        lo = n % 2 * CHUNK
                        tiles = bass.ds(i * 2 + n // 2, B, step=PAIRS)

                        def by(k):
                            return spread(tot[:, n % 2, k, tiles], D).unsqueeze(1).to_broadcast([P, BLK, B, D])

                        part = slice(lo, lo + CHUNK)
                        dve.wait_ge(predicted, i * HALVES + (n + 1))
                        link(dve.tensor_tensor(error[part, :, :], pred_ps[part, :].rearrange("p (b d) -> p b d", d=D),
                                               kept["v"][part, tiles, :], ALU.subtract))
                        for k in range(2):
                            link(dve.tensor_tensor(wide[n % 2][part, :, k, :], error[part, :, :],
                                                   spread(coef[part, k, tiles], D), ALU.mult))
                        dve.sem_inc(wide_ready, 1)
                        link(dve.tensor_tensor(old[:, :, :, :], memory[:, :, :, :], by(0), ALU.mult))
                        link(dve.tensor_tensor(push[:, :, :, :], momentum[:, :, :, :], by(1), ALU.mult))
                        link(dve.tensor_tensor(old[:, :, :, :], old[:, :, :, :], push[:, :, :, :], ALU.add))
                        link(dve.tensor_tensor(momentum[:, :, :, :], momentum[:, :, :, :], by(2), ALU.mult))
                        for k in range(BLK):
                            dve.wait_ge(updated, i * HALVES * BLK + (n * BLK + k + 1))
                            link(dve.tensor_tensor(memory[:, k, :, :], old[:, k, :, :], up[:, k * B:(k + 1) * B, 0, :],
                                                   ALU.add))
                        dve.sem_inc(memory_ready, 1)
                        link(dve.tensor_tensor(merged(momentum), merged(momentum), up[:, :, 1, :], ALU.add))
                        dve.sem_inc(momentum_ready, 1)
        s.clear()


def give_back(nc, g, w, kept):
    h, ident, got = g["h"], g["ident"], kept["retrieved"]
    with ExitStack() as ctx:
        s = Stage(nc, ctx, "memo")
        proj = s.sb("proj", [D, D])
        gb = s.sb("gb", [P, 2, D])
        o_chunk = s.sb("o_chunk", [P, CT, D])
        oT = s.sb("oT", [D, T])
        turn_ps, out_ps = s.ps("turn_ps", [P, T]), s.ps("out_ps", [P, T])
        norm = Norm(s, g)
        names = ["loaded", "chained", "o_ready", "chunk_ready", "chunk_turned", "oT_ready", "projected", "out_taken"]
        loaded, chained, o_ready, chunk_ready, chunk_turned, oT_ready, projected, out_taken = \
            [s.sem(n) for n in names]
        with nc.Block() as block:
            @block.sync
            def _(sp):
                sp.dma_start(proj[:, :], w["W_proj"]).then_inc(loaded, 16)
                sp.dma_start(gb[:, 0, :], row_bc(w["ln_g"], P)).then_inc(loaded, 16)
                sp.dma_start(gb[:, 1, :], row_bc(w["ln_b"], P)).then_inc(loaded, 16)

            @block.gpsimd
            def _(pool):
                norm.gpsimd(pool)
                pool.wait_ge(o_ready, 1)
                with pool.Fori(0, B) as i:
                    pool.wait_ge(chunk_turned, i + 1)
                    pool.tensor_copy(o_chunk[:, :, :], got[:, bass.ds(i * CT, CT), :]).then_inc(chunk_ready, 1)

            @block.tensor
            def _(pe):
                pe.wait_ge(loaded, 48)
                pe.sem_inc(chunk_turned, 1)
                with pe.Fori(0, B) as i:
                    pe.wait_ge(chunk_ready, i + 1)
                    turn_pairs(pe, turn_ps, o_chunk, ident, CT).then_inc(chunk_turned, 1)
                    pe.wait_ge(out_taken, i + 1)
                    pe.wait_ge(oT_ready, i + 1)
                    for j in range(CT):
                        last = pe.matmul(out_ps[:, j * D:(j + 1) * D], oT[:, j * P:(j + 1) * P], proj[:, :],
                                         start=True, stop=True)
                    last.then_inc(projected, 1)

            @block.scalar
            def _(a):
                norm.scalar(a, got[:, :, :])
                with a.Fori(0, B) as i:
                    a.wait_ge(chunk_turned, i + 2)
                    take_pairs(lambda o, i_: a.activation(o, i_, ACT.Copy), oT[:, :], turn_ps, CT)\
                        .then_inc(oT_ready, 1)

            @block.vector
            def _(dve):
                link = Chain(dve, chained)
                dve.wait_ge(loaded, 48)
                norm.vector(dve, link, got[:, :, :], got[:, :, :], gb[:, 0, :], gb[:, 1, :])
                link(dve.tensor_tensor(got[:, :, :], got[:, :, :], kept["gate"][:, 0:TILES, :], ALU.mult))
                dve.sem_inc(o_ready, 1)
                dve.sem_inc(out_taken, 1)
                with dve.Fori(0, B) as i:
                    dve.wait_ge(projected, i + 1)
                    h_chunk = h[:, bass.ds(i * CT, CT), :]
                    dve.tensor_tensor(h_chunk, h_chunk, out_ps[:, 0:CT * D].rearrange("p (j d) -> p j d", d=D),
                                      ALU.add).then_inc(out_taken, 1)
        s.clear()


SQ_HEADS, SQ_DH = 8, 8


def square_stage(nc, g, w):
    h, ident = g["h"], g["ident"]
    PAIRS = SQ_HEADS // 2
    WV = SQ_HEADS + D
    WK = D + WV
    with ExitStack() as ctx:
        s = Stage(nc, ctx, "sq")
        q_i, q_j = s.sb("q_i", [P, PAIRS, P]), s.sb("q_j", [P, PAIRS, P])
        q_i_parts = [s.sb(f"q_i_{n}", [P, PAIRS, P], F32R) for n in ("high", "low")]
        q_j_parts = [s.sb(f"q_j_{n}", [P, PAIRS, P], F32R) for n in ("high", "low")]
        qb_i, qb_j = s.sb("qb_i", [P, PAIRS]), s.sb("qb_j", [P, PAIRS])
        qb = s.sb("qb", [D, 1])
        wt = s.sb("wt", [P, 3 * D])
        wt_parts = [s.sb(f"wt_{n}", [P, 3 * D], F32R) for n in ("high", "low")]
        kvb = s.sb("kvb", [P, 2 * D])
        proj_w, proj_b = s.sb("proj_w", [D, D]), s.sb("proj_b", [P, D])
        blocks = s.sb("blocks", [P, PAIRS + 1, WV])
        x = s.sb("x", [P, TILES + CT, D])
        x_now = s.sb("x_now", [P, CT, D])
        x_chunk = s.sb("x_chunk", [P, CT, 2, D], F32R)
        xT = s.sb("xT", [P, T], F32R)
        kv = s.sb("kv", [P, CT, WK])
        kk = s.sb("kk", [P, CT, SQ_HEADS, SQ_DH * SQ_DH])
        sums = s.sb("sums", [P, PAIRS + 1, WV])
        left = s.sb("left", [P, 2, T])
        qq = s.sb("qq", [P, PAIRS, T])
        q1 = s.sb("q1", [D + 1, T])
        recip = s.sb("recip", [P, CT, SQ_HEADS])
        mix = s.sb("mix", [P, CT, D])
        mixT = s.sb("mixT", [D, T])
        part = s.sb("part", [P, CT, D])
        turn_ps, sum_ps = s.ps("turn_ps", [P, T]), s.ps("sum_ps", [P, T])
        kv_ps = s.ps("kv_ps", [P, T])
        mix_ps = q1_ps = proj_ps = s.ps("few_ps", [P, T])
        left_ps = [s.ps(f"left_ps{n}", [P, T]) for n in range(2)]
        right_ps = [s.ps(f"right_ps{n}", [P, T]) for n in range(2)]
        norm = Norm(s, g)
        names = ["loaded", "chained", "x_ready", "chunk_ready", "chunk_turned", "xT_ready", "kv_projected",
                 "kk_ready", "summed", "sums_ready", "q1_projected", "q1_ready", "paired", "left_ready",
                 "qq_ready", "mixed", "mix_ready", "mix_turned", "mixT_ready", "projected", "out_taken", "w_split", "x_high", "past_end", "w_high"]
        (loaded, chained, x_ready, chunk_ready, chunk_turned, xT_ready, kv_projected, kk_ready, summed,
         sums_ready, q1_projected, q1_ready, paired, left_ready, qq_ready, mixed, mix_ready, mix_turned,
         mixT_ready, projected, out_taken, w_split, x_high, past_end, w_high) = [s.sem(n) for n in names]
        weights = ((q_i[:, :, :], [v[:, :, :] for v in q_i_parts]), (q_j[:, :, :], [v[:, :, :] for v in q_j_parts]),
                   (wt[:, :], [v[:, :] for v in wt_parts]))
        LOADS = 13

        with nc.Block() as block:
            @block.sync
            def _(sp):
                for half in (slice(0, D), slice(D, P)):
                    sp.dma_start(q_i[half, :, :], w["q_i"].rearrange("d (a p) -> d a p", p=P)).then_inc(loaded, 16)
                    sp.dma_start(q_j[half, :, :], w["q_j"].rearrange("d (a p) -> d a p", p=P)).then_inc(loaded, 16)
                    sp.dma_start(wt[half, :], w["w"]).then_inc(loaded, 16)
                sp.dma_start(blocks[:, :, :], w["blocks"]).then_inc(loaded, 16)
                for to, of in ((qb_i, w["qb_i"]), (qb_j, w["qb_j"]), (qb, w["qb"]),
                               (proj_w, w["proj_w"]), (proj_b, row_bc(w["proj_b"], P)),
                               (kvb, row_bc(w["b"][D:3 * D], P))):
                    sp.dma_start(to[:, :], of).then_inc(loaded, 16)

            @block.gpsimd
            def _(pool):
                pool.memset(x[:, TILES:, :], 0.0).then_inc(past_end, 1)
                norm.gpsimd(pool)
                pool.wait_ge(w_high, 3)
                for of, (high, low) in weights:
                    pool.tensor_tensor(low, of, high, ALU.subtract).then_inc(w_split, 1)
                pool.wait_ge(x_ready, 1)
                pool.wait_ge(past_end, 1)
                with pool.Fori(0, B + 1) as i:
                    pool.wait_ge(chunk_turned, i + 1)
                    pool.tensor_copy(x_now[:, :, :], x[:, bass.ds(i * CT, CT), :]).then_inc(x_high, 1)
                    pool.wait_ge(x_high, 1)
                    pool.tensor_copy(x_chunk[:, :, 0, :], x_now[:, :, :]).then_inc(x_high, 1)
                    pool.wait_ge(x_high, 2)
                    pool.tensor_tensor(x_chunk[:, :, 1, :], x_now[:, :, :], x_chunk[:, :, 0, :], ALU.subtract)\
                        .then_inc(chunk_ready, 1)
                    pool.sem_clear(x_high)

            @block.tensor
            def _(pe):
                pe.wait_ge(loaded, 16 * LOADS)
                pe.sem_inc(chunk_turned, 1)
                pe.wait_ge(w_split, 3)

                def project_kv(c):
                    pe.wait_ge(chunk_ready, c + 1)
                    for j in range(CT):
                        last = pe.transpose(turn_ps[:, j * P:(j + 1) * P],
                                            x_chunk[:, j, :, :].rearrange("p a d -> p (a d)").bitcast(F32), ident[:, :])
                    last.then_inc(chunk_turned, 1)
                    pe.wait_ge(xT_ready, c + 1)
                    for j in range(CT):
                        for k, part in enumerate(wt_parts):
                            last = pe.matmul(kv_ps[:, j * 2 * D:(j + 1) * 2 * D], xT[:, j * P:(j + 1) * P],
                                             part[:, D:3 * D], start=(k == 0), stop=(k == 1))
                    last.then_inc(kv_projected, 1)

                def project_q1():
                    for k, part in enumerate(wt_parts):
                        last = pe.matmul(q1_ps[0:D, :], part[:, 0:D], xT[:, :], start=(k == 0), stop=(k == 1))
                    last.then_inc(q1_projected, 1)

                def project_pair(c, a):
                    pe.wait_ge(qq_ready, c * PAIRS + (a + 1))
                    for out, parts in ((left_ps, q_i_parts), (right_ps, q_j_parts)):
                        for k, part in enumerate(parts):
                            last = pe.matmul(out[a % 2][:, :], part[:, a, :], xT[:, :], start=(k == 0), stop=(k == 1))
                    last.then_inc(paired, 1)

                project_kv(0)
                project_q1()
                for a in range(PAIRS):
                    project_pair(0, a)
                with pe.Fori(0, B) as i:
                    pe.wait_ge(kk_ready, i + 1)
                    for a in range(PAIRS):
                        for j in range(CT):
                            pe.matmul(sum_ps[:, a * WV:(a + 1) * WV],
                                      kk[:, j, 2 * a:2 * a + 2, :].rearrange("p a f -> p (a f)"),
                                      kv[:, j, D:WK], start=(j == 0), stop=(j == CT - 1))
                    for j in range(CT):
                        last = pe.matmul(sum_ps[0:D + 1, PAIRS * WV:(PAIRS + 1) * WV], kv[:, j, 0:D + 1],
                                         kv[:, j, D:WK], start=(j == 0), stop=(j == CT - 1))
                    last.then_inc(summed, 1)
                    project_kv(i + 1)
                    pe.wait_ge(sums_ready, i + 1)
                    pe.wait_ge(qq_ready, i * PAIRS + (PAIRS + 2))
                    pe.wait_ge(q1_ready, i + 1)
                    pe.wait_ge(out_taken, i + 1)
                    for j in range(CT):
                        out = mix_ps[:, j * WV:(j + 1) * WV]
                        for a in range(PAIRS):
                            pe.matmul(out, qq[:, a, j * P:(j + 1) * P], sums[:, a, :], start=(a == 0), stop=False)
                        last = pe.matmul(out, q1[:, j * P:(j + 1) * P], sums[0:D + 1, PAIRS, :],
                                         start=False, stop=True)
                    last.then_inc(mixed, 1)
                    project_pair(i + 1, 0)
                    pe.wait_ge(mix_ready, i + 1)
                    turn_pairs(pe, turn_ps, mix, ident, CT).then_inc(mix_turned, 1)
                    project_q1()
                    project_pair(i + 1, 1)
                    pe.wait_ge(mixT_ready, i + 1)
                    pe.wait_ge(q1_ready, i + 2)
                    for j in range(CT):
                        last = pe.matmul(proj_ps[:, j * D:(j + 1) * D], mixT[:, j * P:(j + 1) * P],
                                         proj_w[:, :], start=True, stop=True)
                    last.then_inc(projected, 1)
                    project_pair(i + 1, 2)
                    project_pair(i + 1, 3)

            @block.scalar
            def _(a_):
                a = a_
                copy = lambda o, i_: a.activation(o, i_, ACT.Copy)
                norm.scalar(a, x[:, 0:TILES, :])
                a.wait_ge(loaded, 16 * LOADS)
                for of, (high, _) in weights:
                    a.activation(high, of, ACT.Copy).then_inc(w_high, 1)
                a.activation(left[0:1, 0, 0:1], g["ones"][0:1, 0:1], ACT.Copy)

                def take_xT(c):
                    a.wait_ge(chunk_turned, c + 2)
                    copy(xT[:, :], turn_ps[:, :]).then_inc(xT_ready, 1)

                def take_q1(c):
                    a.wait_ge(q1_projected, c + 1)
                    a.activation(q1[0:D, :], q1_ps[0:D, :], ACT.Identity, bias=qb[:, 0:1]).then_inc(q1_ready, 1)

                def take_left(c, n):
                    a.wait_ge(paired, c * PAIRS + (n + 1))
                    a.activation(left[:, n % 2, :], left_ps[n % 2][:, :], ACT.Identity, bias=qb_i[:, n:n + 1])\
                        .then_inc(left_ready, 1)

                take_xT(0)
                take_q1(0)
                for n in range(PAIRS):
                    take_left(0, n)
                with a.Fori(0, B) as i:
                    take_xT(i + 1)
                    take_left(i + 1, 0)
                    a.wait_ge(mix_turned, i + 1)
                    take_pairs(copy, mixT[:, :], turn_ps, CT).then_inc(mixT_ready, 1)
                    take_q1(i + 1)
                    for n in range(1, PAIRS):
                        take_left(i + 1, n)

            @block.vector
            def _(dve):
                link = Chain(dve, chained)
                norm.vector(dve, link, h[:, :, :], x[:, 0:TILES, :])
                dve.sem_inc(x_ready, 1)
                dve.sem_inc(qq_ready, 2)
                dve.wait_ge(loaded, 16 * LOADS)
                link(dve.memset(kv[:, :, D:D + SQ_HEADS], 1.0))
                link(dve.memset(q1[D:D + 1, :], 1.0))

                def take_kv(c):
                    dve.wait_ge(kv_projected, c + 1)
                    raw = kv_ps[:, :].rearrange("p (j c) -> p j c", j=CT)
                    bias = lambda a: kvb[:, a * D:(a + 1) * D].unsqueeze(1).to_broadcast([P, CT, D])
                    link(dve.tensor_tensor(kv[:, :, 0:D], raw[:, :, 0:D], bias(0), ALU.add))
                    link(dve.tensor_tensor(kv[:, :, D + SQ_HEADS:WK], raw[:, :, D:2 * D], bias(1), ALU.add))
                    for j in range(CT):
                        k = kv[:, j, 0:D].rearrange("p (h i) -> p h i", i=SQ_DH)
                        last = dve.tensor_tensor(kk[:, j, :, :].rearrange("p h (i j) -> p h i j", j=SQ_DH),
                                                 spread(k, SQ_DH), k.unsqueeze(2).to_broadcast([P, SQ_HEADS, SQ_DH, SQ_DH]),
                                                 ALU.mult)
                    last.then_inc(kk_ready, 1)

                def pair_up(c, n):
                    dve.wait_ge(left_ready, c * PAIRS + (n + 1))
                    dve.scalar_tensor_tensor(out=qq[:, n, :], in0=right_ps[n % 2][:, :], scalar=qb_j[:, n:n + 1],
                                             in1=left[:, n % 2, :], op0=ALU.add, op1=ALU.mult)\
                        .then_inc(qq_ready, 1)

                take_kv(0)
                for n in range(PAIRS):
                    pair_up(0, n)
                dve.sem_inc(out_taken, 1)
                with dve.Fori(0, B) as i:
                    link.restart()
                    dve.wait_ge(summed, i + 1)
                    full = sum_ps[:, 0:(PAIRS + 1) * WV].rearrange("p (a c) -> p a c", c=WV)
                    link(dve.tensor_tensor(sums[:, 0:PAIRS, :], full[:, 0:PAIRS, :], blocks[:, 0:PAIRS, :], ALU.mult))
                    dve.tensor_tensor(sums[0:D + 1, PAIRS, :], full[0:D + 1, PAIRS, :], blocks[0:D + 1, PAIRS, :],
                                      ALU.mult).then_inc(sums_ready, 1)
                    take_kv(i + 1)
                    dve.wait_ge(mixed, i + 1)
                    got = mix_ps[:, 0:CT * WV].rearrange("p (j c) -> p j c", c=WV)
                    link(dve.reciprocal(recip[:, :, :], got[:, :, 0:SQ_HEADS]))
                    dve.tensor_tensor(mix[:, :, :].rearrange("p j (h e) -> p j h e", e=SQ_DH),
                                      got[:, :, SQ_HEADS:WV].rearrange("p j (h e) -> p j h e", e=SQ_DH),
                                      spread(recip[:, :, :], SQ_DH), ALU.mult).then_inc(mix_ready, 1)
                    pair_up(i + 1, 0)
                    pair_up(i + 1, 1)
                    dve.wait_ge(projected, i + 1)
                    link(dve.tensor_tensor(part[:, :, :], proj_ps[:, 0:CT * D].rearrange("p (j d) -> p j d", d=D),
                                           proj_b[:, :].unsqueeze(1).to_broadcast([P, CT, D]), ALU.add))
                    dve.sem_inc(out_taken, 1)
                    h_chunk = h[:, bass.ds(i * CT, CT), :]
                    link(dve.tensor_tensor(h_chunk, h_chunk, part[:, :, :], ALU.add))
                    pair_up(i + 1, 2)
                    pair_up(i + 1, 3)
        s.clear()


def softmax_stage(nc, g, w):
    h, ident = g["h"], g["ident"]
    SCALE = float(D) ** -0.5
    with ExitStack() as ctx:
        s = Stage(nc, ctx, "soft")
        wt = s.sb("wt", [P, 2 * D])
        wt_parts = [s.sb(f"wt_{n}", [P, 2 * D], F32R) for n in ("high", "low")]
        x = s.sb("x", [P, TILES + CT, D])
        x_now = s.sb("x_now", [P, CT, D])
        x_chunk = s.sb("x_chunk", [P, CT, 2, D], F32R)
        xT = s.sb("xT", [P, T], F32R)
        yT_parts = [s.sb(f"yT_{n}", [P, T], F32R) for n in ("high", "low")]
        top = s.sb("top", [P, CT])
        total = s.sb("total", [P, CT])
        prob = s.sb("prob", [P, 2, T])
        probT = s.sb("probT", [P, 2, CT, P])
        part = s.sb("part", [P, CT, D])
        xT_ps, y_ps, out_ps = s.ps("xT_ps", [P, T]), s.ps("y_ps", [P, T]), s.ps("out_ps", [P, T])
        score_ps = [s.ps(f"score_ps{n}", [P, T]) for n in range(2)]
        turn_ps = [s.ps(f"turn_ps{n}", [P, T]) for n in range(2)]
        norm = Norm(s, g)
        names = ["loaded", "chained", "x_ready", "chunk_ready", "chunk_turned", "xT_ready", "y_ready",
                 "yT_ready", "scored", "top_ready", "prob_ready", "prob_turned", "probT_ready",
                 "mixed", "out_taken", "w_split", "x_high", "y_high", "past_end"]
        (loaded, chained, x_ready, chunk_ready, chunk_turned, xT_ready, y_ready, yT_ready, scored,
         top_ready, prob_ready, prob_turned, probT_ready, mixed, out_taken, w_split, x_high, y_high, past_end) = [s.sem(n) for n in names]

        with nc.Block() as block:
            @block.sync
            def _(sp):
                for rows in (slice(0, D), slice(D, P)):
                    for columns in (slice(0, D), slice(D, P)):
                        sp.dma_start(wt[rows, columns], w["W"]).then_inc(loaded, 16)

            @block.gpsimd
            def _(pool):
                pool.memset(x[:, TILES:, :], 0.0).then_inc(past_end, 1)
                norm.gpsimd(pool)
                pool.wait_ge(loaded, 64)
                pool.tensor_copy(wt_parts[0][:, :], wt[:, :]).then_inc(w_split, 1)
                pool.wait_ge(w_split, 1)
                pool.tensor_tensor(wt_parts[1][:, :], wt[:, :], wt_parts[0][:, :], ALU.subtract).then_inc(w_split, 1)
                pool.wait_ge(x_ready, 1)
                pool.wait_ge(past_end, 1)
                with pool.Fori(0, B + 1) as i:
                    pool.wait_ge(chunk_turned, i + 1)
                    pool.tensor_copy(x_now[:, :, :], x[:, bass.ds(i * CT, CT), :]).then_inc(x_high, 1)
                    pool.wait_ge(x_high, 1)
                    pool.tensor_copy(x_chunk[:, :, 0, :], x_now[:, :, :]).then_inc(x_high, 1)
                    pool.wait_ge(x_high, 2)
                    pool.tensor_tensor(x_chunk[:, :, 1, :], x_now[:, :, :], x_chunk[:, :, 0, :], ALU.subtract)\
                        .then_inc(chunk_ready, 1)
                    pool.sem_clear(x_high)

            @block.tensor
            def _(pe):
                pe.wait_ge(w_split, 2)
                pe.sem_inc(mixed, CT)
                pe.sem_inc(chunk_turned, 1)

                def turn_chunk(c):
                    pe.wait_ge(chunk_ready, c + 1)
                    for j in range(CT):
                        last = pe.transpose(xT_ps[:, j * P:(j + 1) * P],
                                            x_chunk[:, j, :, :].rearrange("p a d -> p (a d)").bitcast(F32), ident[:, :])
                    last.then_inc(chunk_turned, 1)

                def project(c):
                    pe.wait_ge(xT_ready, c + 1)
                    for k, part in enumerate(wt_parts):
                        last = pe.matmul(y_ps[:, :], part[:, :], xT[:, :], start=(k == 0), stop=(k == 1))
                    last.then_inc(y_ready, 1)

                turn_chunk(0)
                project(0)
                with pe.Fori(0, B) as i:
                    pe.wait_ge(yT_ready, i + 1)

                    def score(j):
                        pe.wait_ge(prob_ready, i * CT + (j + 1))
                        for k, part in enumerate(yT_parts):
                            last = pe.matmul(score_ps[j % 2][:, :], part[:, j * P:(j + 1) * P], xT[:, :],
                                             start=(k == 0), stop=(k == 1))
                        last.then_inc(scored, 1)

                    def turn(j):
                        pe.wait_ge(prob_ready, i * CT + (j + 3))
                        pe.wait_ge(probT_ready, i * CT + (j + 1))
                        for m in range(CT):
                            last = pe.transpose(turn_ps[j % 2][:, m * P:(m + 1) * P],
                                                prob[:, j % 2, m * P:(m + 1) * P], ident[:, :])
                        last.then_inc(prob_turned, 1)

                    def mix(j):
                        pe.wait_ge(probT_ready, i * CT + (j + 3))
                        if j == 0:
                            pe.wait_ge(out_taken, i + 1)
                        for m in range(CT):
                            last = pe.matmul(out_ps[:, j * D:(j + 1) * D], probT[:, j % 2, m, :],
                                             x[:, bass.ds(i * CT + m, 1), :].rearrange("p a d -> p (a d)"), start=(m == 0), stop=(m == CT - 1))
                        last.then_inc(mixed, 1)

                    score(0)
                    for j in range(CT):
                        if j + 1 < CT:
                            score(j + 1)
                        turn(j)
                        if j == CT - 2:
                            turn_chunk(i + 1)
                        if j:
                            mix(j - 1)
                    project(i + 1)
                    mix(CT - 1)

            @block.scalar
            def _(a):
                a.sem_inc(prob_ready, 2)
                norm.scalar(a, x[:, 0:TILES, :])
                a.activation(prob[0:1, 0, 0:1], g["ones"][0:1, 0:1], ACT.Exp)

                def take_x(c):
                    a.wait_ge(chunk_turned, c + 2)
                    a.activation(xT[:, :], xT_ps[:, :], ACT.Copy).then_inc(xT_ready, 1)
                    a.wait_ge(y_ready, c + 1)
                    a.activation(yT_parts[0][:, :], y_ps[:, :], ACT.Copy).then_inc(y_high, 1)

                take_x(0)
                with a.Fori(0, B) as i:
                    for j in range(CT):
                        a.wait_ge(top_ready, i * CT + (j + 1))
                        a.wait_ge(prob_turned, i * CT + (j + 1))
                        a.activation(prob[:, j % 2, :], score_ps[j % 2][:, :], ACT.Exp, bias=top[:, j:j + 1],
                                     scale=SCALE, accum_out=total[:, j:j + 1]).then_inc(prob_ready, 1)
                    take_x(i + 1)

            @block.vector
            def _(dve):
                link = Chain(dve, chained)
                norm.vector(dve, link, h[:, :, :], x[:, 0:TILES, :])
                dve.sem_inc(x_ready, 1)
                dve.sem_inc(prob_turned, 2)
                dve.sem_inc(probT_ready, 2)
                dve.sem_inc(out_taken, 1)

                def low_part(c):
                    dve.wait_ge(y_high, c + 1)
                    dve.tensor_tensor(yT_parts[1][:, :], y_ps[:, :], yT_parts[0][:, :], ALU.subtract)\
                        .then_inc(yT_ready, 1)

                low_part(0)
                with dve.Fori(0, B) as i:
                    link.restart()

                    def maximum(j):
                        dve.wait_ge(scored, i * CT + (j + 1))
                        link(dve.tensor_reduce(top[:, j:j + 1], score_ps[j % 2][:, :], X, ALU.max))
                        dve.tensor_scalar(top[:, j:j + 1], top[:, j:j + 1], -SCALE, None, ALU.mult)\
                            .then_inc(top_ready, 1)

                    maximum(0)
                    for j in range(CT):
                        if j + 1 < CT:
                            maximum(j + 1)
                        dve.wait_ge(prob_turned, i * CT + (j + 3))
                        dve.wait_ge(mixed, i * CT + (j - 1 + CT))
                        dve.tensor_copy(probT[:, j % 2, :, :],
                                        turn_ps[j % 2][:, :].rearrange("p (m q) -> p m q", m=CT))\
                            .then_inc(probT_ready, 1)
                    low_part(i + 1)
                    dve.wait_ge(mixed, i * CT + 2 * CT)
                    link(dve.reciprocal(total[:, :], total[:, :]))
                    link(dve.tensor_tensor(part[:, :, :], out_ps[:, 0:CT * D].rearrange("p (j d) -> p j d", d=D),
                                           spread(total[:, :], D), ALU.mult))
                    dve.sem_inc(out_taken, 1)
                    h_chunk = h[:, bass.ds(i * CT, CT), :]
                    link(dve.tensor_tensor(h_chunk, h_chunk, part[:, :, :], ALU.add))
        s.clear()


def named(arrays, prefix):
    return {k[len(prefix) + 1:]: a for k, a in arrays.items() if k.startswith(prefix + "_")}


def tower(nc, arrays, out):
    capacity = -(-5 * N // (4 * E))
    with ExitStack() as ctx:
        h = ctx.enter_context(nc.sbuf_tensor("h", [P, TILES, D], F32))
        stored = ctx.enter_context(nc.semaphore("stored"))
        g = {"ctx": ctx, "h": h}
        constants(nc, g)
        token_stage(nc, g, arrays["ids"], [arrays[f"emb_{n}"] for n in GRAMS])
        recurrent_stage(nc, g, named(arrays, "L0_attn"))
        expert_stage(nc, g, "L0_ffn", named(arrays, "L0_ffn"), ACT.Relu, 2, "top", 1,
                     capacity=capacity, limit_infinite=True)
        memory_stage(nc, g, named(arrays, "L1_attn"))
        expert_stage(nc, g, "L1_ffn", named(arrays, "L1_ffn"), ACT.Gelu, 1, "mask", 2)
        square_stage(nc, g, named(arrays, "L2_attn"))
        w = named(arrays, "L2_ffn")
        expert_stage(nc, g, "L2_ffn", w, ACT.Gelu, 1, "softmax", 2, norms=2,
                     gamma_beta=(w["gamma"], w["beta"]))
        softmax_stage(nc, g, named(arrays, "L3_attn"))
        w = named(arrays, "L3_ffn")
        expert_stage(nc, g, "L3_ffn", w, ACT.Gelu, 2, "renormed", 2, norms=2,
                     expert_norm=(w["ln_g"], w["ln_b"]))
        with nc.Block() as block:
            @block.sync
            def _(sp):
                sp.dma_start(out.rearrange("b t d -> (b t) d").rearrange("(j p) d -> p j d", p=P), h[:, :, :])\
                    .then_inc(stored, 16)
                sp.wait_ge(stored, 16)


def square_blocks():
    column = np.concatenate([np.arange(8), np.repeat(np.arange(8), 8)])
    out = np.zeros((128, 5, 72), np.float32)
    row = np.arange(128)
    for pair in range(4):
        out[:, pair] = np.where((2 * pair + row // 64)[:, None] == column, 1 / 8, 0)
    out[0:64, 4] = np.where((row[0:64] // 8)[:, None] == column, 10 / np.sqrt(8), 0)
    out[64, 4] = 25
    return out


def lay_out(v):
    c = np.ascontiguousarray
    out = {"ids": c(v["x"])}
    for n in (2, 3, 4):
        out[f"emb_{n}"] = c(v[f"L0_tok_emb_{n}"])

    def experts(name, w1, b1, w2, b2, wg, bg):
        w1, b1, w2 = v[w1], v[b1], v[w2]
        blocks = b1.size // 128
        out[f"{name}_w1"] = c(w1.transpose(1, 0, 2).reshape(w1.shape[1], -1))
        out[f"{name}_b1"] = c(b1.reshape(blocks, 128).T)
        out[f"{name}_w2"] = c(w2.reshape(blocks, 128, -1).transpose(1, 0, 2))
        out[f"{name}_b2"] = c(v[b2].reshape(4, 128).T)
        out[f"{name}_wg"] = c(v[wg])
        out[f"{name}_bg"] = c(v[bg])

    experts("L0_ffn", "L0_ffn_w1", "L0_ffn_b1", "L0_ffn_w2", "L0_ffn_b2", "L0_ffn_gate_w", "L0_ffn_gate_b")
    experts("L1_ffn", "L1_ffn_W1", "L1_ffn_b1", "L1_ffn_W2", "L1_ffn_b2", "L1_ffn_Wg", "L1_ffn_bg")
    experts("L2_ffn", "L2_ffn_W1", "L2_ffn_b1", "L2_ffn_W2", "L2_ffn_b2", "L2_ffn_Wr", "L2_ffn_br")
    experts("L3_ffn", "L3_ffn_W1", "L3_ffn_b1", "L3_ffn_W2", "L3_ffn_b2", "L3_ffn_Wr", "L3_ffn_br")
    out["L2_ffn_gamma"], out["L2_ffn_beta"] = c(v["L2_ffn_gamma"]), c(v["L2_ffn_beta"])
    out["L3_ffn_ln_g"], out["L3_ffn_ln_b"] = c(v["L3_ffn_ln_g"].T), c(v["L3_ffn_ln_b"].T)

    w = v["L0_attn_slow_W"].reshape(8, 162, 64)
    kinds = [w[:, a:b].reshape(-1, 64) for a, b in zip((0, 32, 64, 128, 96, 160, 161), (32, 64, 96, 160, 128, 161, 162))]
    out["L0_attn_w_in"] = c(np.concatenate(kinds).T)
    out["L0_attn_w_out"] = c(v["L0_attn_out_W"].T.reshape(2, 128, 64).transpose(1, 0, 2))
    out["L0_attn_ln_g"], out["L0_attn_ln_b"] = c(v["L0_attn_ln_g"]), c(v["L0_attn_ln_b"])

    for n in ("W_K", "W_V", "W_Q", "W_th", "W_et", "W_al", "W_gate", "W_proj", "W1"):
        out[f"L1_attn_{n}"] = c(v[f"L1_attn_{n}"].T)
    out["L1_attn_W2"] = c(v["L1_attn_W2"].T.reshape(2, 128, 64).transpose(1, 0, 2))
    for n in ("conv_k", "conv_v", "conv_q"):
        out[f"L1_attn_{n}"] = c(v[f"L1_attn_{n}"].reshape(64, 3))
    for n in ("b_th", "b_et", "b_al"):
        out[f"L1_attn_{n}"] = c(v[f"L1_attn_{n}"].reshape(64, 1))
    out["L1_attn_ln_g"], out["L1_attn_ln_b"] = c(v["L1_attn_ln_g"]), c(v["L1_attn_ln_b"])

    w, b = v["L2_attn_qkv_w"], v["L2_attn_qkv_b"]
    q, qb = w[0:64].reshape(8, 8, 64), b[0:64].reshape(8, 8)
    out["L2_attn_q_i"] = c(np.repeat(q, 8, axis=1).reshape(512, 64).T)
    out["L2_attn_q_j"] = c(np.tile(q, (1, 8, 1)).reshape(512, 64).T)
    out["L2_attn_qb_i"] = c(np.repeat(qb, 8, axis=1).reshape(4, 128).T)
    out["L2_attn_qb_j"] = c(np.tile(qb, (1, 8)).reshape(4, 128).T)
    out["L2_attn_w"] = c(w.T)
    out["L2_attn_qb"] = c(b[0:64].reshape(64, 1))
    out["L2_attn_b"] = c(b)
    out["L2_attn_proj_w"] = c(v["L2_attn_proj_w"].T)
    out["L2_attn_proj_b"] = c(v["L2_attn_proj_b"])
    out["L3_attn_W"] = c(v["L3_attn_W"])
    out["L2_attn_blocks"] = square_blocks()
    return out


def kernel(**inputs):
    import concourse.bacc as bacc
    from concourse.bass_utils import run_bass_kernel_spmd

    nc = bacc.Bacc("TRN2", target_bir_lowering=False, num_devices=1)
    laid = lay_out({k: np.asarray(a) for k, a in inputs.items()})
    arrays = {k: nc.dram_tensor(f"in_{k}", a.shape, mybir.dt.from_np(a.dtype), kind="ExternalInput").ap()
              for k, a in laid.items()}
    out = nc.dram_tensor("out", (B, T, D), F32, kind="ExternalOutput").ap()
    tower(nc, arrays, out)
    r = run_bass_kernel_spmd(nc, [{f"in_{k}": a for k, a in laid.items()}], core_ids=[0])
    return r.results[0]["out"]
```
